# Optimizing a Trainium2 kernel written in Bass

```python
import numpy as np
import jax
import jax.numpy as jnp

def _softmax(x, axis=-1):
    return jax.nn.softmax(x, axis=axis)

def _gelu(x):
    return jax.nn.gelu(x, approximate=True)

def _silu(x):
    return jax.nn.silu(x)

def _sigmoid(x):
    return jax.nn.sigmoid(x)

def _layernorm(x, axis=-1, eps=1e-05):
    m = jnp.mean(x, axis=axis, keepdims=True)
    v = jnp.var(x, axis=axis, keepdims=True)
    return (x - m) / jnp.sqrt(v + eps)

def _scatter_add(tgt, idx, src, axis=0):
    return tgt.at[idx].add(src)

def _segment_sum(src, seg, n):
    return jax.ops.segment_sum(src, seg, n)
kernel_name = 'mk_gnn_resnorm_d4_gnn_r32_b3cb0f'

def setup_inputs(seed: int=0):
    np.random.seed(seed)
    _w = jnp.asarray

    def _rec_inputs():
        import jax
        import jax.numpy as jnp
        _gk = jax.random.key(seed)
        x = -0.000202 + 1 * jax.random.normal(jax.random.fold_in(_gk, 1), (50000, 128), jnp.float32)
        src = jax.random.randint(jax.random.fold_in(_gk, 2), (25000,), 0, 50000, jnp.int32)
        dst = jax.random.randint(jax.random.fold_in(_gk, 3), (25000,), 0, 50000, jnp.int32)
        _o = jnp.argsort(dst, stable=True)
        src = src[_o]
        dst = dst[_o]
        edge_attr_10 = jax.random.uniform(jax.random.fold_in(_gk, 12), (25000, 10), jnp.float32, 0.0, 1)
        edge_attr_4 = 0.00109026 + 0.999989 * jax.random.normal(jax.random.fold_in(_gk, 13), (25000, 4), jnp.float32)
        edge_type_64 = jax.random.randint(jax.random.fold_in(_gk, 15), (25000,), 0, 64, jnp.int32)
        edge_weight = jax.random.uniform(jax.random.fold_in(_gk, 16), (25000,), jnp.float32, 0.0, 1)
        node_vec = jax.random.uniform(jax.random.fold_in(_gk, 17), (50000,), jnp.float32, 0.0, 0.999994)
        return (x, src, dst, edge_attr_10, edge_attr_4, edge_type_64, edge_weight, node_vec)
    x, src, dst, edge_attr_10, edge_attr_4, edge_type_64, edge_weight, node_vec = _rec_inputs()

    def _L0_gnn_setup():
        import jax, jax.numpy as jnp
        import numpy as np
        N = 50000
        E = 25000
        MUL = 32
        NB = 10
        RN = 100
        NUM_NEIGHBORS = 16
        INV_SQRT3 = 1.0 / np.sqrt(3.0).astype(np.float32)

        def _lin_irreps(x0, x1, W0, W1):
            fan = x0.shape[-1]
            y0 = x0 @ W0 / jnp.sqrt(jnp.asarray(fan, x0.dtype))
            y1 = jnp.einsum('num,uw->nwm', x1, W1) / jnp.sqrt(jnp.asarray(x1.shape[1], x1.dtype))
            return (y0, y1)
        key = jax.random.key(seed)
        ks = jax.random.split(key, 13)
        x = jax.random.normal(ks[0], (N, MUL * 4), jnp.float32)
        edge_src = jax.random.randint(ks[1], (E,), 0, N, dtype=jnp.int32)
        edge_dst = jax.random.randint(ks[2], (E,), 0, N, dtype=jnp.int32)
        edge_attr = jax.random.normal(ks[3], (E, 4), jnp.float32)
        edge_length_embedded = jax.random.uniform(ks[4], (E, NB), dtype=jnp.float32)
        W_si_0e = jax.random.normal(ks[5], (MUL, MUL), jnp.float32)
        W_si_1o = jax.random.normal(ks[6], (MUL, MUL), jnp.float32)
        W_l1_0e = jax.random.normal(ks[7], (MUL, MUL), jnp.float32)
        W_l1_1o = jax.random.normal(ks[8], (MUL, MUL), jnp.float32)
        W_fc1 = jax.random.normal(ks[9], (NB, RN), jnp.float32)
        W_fc2 = jax.random.normal(ks[10], (RN, 4 * MUL), jnp.float32)
        W_l2_0e = jax.random.normal(ks[11], (2 * MUL, MUL), jnp.float32)
        W_l2_1o = jax.random.normal(ks[12], (2 * MUL, MUL), jnp.float32)
        return dict(x=x, edge_src=edge_src, edge_dst=edge_dst, edge_attr=edge_attr, edge_length_embedded=edge_length_embedded, W_si_0e=W_si_0e, W_si_1o=W_si_1o, W_l1_0e=W_l1_0e, W_l1_1o=W_l1_1o, W_fc1=W_fc1, W_fc2=W_fc2, W_l2_0e=W_l2_0e, W_l2_1o=W_l2_1o)
    _L0_gnn_all = _L0_gnn_setup()
    _L0_gnn_in = {k: v for k, v in _L0_gnn_all.items() if k in ('W_si_0e', 'W_si_1o', 'W_l1_0e', 'W_l1_1o', 'W_fc1', 'W_fc2', 'W_l2_0e', 'W_l2_1o')}
    del _L0_gnn_all

    def _L1_gnn_setup():
        import jax, jax.numpy as jnp
        import numpy as np
        N_NODES = 50000
        N_EDGES = 18750
        D = 128
        key = jax.random.key(seed)
        k1, k2, k3, k4, k5 = jax.random.split(key, 5)
        x = jax.random.normal(k1, (N_NODES, D), dtype=jnp.float32)
        W = jax.random.normal(k2, (D, 2 * D), dtype=jnp.float32) * (1.0 / np.sqrt(2 * D))
        b = jax.random.normal(k3, (D,), dtype=jnp.float32) * 0.01
        src = jax.random.randint(k4, (N_EDGES,), 0, N_NODES, dtype=jnp.int32)
        dst = jax.random.randint(k5, (N_EDGES,), 0, N_NODES, dtype=jnp.int32)
        return {'x': x, 'W': W, 'b': b, 'src': src, 'dst': dst}
    _L1_gnn_all = _L1_gnn_setup()
    _L1_gnn_in = {k: v for k, v in _L1_gnn_all.items() if k in ('W', 'b')}
    del _L1_gnn_all

    def _L2_gnn_setup():
        import jax, jax.numpy as jnp
        import numpy as np
        HEADS = 4
        OUT_DIM = 32
        N_NODES = 50000
        N_EDGES = 25000
        IN_DIM = 128
        key = jax.random.key(seed)
        k1, k2, k3, k4, k5 = jax.random.split(key, 5)
        x = jax.random.normal(k1, (N_NODES, IN_DIM), dtype=jnp.float32)
        edge_index = jax.random.randint(k2, (2, N_EDGES), 0, N_NODES, dtype=jnp.int64)
        W = jax.random.normal(k3, (IN_DIM, HEADS * OUT_DIM), dtype=jnp.float32) * (1.0 / np.sqrt(IN_DIM))
        attn_src = jax.random.normal(k4, (HEADS, OUT_DIM), dtype=jnp.float32) * (1.0 / np.sqrt(OUT_DIM))
        attn_dst = jax.random.normal(k5, (HEADS, OUT_DIM), dtype=jnp.float32) * (1.0 / np.sqrt(OUT_DIM))
        bias = jnp.zeros((HEADS * OUT_DIM,), dtype=jnp.float32)
        return {'x': x, 'edge_index': edge_index, 'W': W, 'attn_src': attn_src, 'attn_dst': attn_dst, 'bias': bias, 'num_nodes': N_NODES}
    _L2_gnn_all = _L2_gnn_setup()
    _L2_gnn_in = {k: v for k, v in _L2_gnn_all.items() if k in ('W', 'attn_src', 'attn_dst', 'bias')}
    del _L2_gnn_all

    def _L3_gnn_setup():
        import jax, jax.numpy as jnp
        import numpy as np
        N_NODES = 50000
        N_EDGES = 25000
        HIDDEN = 128
        N_REL = 64
        NUM_HEADS = 8
        HEAD_DIM = HIDDEN // NUM_HEADS
        key = jax.random.key(seed)
        ks = jax.random.split(key, 20)
        s = 0.05
        inp = {'x': jax.random.normal(ks[0], (N_NODES, HIDDEN), dtype=jnp.float32), 'timestamps': jax.random.uniform(ks[1], (N_NODES,), dtype=jnp.float32), 'src': jax.random.randint(ks[2], (N_EDGES,), 0, N_NODES), 'dst': jax.random.randint(ks[3], (N_EDGES,), 0, N_NODES), 'edge_type': jax.random.randint(ks[4], (N_EDGES,), 0, N_REL), 'edge_time': jax.random.uniform(ks[5], (N_EDGES,), dtype=jnp.float32), 'rel_table': jax.random.normal(ks[6], (N_REL, HIDDEN), dtype=jnp.float32) * s, 'Wq': jax.random.normal(ks[7], (HIDDEN, HIDDEN), dtype=jnp.float32) * s, 'bq': jnp.zeros((HIDDEN,), dtype=jnp.float32), 'Wk': jax.random.normal(ks[8], (HIDDEN, HIDDEN), dtype=jnp.float32) * s, 'bk': jnp.zeros((HIDDEN,), dtype=jnp.float32), 'Wv': jax.random.normal(ks[9], (HIDDEN, HIDDEN), dtype=jnp.float32) * s, 'bv': jnp.zeros((HIDDEN,), dtype=jnp.float32), 'W1': jax.random.normal(ks[10], (2 * HIDDEN + 1, HIDDEN), dtype=jnp.float32) * s, 'b1': jnp.zeros((HIDDEN,), dtype=jnp.float32), 'W2': jax.random.normal(ks[11], (HIDDEN, 1), dtype=jnp.float32) * s, 'b2': jnp.zeros((1,), dtype=jnp.float32), 'time_coeff': jnp.array(1.0, dtype=jnp.float32)}
        return inp
    _L3_gnn_all = _L3_gnn_setup()
    _L3_gnn_in = {k: v for k, v in _L3_gnn_all.items() if k in ('rel_table', 'Wq', 'bq', 'Wk', 'bk', 'Wv', 'bv', 'W1', 'b1', 'W2', 'b2', 'time_coeff')}
    del _L3_gnn_all
    return {'x': x, 'src': src, 'dst': dst, 'edge_attr_10': edge_attr_10, 'edge_attr_4': edge_attr_4, 'edge_type_64': edge_type_64, 'edge_weight': edge_weight, 'node_vec': node_vec, 'L0_gnn_W_si_0e': _L0_gnn_in['W_si_0e'], 'L0_gnn_W_si_1o': _L0_gnn_in['W_si_1o'], 'L0_gnn_W_l1_0e': _L0_gnn_in['W_l1_0e'], 'L0_gnn_W_l1_1o': _L0_gnn_in['W_l1_1o'], 'L0_gnn_W_fc1': _L0_gnn_in['W_fc1'], 'L0_gnn_W_fc2': _L0_gnn_in['W_fc2'], 'L0_gnn_W_l2_0e': _L0_gnn_in['W_l2_0e'], 'L0_gnn_W_l2_1o': _L0_gnn_in['W_l2_1o'], 'L1_gnn_W': _L1_gnn_in['W'], 'L1_gnn_b': _L1_gnn_in['b'], 'L2_gnn_W': _L2_gnn_in['W'], 'L2_gnn_attn_src': _L2_gnn_in['attn_src'], 'L2_gnn_attn_dst': _L2_gnn_in['attn_dst'], 'L2_gnn_bias': _L2_gnn_in['bias'], 'L3_gnn_rel_table': _L3_gnn_in['rel_table'], 'L3_gnn_Wq': _L3_gnn_in['Wq'], 'L3_gnn_bq': _L3_gnn_in['bq'], 'L3_gnn_Wk': _L3_gnn_in['Wk'], 'L3_gnn_bk': _L3_gnn_in['bk'], 'L3_gnn_Wv': _L3_gnn_in['Wv'], 'L3_gnn_bv': _L3_gnn_in['bv'], 'L3_gnn_W1': _L3_gnn_in['W1'], 'L3_gnn_b1': _L3_gnn_in['b1'], 'L3_gnn_W2': _L3_gnn_in['W2'], 'L3_gnn_b2': _L3_gnn_in['b2'], 'L3_gnn_time_coeff': _L3_gnn_in['time_coeff']}

def reference(x, src, dst, edge_attr_10, edge_attr_4, edge_type_64, edge_weight, node_vec, L0_gnn_W_si_0e, L0_gnn_W_si_1o, L0_gnn_W_l1_0e, L0_gnn_W_l1_1o, L0_gnn_W_fc1, L0_gnn_W_fc2, L0_gnn_W_l2_0e, L0_gnn_W_l2_1o, L1_gnn_W, L1_gnn_b, L2_gnn_W, L2_gnn_attn_src, L2_gnn_attn_dst, L2_gnn_bias, L3_gnn_rel_table, L3_gnn_Wq, L3_gnn_bq, L3_gnn_Wk, L3_gnn_bk, L3_gnn_Wv, L3_gnn_bv, L3_gnn_W1, L3_gnn_b1, L3_gnn_W2, L3_gnn_b2, L3_gnn_time_coeff):
    import jax
    import jax.numpy as jnp

    def _L0_gnn_ref(x, edge_src, edge_dst, edge_attr, edge_length_embedded, W_si_0e, W_si_1o, W_l1_0e, W_l1_1o, W_fc1, W_fc2, W_l2_0e, W_l2_1o):
        import jax, jax.numpy as jnp
        import numpy as np
        N = 50000
        E = 25000
        MUL = 32
        NB = 10
        RN = 100
        NUM_NEIGHBORS = 16
        INV_SQRT3 = 1.0 / np.sqrt(3.0).astype(np.float32)

        def _lin_irreps(x0, x1, W0, W1):
            fan = x0.shape[-1]
            y0 = x0 @ W0 / jnp.sqrt(jnp.asarray(fan, x0.dtype))
            y1 = jnp.einsum('num,uw->nwm', x1, W1) / jnp.sqrt(jnp.asarray(x1.shape[1], x1.dtype))
            return (y0, y1)
        n = x.shape[0]
        x0 = x[:, :MUL]
        x1 = x[:, MUL:].reshape(n, MUL, 3)
        h = jax.nn.relu(edge_length_embedded @ W_fc1 / jnp.sqrt(jnp.float32(NB)))
        w = h @ W_fc2 / jnp.sqrt(jnp.float32(RN))
        wA, wB, wC, wD = (w[:, :MUL], w[:, MUL:2 * MUL], w[:, 2 * MUL:3 * MUL], w[:, 3 * MUL:])
        si0, si1 = _lin_irreps(x0, x1, W_si_0e, W_si_1o)
        y0, y1 = _lin_irreps(x0, x1, W_l1_0e, W_l1_1o)
        g0 = y0[edge_src]
        g1 = y1[edge_src]
        sh0 = edge_attr[:, 0]
        sh1 = edge_attr[:, 1:4]
        outA = wA * g0 * sh0[:, None]
        outB = wB[:, :, None] * g0[:, :, None] * sh1[:, None, :]
        outC = wC[:, :, None] * g1 * sh0[:, None, None]
        outD = wD * jnp.einsum('eum,em->eu', g1, sh1) * INV_SQRT3
        seg = lambda v: jax.ops.segment_sum(v, edge_dst, num_segments=n)
        inv_sqrt_nn = 1.0 / jnp.sqrt(jnp.float32(NUM_NEIGHBORS))
        mid0 = jnp.concatenate([seg(outA), seg(outD)], axis=1) * inv_sqrt_nn
        mid1 = jnp.concatenate([seg(outB), seg(outC)], axis=1) * inv_sqrt_nn
        o0, o1 = _lin_irreps(mid0, mid1, W_l2_0e, W_l2_1o)
        out0 = si0 + 0.5 * o0
        out1 = si1 + 0.5 * o1
        return jnp.concatenate([out0, out1.reshape(n, MUL * 3)], axis=1)

    def _L1_gnn_ref(x, W, b, src, dst):
        import jax, jax.numpy as jnp
        import numpy as np
        N_NODES = 50000
        N_EDGES = 18750
        D = 128
        N = x.shape[0]
        neigh_sum = jax.ops.segment_sum(x[src], dst, num_segments=N)
        deg = jax.ops.segment_sum(jnp.ones_like(src, dtype=x.dtype), dst, num_segments=N)
        mean = neigh_sum / jnp.maximum(deg, 1.0)[:, None]
        neigh_agg = jnp.where(deg[:, None] > 0, mean, x)
        h = jnp.concatenate([x, neigh_agg], axis=-1)
        return jax.nn.relu(h @ W.T + b)

    def _L2_gnn_ref(x, edge_index, W, attn_src, attn_dst, bias, num_nodes):
        import jax, jax.numpy as jnp
        import numpy as np
        HEADS = 4
        OUT_DIM = 32
        N_NODES = 50000
        N_EDGES = 25000
        IN_DIM = 128
        s0, d0 = (edge_index[0], edge_index[1])
        loop = jnp.arange(num_nodes, dtype=edge_index.dtype)
        src = jnp.concatenate([s0, d0, loop])
        dst = jnp.concatenate([d0, s0, loop])
        proj = (x @ W).reshape(num_nodes, HEADS, OUT_DIM)
        src_proj = proj[src]
        dst_proj = proj[dst]
        scores = jnp.einsum('ehd,hd->eh', src_proj, attn_src) + jnp.einsum('ehd,hd->eh', dst_proj, attn_dst)
        scores = jax.nn.leaky_relu(scores, negative_slope=0.2)
        seg_max = jax.ops.segment_max(scores, dst, num_segments=num_nodes)
        exp = jnp.exp(scores - jax.lax.stop_gradient(seg_max)[dst])
        denom = jax.ops.segment_sum(exp, dst, num_segments=num_nodes)
        attn = exp / jnp.maximum(denom, 1e-12)[dst]
        messages = src_proj * attn[..., None]
        out = jax.ops.segment_sum(messages, dst, num_segments=num_nodes)
        out = out.reshape(num_nodes, HEADS * OUT_DIM) + bias
        return jax.nn.elu(out)

    def _L3_gnn_ref(x, timestamps, src, dst, edge_type, edge_time, rel_table, Wq, bq, Wk, bk, Wv, bv, W1, b1, W2, b2, time_coeff):
        import jax, jax.numpy as jnp
        import numpy as np
        N_NODES = 50000
        N_EDGES = 25000
        HIDDEN = 128
        N_REL = 64
        NUM_HEADS = 8
        HEAD_DIM = HIDDEN // NUM_HEADS
        N = x.shape[0]
        delta_t = (timestamps[dst] - edge_time) / (jnp.abs(time_coeff) + 1e-09)
        time_mask = jax.nn.sigmoid(delta_t)[:, None]
        rel_emb = rel_table[edge_type] * time_mask
        src_emb = x[src]
        weight_input = jnp.concatenate([src_emb, rel_emb, time_mask], axis=-1)
        h = jax.nn.relu(weight_input @ W1 + b1)
        dynamic_weights = jax.nn.sigmoid(h @ W2 + b2)
        message = src_emb * rel_emb * dynamic_weights
        q = (x[dst] @ Wq + bq).reshape(-1, NUM_HEADS, HEAD_DIM)
        k = (message @ Wk + bk).reshape(-1, NUM_HEADS, HEAD_DIM)
        v = (message @ Wv + bv).reshape(-1, NUM_HEADS, HEAD_DIM)
        scores = (q * k).sum(-1) / HEAD_DIM ** 0.5
        seg_max = jax.ops.segment_max(scores, dst, num_segments=N)
        e = jnp.exp(scores - seg_max[dst])
        denom = jax.ops.segment_sum(e, dst, num_segments=N)
        attn = e / denom[dst]
        out = jax.ops.segment_sum(v * attn[..., None], dst, num_segments=N)
        return out.reshape(N, NUM_HEADS * HEAD_DIM)
    edge_index = jnp.stack([src, dst])
    x = _layernorm(x + _L0_gnn_ref(x, src, dst, edge_attr_4, edge_attr_10, L0_gnn_W_si_0e, L0_gnn_W_si_1o, L0_gnn_W_l1_0e, L0_gnn_W_l1_1o, L0_gnn_W_fc1, L0_gnn_W_fc2, L0_gnn_W_l2_0e, L0_gnn_W_l2_1o), axis=-1)
    x = _layernorm(x + _L1_gnn_ref(x, L1_gnn_W, L1_gnn_b, src, dst), axis=-1)
    x = _layernorm(x + _L2_gnn_ref(x, edge_index, L2_gnn_W, L2_gnn_attn_src, L2_gnn_attn_dst, L2_gnn_bias, 50000), axis=-1)
    x = _layernorm(x + _L3_gnn_ref(x, node_vec, src, dst, edge_type_64, edge_weight, L3_gnn_rel_table, L3_gnn_Wq, L3_gnn_bq, L3_gnn_Wk, L3_gnn_bk, L3_gnn_Wv, L3_gnn_bv, L3_gnn_W1, L3_gnn_b1, L3_gnn_W2, L3_gnn_b2, L3_gnn_time_coeff), axis=-1)
    return x

_drawn_inputs = setup_inputs


def setup_inputs(seed=0):
    import zlib

    import numpy as np

    out = dict(_drawn_inputs(seed))
    spreads = {'L2_gnn_bias': (0.0, 0.1),
     'L3_gnn_bq': (0.0, 2.0),
     'L3_gnn_bk': (0.0, 2.0),
     'L3_gnn_bv': (0.0, 0.1),
     'L3_gnn_b1': (0.0, 0.8)}
    factors = {'edge_attr_10': 4.681,
     'edge_weight': 8.0,
     'node_vec': 8.0,
     'L0_gnn_W_l1_0e': 3.261,
     'L0_gnn_W_l1_1o': 3.295,
     'L0_gnn_W_l2_0e': 4.414,
     'L1_gnn_b': 8.0,
     'L3_gnn_rel_table': 8.0,
     'L3_gnn_Wq': 8.0,
     'L3_gnn_Wk': 8.0,
     'L3_gnn_Wv': 8.0,
     'L3_gnn_W1': 8.0,
     'L3_gnn_W2': 8.0}
    for name, (base, spread) in spreads.items():
        noise = np.random.default_rng([zlib.crc32(name.encode()), seed]).standard_normal(out[name].shape)
        drawn = base * np.exp(spread * noise) if base else spread * noise
        out[name] = jnp.asarray(drawn.astype(out[name].dtype))
    for name, factor in factors.items():
        out[name] = (out[name] * factor).astype(out[name].dtype)
    return out
```

```python
import concourse.bass as bass
from concourse import mybir
from contextlib import ExitStack

F32 = mybir.dt.float32
I32 = mybir.dt.int32
BF16 = mybir.dt.bfloat16
F16 = mybir.dt.float16
ALU = mybir.AluOpType
ACT = mybir.ActivationFunctionType
AX_X = mybir.AxisListType.X

D = 128
MUL = 32
TILE = 128
TPC = 4
CH = TILE * TPC
LN_EPS = 1e-5
FAR = 1 << 20
ACT_SET = "natural_log_exp_and_others"
NEG = -1e30

W_DST, W_SRC, W_TYPE, W_NV, W_EW, W_SH, W_LEN = 0, 1, 2, 3, 4, 5, 9
N_SH, N_LEN = 4, 10
N_ATTR = N_SH + N_LEN
REC = 20


class Chunk:

    def __init__(self, i, slot, turn, ring):
        self.i, self.slot, self.turn, self.ring = i, slot, turn, ring

    def has(self, back):
        return not isinstance(self.i, int) or self.i >= back

    def count(self, back=0):
        return self.i + (1 - back)

    def slot_used(self):
        return not isinstance(self.turn, int) or self.turn > 0

    def landed(self, amount, back=0):
        return (self.turn + (1 - back)) * amount


def run_chunks(eng, n, ring, lags, body, base=0):
    deep = max(lags)
    before = base // ring

    def at(i):
        return [Chunk(i - k + base, (i - k) % ring, (i - k) // ring + before, ring) if 0 <= i - k < n else None
                for k in lags]

    lo = -(-(deep + ring) // ring)
    hi = max(lo, (n - 1) // ring)
    for i in range(min(lo * ring, n + deep)):
        body(at(i))
    if hi > lo:
        with eng.Fori(lo, hi) as turn:
            for p in range(ring):
                body([Chunk(turn * ring + (p - k + base), (p - k) % ring, turn + ((p - k) // ring + before), ring)
                      for k in lags])
    for i in range(hi * ring, n + deep):
        body(at(i))


def hold(eng, w):
    eng.sem_inc(w["held"], 1)


class Phase:

    def __init__(self, nc, ctx, tag):
        self.nc, self.ctx, self.tag, self.taken = nc, ctx, tag, []

    def sb(self, name, shape, dt=F32):
        return self.ctx.enter_context(self.nc.sbuf_tensor(f"{self.tag}_{name}", shape, dt))

    def ps(self, name, shape=(128, 512), dt=F32):
        return self.ctx.enter_context(self.nc.psum_tensor(f"{self.tag}_{name}", list(shape), dt))

    def sem(self, name):
        s = self.nc.alloc_semaphore(f"{self.tag}_{name}")
        self.taken.append(s)
        return s

    def sems(self, name, n):
        return [self.sem(f"{name}{k}") for k in range(n)]


def end_phase(nc, P):
    nc.all_engine_barrier()
    nc.clear_and_free_semaphores(P.taken)
    nc.all_engine_barrier()


def tiles(t):
    return t.rearrange("p (t c) -> p t c", t=TPC)



def ln_stats(nc, y, stats, mv, tiles_of=range(TPC), at=0):
    for t in tiles_of:
        nc.vector.bn_stats(stats[:, at + t, :], y[:, t, :])


def ln_aggregate(nc, stats, mv, n):
    last = None
    for t in range(n):
        last = nc.vector.bn_aggr(mv[:, t, :], stats[:, t, :])
    return last


def ln_rstd(nc, act, mv, rstd, eps):
    nc.scalar.activation(rstd, mv, ACT.Ln, bias=eps[:, 0:1])
    act.drain()
    return nc.scalar.activation(rstd, rstd, ACT.Exp, scale=-0.5)


def ln_apply(nc, out, y, mv, rstd):
    last = None
    for t in range(TPC):
        last = nc.vector.tensor_scalar(out[:, t, :], y[:, t, :], mv[:, t, 0:1], rstd[:, t:t + 1],
                                       ALU.subtract, ALU.mult)
    return last


def transpose4(nc, out, rows, ident):
    last = None
    for t in range(TPC):
        last = nc.tensor.transpose(out[:, t * TILE:(t + 1) * TILE], rows[:, t, :], ident[:, :])
    return last


def spread(nc, out, cols, ident):
    last = None
    for t in range(TPC):
        last = nc.tensor.matmul(out[:, t * TILE:(t + 1) * TILE], cols[:, t:t + 1].to_broadcast([128, 128]),
                                ident[:, :], start=True, stop=True)
    return last


def build_constants(nc, P, g, A):
    w = {}
    for n in ("ident", "Wsi", "WsiI", "W1a", "W1b", "W1sum", "W2", "Asrc", "Adst", "Aself", "g1", "g2",
              "o1", "o2", "o3", "R1a", "R1b", "R2", "Wq", "Wk", "Wv", "heads16", "heads32"):
        w[n] = P.sb(n, [128, 128])
    w["held"] = P.sem("held")
    w["identb"] = P.sb("identb", [128, 128], BF16)
    w["eps"] = P.sb("eps", [128, 1])
    w["ones_row"] = P.sb("ones_row", [1, 128])
    w["bias1"] = P.sb("bias1", [1, TPC, D])
    w["bias2"] = P.sb("bias2", [1, TPC, D])
    w["bias3v"] = P.sb("bias3v", [128, 1])
    w["bq"] = P.sb("bq", [128, 1])
    w["bk"] = P.sb("bk", [128, 1])
    w["b1"] = P.sb("b1", [128, 1])
    w["b2"] = P.sb("b2", [128, 1])
    w["inv_tc"] = P.sb("inv_tc", [128, 1])
    w["fc1"] = P.sb("fc1", [N_ATTR, 100])
    for n in ("h1", "h2", "h3"):
        w[n] = P.sb(n, [100, 128])
    w["sel_sh"] = P.sb("sel_sh", [N_ATTR, 128])
    w["sel_sh0"] = P.sb("sel_sh0", [N_ATTR, 128])
    w["rel"] = P.sb("rel", [64, 128])
    w["W1c"] = P.sb("W1c", [1, 128])
    w["sel_type"] = P.sb("sel_type", [3, 64])
    w["sel_dt"] = P.sb("sel_dt", [3, 128])
    w["iota64"] = P.sb("iota64", [64, 1])
    w["pick32"], w["pick16"] = P.sb("pick32", [128, 4]), P.sb("pick16", [128, 8])
    w["bias2r"] = P.sb("bias2r", [128, D])
    with ExitStack() as ctx:
        Q = Phase(nc, ctx, "prep")
        l1w = Q.sb("l1w", [128, 256])
        acol = Q.sb("acol", [128, 2])
        asel = Q.sb("asel", [128, 2, 128])
        w2t = Q.sb("w2t", [128, 128])
        r2c = Q.sb("r2c", [128, 1])
        tcn = Q.sb("tcn", [128, 1])
        ones = Q.sb("ones", [128, 128])
        pt = Q.ps("pt")
        pa = Q.ps("pa")
        zeroed, made, loaded, transposed, turned, combined = (
            Q.sem(n) for n in ("zeroed", "made", "loaded", "transposed", "turned", "combined"))
        n_loads = [0]
        zero_first = ("Wsi", "g1", "g2", "o1", "o2", "o3", "fc1", "h1", "h2", "h3")
        with nc.Block() as block:
            @block.vector
            def _(dve):
                for n in zero_first:
                    last = nc.vector.memset(w[n][:, :], 0.0)
                nc.vector.memset(w["eps"][:, :], LN_EPS)
                last = nc.vector.memset(w["ones_row"][:, :], 1.0)
                last.then_inc(zeroed, 1)

            @block.sync
            def _(sp):
                sp.wait_ge(zeroed, 1)

                def load(dst, src):
                    sp.dma_start(dst, src, allow_slow_non_contiguous=True).then_inc(loaded, 16)
                    n_loads[0] += 1

                def col(v):
                    return v.rearrange("(p a) -> p a", a=1)

                def row(v):
                    return v.rearrange("(a n) -> a n", a=1)

                def vec(mat, m, cols_from=MUL):
                    return mat[MUL + m:128:3, cols_from + m:128:3]

                load(w["Wsi"][0:MUL, 0:MUL], A["L0_gnn_W_si_0e"])
                load(w["g1"][0:MUL, 0:MUL], A["L0_gnn_W_l1_0e"])
                load(w["o1"][0:MUL, 0:MUL], A["L0_gnn_W_l2_0e"][0:MUL, :])
                load(w["h1"][:, 0:MUL], A["L0_gnn_W_fc2"][:, 0:MUL])
                for m in range(3):
                    load(vec(w["Wsi"], m), A["L0_gnn_W_si_1o"])
                    load(w["g1"][0:MUL, MUL + m:128:3], A["L0_gnn_W_l1_0e"])
                    load(vec(w["g2"], m), A["L0_gnn_W_l1_1o"])
                    load(w["o3"][MUL + m:128:3, 0:MUL], A["L0_gnn_W_l2_0e"][MUL:2 * MUL, :])
                    load(vec(w["o1"], m), A["L0_gnn_W_l2_1o"][0:MUL, :])
                    load(vec(w["o2"], m), A["L0_gnn_W_l2_1o"][MUL:2 * MUL, :])
                    for k in range(3):
                        load(w[f"h{k + 1}"][:, MUL + m:128:3], A["L0_gnn_W_fc2"][:, (k + 1) * MUL:(k + 2) * MUL])
                load(w["fc1"][N_SH:N_ATTR, :], A["L0_gnn_W_fc1"])
                load(l1w[:, :], A["L1_gnn_W"])
                for t in range(TPC):
                    load(w["bias1"][:, t, :], row(A["L1_gnn_b"]))
                    load(w["bias2"][:, t, :], row(A["L2_gnn_bias"]))
                load(w["W2"][:, :], A["L2_gnn_W"])
                load(acol[:, 0:1], A["L2_gnn_attn_src"].rearrange("h (d a) -> (h d) a", a=1))
                load(acol[:, 1:2], A["L2_gnn_attn_dst"].rearrange("h (d a) -> (h d) a", a=1))
                load(w["rel"][:, :], A["L3_gnn_rel_table"])
                load(w["Wq"][:, :], A["L3_gnn_Wq"])
                load(w["Wk"][:, :], A["L3_gnn_Wk"])
                load(w["Wv"][:, :], A["L3_gnn_Wv"])
                load(w["bias2r"][:, :], A["L2_gnn_bias"].partition_broadcast(128))
                load(w["bq"][:, :], col(A["L3_gnn_bq"]))
                load(w["bk"][:, :], col(A["L3_gnn_bk"]))
                load(w["bias3v"][:, :], col(A["L3_gnn_bv"]))
                load(w["b1"][:, :], col(A["L3_gnn_b1"]))
                load(w["R1a"][:, :], A["L3_gnn_W1"][0:128, :])
                load(w["R1b"][:, :], A["L3_gnn_W1"][128:256, :])
                load(w["W1c"][:, :], A["L3_gnn_W1"][256:257, :])
                load(r2c[:, :], A["L3_gnn_W2"])
                load(w["b2"][:, :], A["L3_gnn_b2"].partition_broadcast(128))
                load(tcn[:, :], A["L3_gnn_time_coeff"].partition_broadcast(128))

            @block.gpsimd
            def _(pool):
                for n in ("ident", "identb", "heads16", "heads32", "sel_sh", "sel_sh0", "sel_type", "pick32", "pick16"):
                    nc.gpsimd.memset(w[n][:, :], 1.0)
                nc.gpsimd.memset(ones[:, :], 1.0)
                nc.gpsimd.memset(w["sel_dt"][:, :], 0.0)
                pool.drain()

                def keep(t, pattern, base, cm, op):
                    return nc.gpsimd.affine_select(out=t, in_=t, compare_op=op, fill=0.0, base=base,
                                                   pattern=pattern, channel_multiplier=cm)

                for n in ("ident", "identb"):
                    keep(w[n][:, :], [[-1, 128]], 0, 1, ALU.is_equal)
                for n, size in (("heads16", 16), ("heads32", 32)):
                    v = w[n][:, :].rearrange("p (h d) -> p h d", d=size)
                    keep(v, [[-size, 128 // size], [0, size]], 0, 1, ALU.is_ge)
                    pool.drain()
                    keep(v, [[size, 128 // size], [0, size]], size - 1, -1, ALU.is_ge)
                keep(w["sel_sh"][:, 0:MUL], [[0, MUL]], 0, 1, ALU.is_equal)
                keep(w["sel_sh"][:, MUL:128].rearrange("p (u m) -> p u m", m=3), [[0, MUL], [-1, 3]], -1, 1,
                     ALU.is_equal)
                for n, size in (("pick32", 32), ("pick16", 16)):
                    keep(w[n][:, :], [[-size, 128 // size]], 0, 1, ALU.is_equal)
                keep(w["sel_sh0"][:, :], [[0, 128]], 0, 1, ALU.is_equal)
                keep(w["sel_type"][:, :], [[0, 64]], 0, 1, ALU.is_equal)
                s = w["sel_dt"]
                nc.gpsimd.affine_select(out=s[:, :], in_=s[:, :], compare_op=ALU.not_equal, fill=1.0, base=-1,
                                        pattern=[[0, 128]], channel_multiplier=1)
                pool.drain()
                nc.gpsimd.affine_select(out=s[:, :], in_=s[:, :], compare_op=ALU.not_equal, fill=-1.0, base=-2,
                                        pattern=[[0, 128]], channel_multiplier=1)
                nc.gpsimd.iota(w["iota64"][:, :], pattern=[[0, 1]], base=0, channel_multiplier=1,
                               allow_small_or_imprecise_dtypes=True)
                pool.drain()
                nc.gpsimd.memset(ones[:, 0:1], 1.0).then_inc(made, 1)

            @block.tensor
            def _(pe):
                pe.wait_ge(made, 1)
                pe.wait_ge(loaded, 16 * n_loads[0])
                nc.tensor.transpose(pt[:, 0:128], l1w[:, 0:128], w["ident"][:, :])
                nc.tensor.transpose(pt[:, 128:256], l1w[:, 128:256], w["ident"][:, :])
                nc.tensor.transpose(pt[:, 256:384], w["W2"][:, :], w["ident"][:, :]).then_inc(transposed, 1)
                pe.wait_ge(turned, 1)
                nc.tensor.matmul(pa[:, 0:128], w2t[:, :], asel[:, 0, :], start=True, stop=True)
                nc.tensor.matmul(pa[:, 128:256], w2t[:, :], asel[:, 1, :], start=True, stop=True).then_inc(combined, 1)

            @block.vector
            def _(dve):
                dve.wait_ge(made, 1)
                dve.wait_ge(loaded, 16 * n_loads[0])
                dve.wait_ge(transposed, 1)
                v = nc.vector
                v.tensor_copy(w["W1a"][:, :], pt[:, 0:128])
                v.tensor_copy(w["W1b"][:, :], pt[:, 128:256])
                v.tensor_copy(w2t[:, :], pt[:, 256:384])
                for k in range(2):
                    v.tensor_scalar(asel[:, k, :], w["heads32"][:, :], acol[:, k:k + 1], None, ALU.mult)
                v.tensor_scalar(w["R2"][:, :], ones[:, :], r2c[:, 0:1], None, ALU.mult)
                for n, s in (("Wsi", MUL ** -0.5), ("g1", MUL ** -0.5), ("g2", MUL ** -0.5),
                             ("o1", 0.5 / 4 / 8), ("o2", 0.5 / 4 / 8), ("o3", 0.5 / 4 / 8),
                             ("h1", 0.1), ("h2", 0.1), ("h3", 0.1), ("fc1", N_LEN ** -0.5)):
                    v.tensor_scalar(w[n][:, :], w[n][:, :], s, None, ALU.mult)
                v.tensor_scalar(w["inv_tc"][:, :], tcn[:, :], -1.0, None, ALU.mult)
                dve.drain()
                v.tensor_tensor(w["W1sum"][:, :], w["W1a"][:, :], w["W1b"][:, :], ALU.add).then_inc(turned, 1)
                v.tensor_tensor(w["WsiI"][:, :], w["Wsi"][:, :], w["ident"][:, :], ALU.add)
                v.tensor_scalar(w["o3"][:, 0:MUL], w["o3"][:, 0:MUL], 3.0 ** -0.5, None, ALU.mult)
                v.tensor_tensor(w["inv_tc"][:, :], w["inv_tc"][:, :], tcn[:, :], ALU.max)
                dve.drain()
                v.tensor_scalar(w["inv_tc"][:, :], w["inv_tc"][:, :], 1e-9, None, ALU.add)
                dve.drain()
                v.reciprocal(w["inv_tc"][:, :], w["inv_tc"][:, :])
                dve.wait_ge(combined, 1)
                v.tensor_copy(w["Asrc"][:, :], pa[:, 0:128])
                v.tensor_copy(w["Adst"][:, :], pa[:, 128:256])
                dve.drain()
                v.tensor_tensor(w["Aself"][:, :], w["Asrc"][:, :], w["Adst"][:, :], ALU.add)
        end_phase(nc, Q)
    return w


def build_isolated(nc, g, w, T):
    N = g.N
    n = -(-N // CH)
    with ExitStack() as ctx:
        P = Phase(nc, ctx, "iso")
        R = 4
        x_in = P.sb("x_in", [128, R, TPC, D])
        normed = P.sb("normed", [128, 4, R, TPC, D])
        xT = P.sb("xT", [128, 3, 2, CH])
        y = P.sb("y", [128, 3, 2, TPC, D])
        low = P.sb("low", [128, TPC, D])
        stats = P.sb("stats", [128, 16, 6])
        mv = P.sb("mv", [128, 16, 2])
        rstd, shift = P.sb("rstd", [128, 16]), P.sb("shift", [128, 16])
        psT = [P.ps(f"psT{k}") for k in range(3)]
        psZ = [[P.ps("psZ00"), P.ps("psZ01")], [P.ps("psZ1")], [P.ps("psZ2")]]
        x_loaded = P.sems("x_loaded", R)
        stored = [P.sems(f"stored{k}_", R) for k in range(4)]
        transposed, xT_copied, z_done, y_done = (P.sems(s, 3) for s in ("transposed", "xT_copied", "z_done", "y_done"))
        elu_done, stats_done, rstd_done, shift_done = (
            P.sem(s) for s in ("elu_done", "stats_done", "rstd_done", "shift_done"))
        applied = P.sems("applied", 4)
        T_LAGS, A_LAGS = [0, 3, 6], [1, 4, 7, 8]
        B_LAGS = [k + 1 for k in A_LAGS]
        weights = [w["WsiI"], w["W1sum"], w["W2"]]
        targets = [T.x1, T.x2, T.x34[:, 0, :], T.x34[:, 1, :]]
        BY_ACT = (0, 1, 3)

        def rows(table, c):
            start = N - CH if isinstance(c.i, int) and c.i == n - 1 else c.i * CH
            part = table[start:start + CH, :] if isinstance(start, int) else table[bass.ds(start, CH), :]
            return part.rearrange("(p t) c -> p t c", t=TPC)

        def source(l, c):
            return x_in[:, c.slot] if l == 0 else normed[:, l - 1, c.slot]

        def present(cs, lags):
            ls = [l for l in range(len(lags)) if cs[l] is not None]
            if not ls:
                return None
            return ls[0], ls[-1] + 1, cs[ls[0]].i + lags[ls[0]]

        def before_norm(l, c):
            return tiles(psZ[0][c.slot % 2][:, :]) if l == 0 else source(3, c) if l == 3 else y[:, l, c.slot % 2]

        with nc.Block() as block:
            @block.sync
            def _(sp):
                def step(cs):
                    c = cs[0]
                    if c is not None:
                        if c.has(R):
                            sp.wait_ge(transposed[0], c.count(R))
                        sp.dma_start(x_in[:, c.slot], rows(T.x, c)).then_inc(x_loaded[c.slot], 16)
                    for l in range(4):
                        c = cs[l + 1]
                        if c is not None:
                            sp.wait_ge(applied[l], c.count())
                            if isinstance(c.i, int) and c.i == n - 1:
                                sp.wait_ge(stored[l][(n - 2) % R], 16 * turns(n - 1, (n - 2) % R, R))
                            sp.dma_start(rows(targets[l], c), normed[:, l, c.slot]).then_inc(stored[l][c.slot], 16)
                run_chunks(sp, n, R, [0] + [k + 1 for k in B_LAGS], step)
                for l in range(4):
                    for s in range(R):
                        sp.wait_ge(stored[l][s], 16 * turns(n, s, R))

            @block.tensor
            def _(pe):
                def step(cs):
                    for l in range(3):
                        c = cs[l + 3]
                        if c is None:
                            continue
                        pe.wait_ge(xT_copied[l], c.count())
                        if l == 0:
                            if c.has(2):
                                pe.wait_ge(applied[0], c.count(2))
                        elif c.has(1):
                            pe.wait_ge(y_done[1] if l == 1 else elu_done, c.count(1))
                        z = psZ[l][c.slot % len(psZ[l])]
                        if l > 0:
                            bias = w["bias1"] if l == 1 else w["bias2"]
                            nc.tensor.matmul(z[:, :], w["ones_row"][:, :],
                                             bias[:, :, :].rearrange("a t c -> a (t c)"), start=True, stop=False)
                        for t in range(TPC):
                            last = nc.tensor.matmul(z[:, t * D:(t + 1) * D], xT[:, l, c.slot % 2, t * D:(t + 1) * D],
                                                    weights[l][:, :], start=l == 0, stop=l == 0 or t == TPC - 1)
                        last.then_inc(z_done[l], 1)
                    for l in range(3):
                        c = cs[l]
                        if c is None:
                            continue
                        if l == 0:
                            pe.wait_ge(x_loaded[c.slot], c.landed(16))
                        else:
                            pe.wait_ge(applied[l - 1], c.count())
                        if c.has(1):
                            pe.wait_ge(xT_copied[l], c.count(1))
                        transpose4(nc, psT[l], source(l, c), w["ident"]).then_inc(transposed[l], 1)
                run_chunks(pe, n, R, T_LAGS + A_LAGS[:3], step)

            @block.scalar
            def _(act):
                nc.scalar.preload_act_table_set(ACT_SET)
                def step(cs):
                    now = present(cs[7:], B_LAGS)
                    if now is not None:
                        lo, hi, t = now
                        act.wait_ge(shift_done, t - 1)
                        for l in range(lo, hi):
                            if l not in BY_ACT:
                                continue
                            c = cs[7 + l]
                            if c.slot_used():
                                act.wait_ge(stored[l][c.slot], c.landed(16, 1))
                            for k in range(TPC):
                                j = 4 * l + k
                                last = nc.scalar.activation(normed[:, l, c.slot, k, :], before_norm(l, c)[:, k, :],
                                                            ACT.Identity, bias=shift[:, j:j + 1], scale=rstd[:, j:j + 1])
                            last.then_inc(applied[l], 1)
                    c = cs[3 + 2]
                    if c is not None:
                        act.wait_ge(y_done[2], c.count())
                        nc.scalar.activation(low[:, :, :], tiles(psZ[2][0][:, :]), ACT.Relu, scale=-1.0)
                        act.drain()
                        nc.scalar.activation(low[:, :, :], low[:, :, :], ACT.Exp, scale=-1.0).then_inc(elu_done, 1)
                    for l in range(3):
                        c = cs[l]
                        if c is None:
                            continue
                        act.wait_ge(transposed[l], c.count())
                        if c.has(2):
                            act.wait_ge(z_done[l], c.count(2))
                        nc.scalar.activation(xT[:, l, c.slot % 2, :], psT[l][:, :], ACT.Copy).then_inc(xT_copied[l], 1)
                    now = present(cs[3:7], A_LAGS)
                    if now is not None:
                        lo, hi, t = now
                        act.drain()
                        act.wait_ge(stats_done, t)
                        ln_rstd(nc, act, mv[:, lo * 4:hi * 4, 1], rstd[:, lo * 4:hi * 4], w["eps"]).then_inc(rstd_done, 1)
                run_chunks(act, n, R, T_LAGS + A_LAGS + B_LAGS, step)

            @block.vector
            def _(dve):
                def step(cs):
                    a, b = cs[0:4], cs[4:8]
                    now_b = present(b, B_LAGS)
                    if now_b is not None:
                        lo, hi, t = now_b
                        dve.wait_ge(rstd_done, t - 1)
                        for l in BY_ACT:
                            if b[l] is not None and b[l].has(1):
                                dve.wait_ge(applied[l], b[l].count(1))
                        nc.vector.scalar_tensor_tensor(shift[:, lo * 4:hi * 4], mv[:, lo * 4:hi * 4, 0], -1.0,
                                                       rstd[:, lo * 4:hi * 4], ALU.mult, ALU.mult).then_inc(shift_done, 1)
                        if b[2] is not None:
                            if b[2].slot_used():
                                dve.wait_ge(stored[2][b[2].slot], b[2].landed(16, 1))
                            ln_apply(nc, normed[:, 2, b[2].slot], y[:, 2, b[2].slot % 2], mv[:, 8:12], rstd[:, 8:12])\
                                .then_inc(applied[2], 1)
                    now_a = present(a, A_LAGS)
                    if now_a is None:
                        return
                    lo, hi, t = now_a
                    early = [l for l in range(lo, hi) if l != 2]

                    def add_x(l):
                        if a[l] is not None:
                            dve.wait_ge(z_done[l], a[l].count())
                            nc.vector.scalar_tensor_tensor(y[:, l, a[l].slot % 2], tiles(psZ[l][0][:, :]), 0.0,
                                                           source(l, a[l]), ALU.max, ALU.add).then_inc(y_done[l], 1)

                    def measure(l):
                        if a[l] is not None:
                            ln_stats(nc, before_norm(l, a[l]), stats, mv, at=4 * l)

                    def aggregate(l):
                        for k in range(4 * l, 4 * l + 4):
                            last = nc.vector.bn_aggr(mv[:, k, :], stats[:, k, :])
                        return last

                    if a[0] is not None:
                        dve.wait_ge(z_done[0], a[0].count())
                    measure(0)
                    add_x(1)
                    dve.drain()
                    measure(3)
                    add_x(2)
                    measure(1)
                    dve.drain()
                    for l in early:
                        last = aggregate(l)
                    if a[2] is not None:
                        dve.wait_ge(elu_done, a[2].count())
                        nc.vector.scalar_tensor_tensor(y[:, 2, a[2].slot % 2], low[:, :, :], -1.0,
                                                       y[:, 2, a[2].slot % 2], ALU.add, ALU.add)
                        dve.drain()
                        measure(2)
                        dve.drain()
                        last = aggregate(2)
                    last.then_inc(stats_done, 1)
                    dve.drain()
                run_chunks(dve, n, R, A_LAGS + B_LAGS, step)
        end_phase(nc, P)


class Sizes:
    def __init__(self, N, E):
        self.N, self.E = N, E
        self.NQ = -(-N // 128)
        self.LE = 125
        self.GT = 4
        self.TT = E // self.LE
        assert E % self.LE == 0 and self.TT % (2 * self.GT) == 0
        self.ED = -(-E // CH) * CH
        self.EC = -(-2 * E // CH) * CH


class Tables:
    pass


def build_sort(nc, g, w, T, A):
    N, E, NQ, LE, GT, TT = g.N, g.E, g.NQ, g.LE, g.GT, g.TT
    GE = GT * LE
    RING = 2 * GT
    with ExitStack() as ctx:
        P = Phase(nc, ctx, "sort")
        ends = P.sb("ends", [LE, 2, TT], I32)
        kind = P.sb("kind", [LE, TT], I32)
        ew = P.sb("ew", [LE, TT])
        part = P.sb("part", [LE, 2 * TT], I32)
        key = P.sb("key", [LE, 2 * TT])
        lane = P.sb("lane", [LE, 2 * TT])
        quot = P.sb("quot", [LE, 2 * TT])
        iota_q = P.sb("iota_q", [128, NQ], F16)
        iota_l = P.sb("iota_l", [128, 128], F16)
        iota_p = P.sb("iota_p", [128, 1])
        earlier = P.sb("earlier", [LE, LE])
        below = P.sb("below", [128, 128])
        zeros = P.sb("zeros", [128, NQ])
        hist = P.sb("hist", [128, 2, NQ])
        base = P.sb("base", [128, 2, NQ])
        nv_tab = P.sb("nv_tab", [128, NQ])
        row_sum = P.sb("row_sum", [128, 2])
        row_pre = P.sb("row_pre", [128, 2])
        running = P.sb("running", [128, 2, NQ])
        oh_lane = P.sb("oh_lane", [LE, 2, 128], BF16)
        oh_quot = P.sb("oh_quot", [LE, 2, NQ], BF16)
        key_row = P.sb("key_row", [128, 2, GE], I32)
        lane_row = P.sb("lane_row", [128, GE], I32)
        oh_row = P.sb("oh_row", [128, 2, GE])
        junk = P.sb("junk", [LE, 3, NQ])
        junk2 = P.sb("junk2", [LE, LE])
        rank = P.sb("rank", [LE, 2])
        found = P.sb("found", [LE, 3, GT])
        at_c = P.sb("at_c", [LE, 2, GT], I32)
        at_d = P.sb("at_d", [LE, 2, GT], I32)
        out_c = P.sb("out_c", [LE, 2, GT, 2], I32)
        out_d = P.sb("out_d", [LE, 2, GT, REC], I32)
        pad = P.sb("pad", [128, REC], I32)
        ps_look = [[P.ps(f"look{k}{s}") for s in range(2)] for k in range(3)]
        ps_run = P.ps("run")
        loaded, made, cols_ready = P.sem("loaded"), P.sem("made"), P.sem("cols_ready")
        oh1, hist_done = P.sem("oh1"), P.sem("hist_done")
        sums_ready, pre_done, base_ready = P.sem("sums_ready"), P.sem("pre_done"), P.sem("base_ready")
        oh_ready, updated, run_copied, looked, selected = (
            P.sem(s) for s in ("oh_ready", "updated", "run_copied", "looked", "selected"))
        row_ready, row_used, rec_ready = P.sem("row_ready"), P.sem("row_used"), P.sem("rec_ready")
        keys_landed, attrs_landed, scattered = (P.sems(s, 2) for s in ("keys_landed", "attrs_landed", "scattered"))
        padded = P.sem("padded")
        A_keys = [A["dst"], A["src"]]
        full_q = N // 128

        def col(t, c):
            return t[:, c.i:c.i + 1] if isinstance(c.i, int) else t[:, bass.ds(c.i, 1)]

        def group(c):
            s = c.slot // GT
            return Chunk(c.turn * 2 + s, s, c.turn, 2)

        def seg(t, start, size):
            return t[start:start + size] if isinstance(start, int) else t[bass.ds(start, size)]

        with nc.Block() as block:
            @block.sync
            def _(sp):
                with nc.allow_non_contiguous_dma(reason="one word per edge"):
                    for k in range(2):
                        sp.dma_start(ends[:, k, :], A_keys[k].rearrange("(j p) -> p j", p=LE)).then_inc(loaded, 16)
                    sp.dma_start(kind[:, :], A["edge_type_64"].rearrange("(j p) -> p j", p=LE)).then_inc(loaded, 16)
                    sp.dma_start(ew[:, :], A["edge_weight"].rearrange("(j p) -> p j", p=LE)).then_inc(loaded, 16)
                    sp.wait_ge(made, 1)
                    sp.dma_start(nv_tab[:, 0:full_q],
                                 A["node_vec"][0:128 * full_q].rearrange("(q p) -> p q", p=128)).then_inc(loaded, 16)
                    if N % 128:
                        sp.dma_start(nv_tab[0:N % 128, full_q:NQ],
                                     A["node_vec"][128 * full_q:N].rearrange("(p q) -> p q", q=1)).then_inc(loaded, 16)
                n_pads = 0
                for table, width, used, slots in ((T.rec_c, 2, 2 * E, g.EC), (T.rec_d, REC, E, g.ED)):
                    sp.dma_start(table[0:1, :], pad[0:1, 0:width]).then_inc(padded, 16)
                    n_pads += 1
                    at = 1 + used
                    while at < slots + 2:
                        k = min(128, slots + 2 - at)
                        sp.dma_start(table[at:at + k, :], pad[0:k, 0:width]).then_inc(padded, 16)
                        at += k
                        n_pads += 1

                def step(cs):
                    c = cs[0]
                    k = step.k
                    first = c.i - k * (TT // GT)
                    if not isinstance(first, int):
                        first = sp.snap(first)
                    start = first * GE if isinstance(first, int) else sp.snap(first * GE)
                    if c.has(2):
                        sp.wait_ge(row_used, c.count(2))
                    sp.dma_start(key_row[:, c.slot, :], seg(A_keys[k], start, GE).partition_broadcast(128))\
                      .then_inc(keys_landed[c.slot], 16)
                    if k == 0:
                        if c.slot_used():
                            sp.wait_ge(scattered[c.slot], c.landed(16 * 2 * GT, 1))
                        hold(sp, w)
                        for lo, hi, name in ((W_SH, W_SH + N_SH, "edge_attr_4"), (W_LEN, W_LEN + N_LEN, "edge_attr_10")):
                            src = seg(A[name], start, GE)
                            sp.dma_start(out_d[:, c.slot, :, lo:hi], src.rearrange("(j p) c -> p j c", p=LE).bitcast(I32))\
                              .then_inc(attrs_landed[c.slot], 16)
                for step.k in range(2):
                    run_chunks(sp, TT // GT, 2, [0], step, base=step.k * (TT // GT))
                sp.wait_ge(padded, 16 * n_pads)

            @block.gpsimd
            def _(pool):
                nc.gpsimd.memset(nv_tab[:, :], 0.0)
                nc.gpsimd.memset(zeros[:, :], 0.0)
                nc.gpsimd.memset(pad[:, :], 0)
                nc.gpsimd.memset(out_d[:, :, :, :], 0)
                nc.gpsimd.memset(earlier[:, :], 1.0)
                nc.gpsimd.memset(below[:, :], 1.0)
                nc.gpsimd.iota(iota_q[:, :], pattern=[[1, NQ]], base=0, channel_multiplier=0,
                               allow_small_or_imprecise_dtypes=True)
                nc.gpsimd.iota(iota_l[:, :], pattern=[[1, 128]], base=0, channel_multiplier=0,
                               allow_small_or_imprecise_dtypes=True)
                nc.gpsimd.iota(iota_p[:, :], pattern=[[0, 1]], base=0, channel_multiplier=1,
                               allow_small_or_imprecise_dtypes=True)
                pool.drain()
                nc.gpsimd.affine_select(out=earlier[:, :], in_=earlier[:, :], compare_op=ALU.is_gt, fill=0.0, base=0,
                                        pattern=[[-1, LE]], channel_multiplier=1)
                nc.gpsimd.affine_select(out=below[:, :], in_=below[:, :], compare_op=ALU.is_gt, fill=0.0, base=0,
                                        pattern=[[1, 128]], channel_multiplier=-1)
                nc.gpsimd.memset(pad[:, 0:1], N)
                pool.drain()
                nc.gpsimd.memset(zeros[:, 0:1], 0.0).then_inc(made, 1)
                bound_c, bound_d = pool.to_reg(g.EC + 1), pool.to_reg(g.ED + 1)

                def step(cs):
                    c = cs[0]
                    pool.wait_ge(rec_ready, c.count())
                    hold(pool, w)
                    for t in range(GT):
                        pool.indirect_dma_start(T.rec_c, bass.IndirectOffsetOnAxis(ap=at_c[:, c.slot, t:t + 1], axis=0),
                                                out_c[:, c.slot, t, :], None, bounds_check=bound_c, oob_is_err=False)\
                            .then_inc(scattered[c.slot], 16)
                        if step.k == 0:
                            pool.indirect_dma_start(T.rec_d, bass.IndirectOffsetOnAxis(ap=at_d[:, c.slot, t:t + 1], axis=0),
                                                    out_d[:, c.slot, t, :], None, bounds_check=bound_d, oob_is_err=False)\
                                .then_inc(scattered[c.slot], 16)
                for step.k in range(2):
                    run_chunks(pool, TT // GT, 2, [0], step, base=step.k * (TT // GT))
                for s in range(2):
                    pool.wait_ge(scattered[s], 16 * 3 * GT * (TT // GT) // 2)

            @block.tensor
            def _(pe):
                pe.wait_ge(made, 1)
                for k in range(2):
                    def step(cs):
                        c = cs[0]
                        pe.wait_ge(oh1, c.count())
                        nc.tensor.matmul(ps_look[k][0][:, 0:NQ], oh_lane[:, c.slot, :], oh_quot[:, c.slot, :],
                                         start=isinstance(c.i, int) and c.i == k * TT,
                                         stop=isinstance(c.i, int) and c.i == k * TT + TT - 1).then_inc(hist_done, 1)
                    run_chunks(pe, TT, 2, [0], step, base=k * TT)
                pe.wait_ge(sums_ready, 1)
                nc.tensor.matmul(ps_look[2][0][:, 0:2], below[:, :], row_sum[:, :], start=True, stop=True).then_inc(pre_done, 1)
                pe.wait_ge(base_ready, 1)
                pe.wait_ge(loaded, 16 * (6 if N % 128 else 5))
                nc.tensor.matmul(ps_run[:, 0:NQ], w["ident"][:, :], base[:, 0, :], start=True, stop=True).then_inc(updated, 1)
                for k in range(2):
                    def step(cs):
                        c = cs[0]
                        pe.wait_ge(oh_ready, c.count())
                        pe.wait_ge(run_copied, c.count())
                        nc.tensor.matmul(ps_run[:, 0:NQ], oh_lane[:, c.slot % 2, :], oh_quot[:, c.slot % 2, :],
                                         start=False, stop=True, skip_group_check=True).then_inc(updated, 1)
                        gr = group(c)
                        pe.wait_ge(row_ready, gr.count())
                        if c.has(2):
                            pe.wait_ge(selected, c.count(2))
                        t = c.slot % GT
                        oh = oh_row[:, gr.slot, t * LE:(t + 1) * LE]
                        tabs = [running[:, c.slot % 2, :]] + ([base[:, 1, :], nv_tab[:, :]] if k == 0 else [])
                        for i, tab in enumerate(tabs):
                            ins = nc.tensor.matmul(ps_look[i][c.slot % 2][0:LE, 0:NQ], oh, tab, start=True, stop=True)
                        ins.then_inc(looked, 1)
                    run_chunks(pe, TT, RING, [0], step, base=k * TT)

            @block.scalar
            def _(act):
                nc.scalar.preload_act_table_set(ACT_SET)
                act.wait_ge(updated, 1)
                nc.scalar.activation(running[:, 0, :], ps_run[:, 0:NQ], ACT.Copy).then_inc(run_copied, 1)

                def step(cs):
                    c = cs[0]
                    if isinstance(c.i, int) and c.i == 2 * TT - 1:
                        return
                    act.wait_ge(updated, c.i + 2)
                    if c.has(1):
                        act.wait_ge(looked, c.count(1))
                    nc.scalar.activation(running[:, (c.slot + 1) % 2, :], ps_run[:, 0:NQ], ACT.Copy).then_inc(run_copied, 1)
                run_chunks(act, 2 * TT, RING, [0], step)

            @block.vector
            def _(dve):
                v = nc.vector
                dve.wait_ge(made, 1)
                dve.wait_ge(loaded, 16 * (6 if N % 128 else 5))
                both = ends[:, :, :].rearrange("p k j -> p (k j)")
                v.tensor_copy(key[:, :], both)
                v.tensor_scalar(part[:, :], both, 127, None, ALU.bitwise_and)
                dve.drain()
                v.tensor_copy(lane[:, :], part[:, :])
                dve.drain()
                v.tensor_scalar(part[:, :], both, 7, None, ALU.logical_shift_right)
                dve.drain()
                v.tensor_copy(quot[:, :], part[:, :])
                dve.drain()

                def one_hots(c, s, sem):
                    v.tensor_scalar(oh_lane[:, s, :], iota_l[0:LE, :], col(lane, c), None, ALU.is_equal)
                    v.tensor_scalar(oh_quot[:, s, :], iota_q[0:LE, :], col(quot, c), None, ALU.is_equal)\
                     .then_inc(sem, 1)

                def step(cs):
                    if cs[0].has(2):
                        dve.wait_ge(hist_done, cs[0].count(2))
                    one_hots(cs[0], cs[0].slot, oh1)
                run_chunks(dve, 2 * TT, 2, [0], step)
                dve.wait_ge(hist_done, 2 * TT)
                for k in range(2):
                    v.tensor_copy(hist[:, k, :], ps_look[k][0][:, 0:NQ])
                dve.drain()
                v.tensor_reduce(row_sum[:, :], hist[:, :, :], AX_X, ALU.add).then_inc(sums_ready, 1)
                dve.wait_ge(pre_done, 1)
                v.tensor_copy(row_pre[:, :], ps_look[2][0][:, 0:2])
                dve.drain()
                for k in range(2):
                    v.tensor_tensor_scan(base[:, k, :], hist[:, k, :], zeros[:, :], row_pre[:, k:k + 1], ALU.add, ALU.add)
                dve.drain()
                v.tensor_tensor(base[:, :, :], base[:, :, :], hist[:, :, :], ALU.subtract)
                dve.drain()
                v.scalar_tensor_tensor(base[:, 0, :], base[:, 0, :], 1.0, base[:, 1, :], ALU.add, ALU.add).then_inc(base_ready, 1)

                for k in range(2):
                    def step(cs):
                        c = cs[0]
                        dve.drain()
                        if c is not None:
                            gr = group(c)
                            if c.slot % GT == 0:
                                dve.wait_ge(keys_landed[gr.slot], gr.landed(16))
                                if c.has(GT + 1):
                                    dve.wait_ge(looked, c.count(GT + 1))
                                v.tensor_scalar(lane_row[:, :], key_row[:, gr.slot, :], 127, None, ALU.bitwise_and)
                                dve.drain()
                                v.tensor_scalar(oh_row[:, gr.slot, :], lane_row[:, :], iota_p[:, 0:1], None,
                                                ALU.is_equal).then_inc(row_ready, 1)
                            if c.has(1):
                                dve.wait_ge(updated, c.count(1))
                            one_hots(c, c.slot % 2, oh_ready)
                            t = c.slot % GT
                            ins = v.scalar_tensor_tensor(junk2[:, :], key_row[0:LE, gr.slot, t * LE:(t + 1) * LE],
                                                         col(key, c), earlier[:, :], ALU.is_equal, ALU.mult,
                                                         accum_out=rank[:, c.slot % 2:c.slot % 2 + 1])
                            if t == GT - 1:
                                ins.then_inc(row_used, 1)
                        c = cs[1]
                        if c is None:
                            return
                        gr = group(c)
                        t = c.slot % GT
                        dve.wait_ge(looked, c.count())
                        for i in range(3 if k == 0 else 1):
                            first = rank[:, c.slot % 2:c.slot % 2 + 1] if i == 0 else 0.0
                            ins = v.tensor_tensor_reduce(junk[:, i, :], ps_look[i][c.slot % 2][0:LE, 0:NQ],
                                                         oh_quot[:, c.slot % 2, :], 1.0, first, ALU.mult, ALU.add,
                                                         found[:, i, t:t + 1])
                        ins.then_inc(selected, 1)
                        if t != GT - 1:
                            return
                        rel = c.i - (GT - 1 + k * TT)
                        dve.drain()
                        wait_scattered(gr, k)
                        def cols(tab, start):
                            return tab[:, start:start + GT] if isinstance(start, int) else tab[:, bass.ds(start, GT)]
                        v.tensor_copy(at_c[:, gr.slot, :], found[:, 0, :])
                        v.tensor_copy(out_c[:, gr.slot, :, 0], cols(ends[:, k, :], rel))
                        if k == 0:
                            dve.wait_ge(attrs_landed[gr.slot], gr.landed(32))
                            v.tensor_copy(out_c[:, gr.slot, :, 1], cols(ends[:, 1, :], rel))
                            v.tensor_tensor(at_d[:, gr.slot, :], found[:, 0, :], found[:, 1, :], ALU.subtract)
                            v.tensor_copy(out_d[:, gr.slot, :, W_DST], cols(ends[:, 0, :], rel))
                            v.tensor_copy(out_d[:, gr.slot, :, W_SRC], cols(ends[:, 1, :], rel))
                            v.tensor_copy(out_d[:, gr.slot, :, W_TYPE], cols(kind[:, :], rel))
                            v.tensor_copy(out_d[:, gr.slot, :, W_EW], cols(ew[:, :].bitcast(I32), rel))
                            v.tensor_copy(out_d[:, gr.slot, :, W_NV], found[:, 2, :].bitcast(I32))
                        else:
                            v.tensor_copy(out_c[:, gr.slot, :, 1], cols(ends[:, 0, :], rel))
                        dve.drain().then_inc(rec_ready, 1)

                    def wait_scattered(gr, k):
                        half = TT // GT // 2
                        if k == 0:
                            if gr.slot_used():
                                dve.wait_ge(scattered[gr.slot], gr.landed(16 * 2 * GT, 1))
                        else:
                            dve.wait_ge(scattered[gr.slot], (gr.turn - half) * (16 * GT) + 16 * 2 * GT * half)
                    run_chunks(dve, TT, RING, [0, 1], step, base=k * TT)
        end_phase(nc, P)


class Slots:

    RING = 4

    def __init__(self, P, nc, g, w, table, width, n, backwards):
        self.nc, self.g, self.w, self.table, self.width, self.n, self.back = nc, g, w, table, width, n, backwards
        R = self.RING
        self.rec = P.sb("rec", [128, R, TPC, width], I32)
        self.near = P.sb("near", [128, R, 2, TPC], I32)
        self.same = P.sb("same", [128, R, 2, TPC], BF16)
        self.inner = P.sb("inner", [128, R, TPC])
        self.row = P.sb("row", [128, R, TPC])
        self.to = P.sb("to", [128, R, TPC], I32)
        self.of = P.sb("of", [128, R, 2, TPC], I32)
        self.landed = P.sems("rec_landed", R)
        self.ready = P.sem("idx_ready")

    def pos(self, c):
        return self.n - 1 - c.i if self.back else c.i

    def start(self, eng, c):
        p = self.pos(c)
        return p * CH if isinstance(p, int) else eng.snap(p * CH)

    def rows(self, t, start, off=0):
        part = t[start + off:start + off + CH] if isinstance(start, int) else t[bass.ds(start + off, CH)]
        return part

    def load(self, sp, c, start):
        R = self.rows
        with self.nc.allow_non_contiguous_dma(reason="one word per slot"):
            sp.dma_start(self.rec[:, c.slot], R(self.table, start, 1).rearrange("(t p) w -> p t w", p=128))\
              .then_inc(self.landed[c.slot], 16)
            for k in range(2):
                sp.dma_start(self.near[:, c.slot, k, :],
                             R(self.table, start, 2 * k)[:, 0].rearrange("(t p) -> p t", p=128))\
                  .then_inc(self.landed[c.slot], 16)

    def index(self, dve, c, other_scale=1, to_scale=1, to_plus=0):
        v = self.nc.vector
        dve.wait_ge(self.landed[c.slot], c.landed(48))
        s = c.slot
        node = self.rec[:, s, :, 0]
        first, last = (1, 0) if self.back else (0, 1)
        v.tensor_tensor(self.same[:, s, 0, :], node, self.near[:, s, first, :], ALU.is_equal)
        v.tensor_tensor(self.inner[:, s, :], node, self.near[:, s, last, :], ALU.is_equal)
        v.tensor_scalar(self.of[:, s, 1, :], node, self.g.N - 1, other_scale, ALU.min, ALU.mult)
        v.tensor_scalar(self.of[:, s, 0, :], self.rec[:, s, :, 1], other_scale, None, ALU.mult)
        if to_scale != 1:
            v.tensor_scalar(self.row[:, s, :], node, to_scale, to_plus, ALU.mult, ALU.add)
            node = self.row[:, s, :]
        dve.drain()
        v.tensor_scalar(self.same[:, s, 1, :], self.same[:, s, 0, :], -1.0, -NEG, ALU.add, ALU.mult)
        v.scalar_tensor_tensor(self.to[:, s, :], self.inner[:, s, :], float(FAR), node, ALU.mult, ALU.add)
        dve.drain().then_inc(self.ready, 1)

    def gather(self, pool, c, which, out, table, bound, sem):
        for t in range(TPC):
            pool.indirect_dma_start(out[:, c.slot, t, :], None, table,
                                    bass.IndirectOffsetOnAxis(ap=self.of[:, c.slot, which, t:t + 1], axis=0),
                                    bounds_check=bound, oob_is_err=False).then_inc(sem[c.slot], 16)

    def scatter(self, pool, c, rows, table, bound, sem):
        for t in range(TPC):
            pool.indirect_dma_start(table, bass.IndirectOffsetOnAxis(ap=self.to[:, c.slot, t:t + 1], axis=0),
                                    rows[:, c.slot, t, :], None,
                                    bounds_check=bound, oob_is_err=False).then_inc(sem[c.slot], 16)


def scan(nc, S, out, mask, data, carry, op0, op1):
    if S.back:
        out, mask, data = out[:, ::-1], mask[:, ::-1], data[:, ::-1]
    return nc.vector.tensor_tensor_scan(out, mask, data, carry if carry is not None else 0.0, op0, op1)


def edge_col(S, t):
    return t[:, 0:1] if S.back else t[:, CH - 1:CH]


def turns(n, slot, ring):
    return (n - slot + ring - 1) // ring


def build_layer0(nc, g, w, T, A):
    n = g.ED // CH
    with ExitStack() as ctx:
        P = Phase(nc, ctx, "l0")
        S = Slots(P, nc, g, w, T.rec_d, REC, n, False)
        R = S.RING
        xs = P.sb("xs", [128, R, TPC, D])
        xd = P.sb("xd", [128, R, TPC, D])
        out = P.sb("out", [128, R, TPC, D])
        xsT = P.sb("xsT", [128, CH])
        xdT = P.sb("xdT", [128, 2, CH])
        attrT = P.sb("attrT", [N_ATTR, CH])
        hT = P.sb("hT", [100, CH])
        mask = P.sb("mask", [128, 2, CH])
        sh = P.sb("sh", [128, 2, CH])
        part = P.sb("part", [128, 3, CH])
        msg = P.sb("msg", [128, 3, CH])
        agg = P.sb("agg", [128, 2, CH])
        y = P.sb("y", [128, TPC, D])
        stats, mv, rstd = P.sb("stats", [128, 4, 6]), P.sb("mv", [128, 4, 2]), P.sb("rstd", [128, 4])
        ps = [P.ps(f"ps{k}") for k in range(8)]
        names = ("tr", "trd", "h", "m", "s1", "s2", "g", "w", "o", "z")
        pe_ = {k: P.sem("pe_" + k) for k in names}
        ac_ = {k: P.sem("ac_" + k) for k in ("tr", "trd", "h", "m", "s1", "s2", "rstd")}
        ve_ = {k: P.sem("ve_" + k) for k in ("part", "msg", "agg", "y", "stats", "out")}
        gathered, scattered, saved = P.sems("gathered", R), P.sems("scattered", R), P.sems("saved", R)
        lags = [0, 2, 3]
        with nc.Block() as block:
            @block.sync
            def _(sp):
                def step(cs):
                    c = cs[0]
                    if c is not None:
                        start = S.start(sp, c)
                        if c.slot_used():
                            sp.wait_ge(scattered[c.slot], c.landed(64, 1))
                        hold(sp, w)
                        if c.slot_used():
                            sp.wait_ge(saved[c.slot], c.landed(16, 1))
                        hold(sp, w)
                        S.load(sp, c, start)
                    c = cs[1]
                    if c is not None:
                        start = S.start(sp, c)
                        sp.wait_ge(ve_["out"], c.count())
                        hold(sp, w)
                        sp.dma_start(S.rows(T.x1_slot, start).rearrange("(t p) c -> p t c", p=128), out[:, c.slot])\
                          .then_inc(saved[c.slot], 16)
                run_chunks(sp, n, R, [0, 3], step)
                for s in range(R):
                    sp.wait_ge(saved[s], 16 * turns(n, s, R))

            @block.gpsimd
            def _(pool):
                bound = pool.to_reg(g.N - 1)

                def step(cs):
                    c = cs[0]
                    if c is not None:
                        pool.wait_ge(S.ready, c.count())
                        hold(pool, w)
                        S.gather(pool, c, 0, xs, T.x, bound, gathered)
                        S.gather(pool, c, 1, xd, T.x, bound, gathered)
                    c = cs[1]
                    if c is not None:
                        pool.wait_ge(ve_["out"], c.count())
                        hold(pool, w)
                        S.scatter(pool, c, out, T.x1, bound, scattered)
                run_chunks(pool, n, R, [0, 2], step)
                for s in range(R):
                    pool.wait_ge(scattered[s], 64 * turns(n, s, R))

            @block.tensor
            def _(pe):
                mm = nc.tensor.matmul

                def step(cs):
                    a, b = cs
                    if a is not None:
                        pe.wait_ge(gathered[a.slot], a.landed(128))
                        if a.has(1):
                            pe.wait_ge(ac_["trd"], a.count(1))
                        if a.has(1):
                            pe.wait_ge(ac_["s1"], a.count(1))
                        transpose4(nc, ps[0], xs[:, a.slot], w["ident"])
                        for t in range(TPC):
                            last = nc.tensor.transpose(ps[1][0:N_ATTR, t * TILE:(t + 1) * TILE],
                                                       S.rec[:, a.slot, t, W_SH:W_SH + N_ATTR].bitcast(F32),
                                                       w["ident"][:, :])
                        last.then_inc(pe_["tr"], 1)
                        if a.has(1):
                            pe.wait_ge(ac_["m"], a.count(1))
                        spread(nc, ps[2], S.same[:, a.slot, 0, :], w["identb"]).then_inc(pe_["m"], 1)
                        pe.wait_ge(ac_["tr"], a.count())
                        transpose4(nc, ps[0], xd[:, a.slot], w["ident"]).then_inc(pe_["trd"], 1)
                        mm(ps[1][0:100, :], w["fc1"][:, :], attrT[:, :], start=True, stop=True).then_inc(pe_["h"], 1)
                        if a.has(1):
                            pe.wait_ge(ve_["msg"], a.count(1))
                        mm(ps[3][:, :], w["g1"][:, :], xsT[:, :], start=True, stop=True)
                        mm(ps[4][:, :], w["g2"][:, :], xsT[:, :], start=True, stop=True).then_inc(pe_["g"], 1)
                        pe.wait_ge(ac_["h"], a.count())
                        mm(ps[1][:, :], w["sel_sh"][:, :], attrT[:, :], start=True, stop=True).then_inc(pe_["s1"], 1)
                        if a.has(2):
                            pe.wait_ge(ve_["agg"], a.count(2))
                        mm(ps[6][:, :], w["sel_sh0"][:, :], attrT[:, :], start=True, stop=True).then_inc(pe_["s2"], 1)
                    if b is not None:
                        if a is not None:
                            pe.wait_ge(ac_["s2"], a.count())
                        pe.wait_ge(ve_["msg"], b.count())
                        for k in range(3):
                            last = mm(ps[6][:, :], w[f"o{k + 1}"][:, :], msg[:, k, :], start=k == 0, stop=k == 2)
                        last.then_inc(pe_["o"], 1)
                    if a is not None:
                        pe.wait_ge(ve_["part"], a.count())
                        mm(ps[5][:, :], w["h1"][:, :], hT[:, :], start=True, stop=True)
                        mm(ps[3][:, :], w["h2"][:, :], hT[:, :], start=True, stop=True)
                        mm(ps[4][:, :], w["h3"][:, :], hT[:, :], start=True, stop=True).then_inc(pe_["w"], 1)
                    if b is not None:
                        pe.wait_ge(ve_["agg"], b.count())
                        if b.has(1):
                            pe.wait_ge(ve_["y"], b.count(1))
                        for t in range(TPC):
                            ts = slice(t * TILE, (t + 1) * TILE)
                            mm(ps[7][:, ts], agg[:, b.slot % 2, ts], w["ident"][:, :], start=True, stop=False)
                            last = mm(ps[7][:, ts], xdT[:, b.slot % 2, ts], w["Wsi"][:, :], start=False, stop=True)
                        last.then_inc(pe_["z"], 1)
                run_chunks(pe, n, R, [0, 1], step)

            @block.scalar
            def _(act):
                nc.scalar.preload_act_table_set(ACT_SET)
                ac = nc.scalar.activation

                def step(cs):
                    a, b = cs
                    if a is not None:
                        act.wait_ge(pe_["tr"], a.count())
                        if a.has(1):
                            act.wait_ge(pe_["g"], a.count(1))
                        if a.has(1):
                            act.wait_ge(pe_["s2"], a.count(1))
                        ac(xsT[:, :], ps[0][:, :], ACT.Copy)
                        ac(attrT[:, :], ps[1][0:N_ATTR, :], ACT.Copy).then_inc(ac_["tr"], 1)
                        act.wait_ge(pe_["h"], a.count())
                        if a.has(1):
                            act.wait_ge(pe_["w"], a.count(1))
                        ac(hT[:, :], ps[1][0:100, :], ACT.Relu).then_inc(ac_["h"], 1)
                        act.wait_ge(pe_["trd"], a.count())
                        if a.has(2):
                            act.wait_ge(pe_["z"], a.count(2))
                        ac(xdT[:, a.slot % 2, :], ps[0][:, :], ACT.Copy).then_inc(ac_["trd"], 1)
                        act.wait_ge(pe_["s1"], a.count())
                        if a.has(1):
                            act.wait_ge(ve_["part"], a.count(1))
                        ac(sh[:, 0, :], ps[1][:, :], ACT.Copy).then_inc(ac_["s1"], 1)
                        act.wait_ge(pe_["s2"], a.count())
                        ac(sh[:, 1, :], ps[6][:, :], ACT.Copy).then_inc(ac_["s2"], 1)
                        act.wait_ge(pe_["m"], a.count())
                        if a.has(2):
                            act.wait_ge(ve_["agg"], a.count(2))
                        ac(mask[:, a.slot % 2, :], ps[2][:, :], ACT.Copy).then_inc(ac_["m"], 1)
                    if b is not None:
                        act.wait_ge(ve_["stats"], b.count())
                        ln_rstd(nc, act, mv[:, :, 1], rstd[:, :], w["eps"]).then_inc(ac_["rstd"], 1)
                run_chunks(act, n, R, [0, 1], step)

            @block.vector
            def _(dve):
                v = nc.vector

                def step(cs):
                    m, a, b = cs
                    dve.drain()
                    if m is not None:
                        S.index(dve, m)
                    if a is not None:
                        dve.wait_ge(pe_["g"], a.count())
                        dve.wait_ge(ac_["s2"], a.count())
                        v.tensor_tensor(part[:, 0, :], ps[3][:, :], sh[:, 0, :], ALU.mult)
                        v.tensor_tensor(part[:, 1, :], ps[4][:, :], sh[:, 1, :], ALU.mult)
                        v.tensor_tensor(part[:, 2, :], ps[4][:, :], sh[:, 0, :], ALU.mult).then_inc(ve_["part"], 1)
                    if b is not None:
                        dve.wait_ge(pe_["o"], b.count())
                        dve.wait_ge(ac_["m"], b.count())
                        if b.has(2):
                            dve.wait_ge(pe_["z"], b.count(2))
                        k = b.slot % 2
                        carry = None if isinstance(b.i, int) and b.i == 0 else edge_col(S, agg[:, 1 - k, :])
                        scan(nc, S, agg[:, k, :], mask[:, k, :], ps[6][:, :], carry, ALU.mult, ALU.add)\
                            .then_inc(ve_["agg"], 1)
                    dve.drain()
                    if a is not None:
                        dve.wait_ge(pe_["w"], a.count())
                        if a.has(1):
                            dve.wait_ge(pe_["o"], a.count(1))
                        for k, bank in enumerate((5, 3, 4)):
                            last = v.tensor_tensor(msg[:, k, :], ps[bank][:, :], part[:, k, :], ALU.mult)
                        last.then_inc(ve_["msg"], 1)
                    if b is not None:
                        dve.wait_ge(pe_["z"], b.count())
                        v.tensor_tensor(y[:, :, :], tiles(ps[7][:, :]), xd[:, b.slot], ALU.add).then_inc(ve_["y"], 1)
                        finish_rows(nc, dve, b, y, stats, mv, rstd, out, ve_, ac_["rstd"])
                run_chunks(dve, n, R, lags, step)
        end_phase(nc, P)


def finish_rows(nc, dve, b, y, stats, mv, rstd, out, ve_, rstd_done):
    dve.drain()
    ln_stats(nc, y, stats, mv)
    dve.drain()
    ln_aggregate(nc, stats, mv, TPC).then_inc(ve_["stats"], 1)
    dve.drain()
    dve.wait_ge(rstd_done, b.count())
    ln_apply(nc, out[:, b.slot], y, mv, rstd).then_inc(ve_["out"], 1)


def build_layer1(nc, g, w, T, A):
    n = g.ED // CH
    with ExitStack() as ctx:
        P = Phase(nc, ctx, "l1")
        S = Slots(P, nc, g, w, T.rec_d, REC, n, False)
        R = S.RING
        xs = P.sb("xs", [128, R, TPC, D])
        xd = P.sb("xd", [128, R, TPC, D])
        out = P.sb("out", [128, R, TPC, D])
        xsT = P.sb("xsT", [128, CH])
        xdT = P.sb("xdT", [128, 2, CH])
        mask = P.sb("mask", [128, CH])
        ones = P.sb("ones", [128, CH])
        sums, degree = P.sb("sums", [128, 2, CH]), P.sb("degree", [128, 2, CH])
        inv = P.sb("inv", [128, CH])
        mean = P.sb("mean", [128, 2, CH])
        y = P.sb("y", [128, TPC, D])
        stats, mv, rstd = P.sb("stats", [128, 4, 6]), P.sb("mv", [128, 4, 2]), P.sb("rstd", [128, 4])
        ps = [P.ps(f"ps{k}") for k in range(4)]
        pe_ = {k: P.sem("pe_" + k) for k in ("tr", "trd", "m", "z")}
        ac_ = {k: P.sem("ac_" + k) for k in ("tr", "trd", "m", "inv", "rstd")}
        ve_ = {k: P.sem("ve_" + k) for k in ("sum", "mean", "y", "stats", "out", "ones")}
        gathered, scattered, loaded = P.sems("gathered", R), P.sems("scattered", R), P.sems("loaded", R)
        with nc.Block() as block:
            @block.sync
            def _(sp):
                def step(cs):
                    c = cs[0]
                    start = S.start(sp, c)
                    if c.slot_used():
                        sp.wait_ge(scattered[c.slot], c.landed(64, 1))
                    hold(sp, w)
                    S.load(sp, c, start)
                    sp.dma_start(xd[:, c.slot], S.rows(T.x1_slot, start).rearrange("(t p) c -> p t c", p=128))\
                      .then_inc(loaded[c.slot], 16)
                run_chunks(sp, n, R, [0], step)

            @block.gpsimd
            def _(pool):
                bound = pool.to_reg(g.N - 1)

                def step(cs):
                    c = cs[0]
                    if c is not None:
                        pool.wait_ge(S.ready, c.count())
                        hold(pool, w)
                        S.gather(pool, c, 0, xs, T.x1, bound, gathered)
                    c = cs[1]
                    if c is not None:
                        pool.wait_ge(ve_["out"], c.count())
                        hold(pool, w)
                        S.scatter(pool, c, out, T.x2, bound, scattered)
                run_chunks(pool, n, R, [0, 2], step)
                for s in range(R):
                    pool.wait_ge(scattered[s], 64 * turns(n, s, R))

            @block.tensor
            def _(pe):
                mm = nc.tensor.matmul

                def step(cs):
                    a, b = cs
                    if a is not None:
                        pe.wait_ge(gathered[a.slot], a.landed(64))
                        if a.has(1):
                            pe.wait_ge(ac_["tr"], a.count(1))
                        transpose4(nc, ps[0], xs[:, a.slot], w["ident"]).then_inc(pe_["tr"], 1)
                        if a.has(1):
                            pe.wait_ge(ac_["m"], a.count(1))
                        spread(nc, ps[2], S.same[:, a.slot, 0, :], w["identb"]).then_inc(pe_["m"], 1)
                        pe.wait_ge(loaded[a.slot], a.landed(16))
                        if a.has(1):
                            pe.wait_ge(ac_["trd"], a.count(1))
                        transpose4(nc, ps[1], xd[:, a.slot], w["ident"]).then_inc(pe_["trd"], 1)
                    if b is not None:
                        pe.wait_ge(ve_["mean"], b.count())
                        pe.wait_ge(ac_["trd"], b.count())
                        if b.has(1):
                            pe.wait_ge(ve_["y"], b.count(1))
                        mm(ps[3][:, :], w["ones_row"][:, :], w["bias1"][:, :, :].rearrange("a t c -> a (t c)"),
                           start=True, stop=False)
                        for t in range(TPC):
                            ts = slice(t * TILE, (t + 1) * TILE)
                            mm(ps[3][:, ts], xdT[:, b.slot % 2, ts], w["W1a"][:, :], start=False, stop=False)
                            last = mm(ps[3][:, ts], mean[:, b.slot % 2, ts], w["W1b"][:, :], start=False,
                                      stop=t == TPC - 1)
                        last.then_inc(pe_["z"], 1)
                run_chunks(pe, n, R, [0, 1], step)

            @block.scalar
            def _(act):
                nc.scalar.preload_act_table_set(ACT_SET)
                ac = nc.scalar.activation

                def step(cs):
                    a, b = cs
                    if a is not None:
                        act.wait_ge(pe_["tr"], a.count())
                        if a.has(1):
                            act.wait_ge(ve_["sum"], a.count(1))
                        ac(xsT[:, :], ps[0][:, :], ACT.Copy).then_inc(ac_["tr"], 1)
                        act.wait_ge(pe_["m"], a.count())
                        ac(mask[:, :], ps[2][:, :], ACT.Copy).then_inc(ac_["m"], 1)
                        act.wait_ge(ve_["sum"], a.count())
                        ac(inv[:, :], degree[:, a.slot % 2, :], ACT.Ln)
                        act.drain()
                        ac(inv[:, :], inv[:, :], ACT.Exp, scale=-1.0).then_inc(ac_["inv"], 1)
                        act.wait_ge(pe_["trd"], a.count())
                        if a.has(2):
                            act.wait_ge(pe_["z"], a.count(2))
                        ac(xdT[:, a.slot % 2, :], ps[1][:, :], ACT.Copy).then_inc(ac_["trd"], 1)
                    if b is not None:
                        act.wait_ge(ve_["stats"], b.count())
                        ln_rstd(nc, act, mv[:, :, 1], rstd[:, :], w["eps"]).then_inc(ac_["rstd"], 1)
                run_chunks(act, n, R, [0, 1], step)

            @block.vector
            def _(dve):
                v = nc.vector
                v.memset(ones[:, :], 1.0)

                def step(cs):
                    m, a, b = cs
                    dve.drain()
                    if m is not None:
                        S.index(dve, m)
                    if a is not None:
                        k = a.slot % 2
                        first = isinstance(a.i, int) and a.i == 0
                        dve.wait_ge(ac_["tr"], a.count())
                        dve.wait_ge(ac_["m"], a.count())
                        scan(nc, S, degree[:, k, :], mask[:, :], ones[:, :],
                             None if first else edge_col(S, degree[:, 1 - k, :]), ALU.mult, ALU.add)
                        scan(nc, S, sums[:, k, :], mask[:, :], xsT[:, :],
                             None if first else edge_col(S, sums[:, 1 - k, :]), ALU.mult, ALU.add)\
                            .then_inc(ve_["sum"], 1)
                        dve.drain()
                        dve.wait_ge(ac_["inv"], a.count())
                        if a.has(2):
                            dve.wait_ge(pe_["z"], a.count(2))
                        v.tensor_tensor(mean[:, k, :], sums[:, k, :], inv[:, :], ALU.mult).then_inc(ve_["mean"], 1)
                    if b is not None:
                        dve.wait_ge(pe_["z"], b.count())
                        v.scalar_tensor_tensor(y[:, :, :], tiles(ps[3][:, :]), 0.0, xd[:, b.slot], ALU.max, ALU.add)\
                            .then_inc(ve_["y"], 1)
                        finish_rows(nc, dve, b, y, stats, mv, rstd, out, ve_, ac_["rstd"])
                run_chunks(dve, n, R, [0, 2, 3], step)
        end_phase(nc, P)


def build_layer2_scores(nc, g, w, T, A):
    n = g.EC // CH
    with ExitStack() as ctx:
        P = Phase(nc, ctx, "l2a")
        S = Slots(P, nc, g, w, T.rec_c, 2, n, False)
        R = S.RING
        xo = P.sb("xo", [128, R, TPC, D])
        xt = P.sb("xt", [128, R, TPC, D])
        xoT = P.sb("xoT", [128, 2, CH])
        xtT = P.sb("xtT", [128, 2, CH])
        fresh = P.sb("fresh", [128, 2, CH])
        raw = P.sb("raw", [128, 2, 2, CH])
        proj = P.sb("proj", [128, R, CH])
        kept = P.sb("kept", [128, R, 3, CH])
        high = P.sb("high", [128, CH])
        ps = [P.ps(f"ps{k}") for k in range(6)]
        pe_ = {k: P.sem("pe_" + k) for k in ("tr", "m", "s", "p")}
        ac_ = {k: P.sem("ac_" + k) for k in ("tr", "m", "s", "p")}
        ve_ = {k: P.sem("ve_" + k) for k in ("s", "max")}
        gathered, saved = P.sems("gathered", R), P.sems("saved", R)
        with nc.Block() as block:
            @block.sync
            def _(sp):
                def step(cs):
                    c = cs[0]
                    if c is not None:
                        start = S.start(sp, c)
                        if c.slot_used():
                            sp.wait_ge(saved[c.slot], c.landed(48, 1))
                        hold(sp, w)
                        S.load(sp, c, start)
                    c = cs[1]
                    if c is not None:
                        p = S.pos(c)
                        p0 = p * 128 if isinstance(p, int) else sp.snap(p * 128)
                        p1 = p * 4 if isinstance(p, int) else sp.snap(p * 4)
                        sp.wait_ge(ac_["p"], c.count())
                        hold(sp, w)
                        sp.dma_start(at_rows(T.proj2, p0, 128), proj[:, c.slot, :]).then_inc(saved[c.slot], 16)
                        sp.dma_start(at_rows(T.row2, p0, 128), xt[:, c.slot].rearrange("p t c -> p (t c)"))\
                          .then_inc(saved[c.slot], 16)
                        sp.wait_ge(ve_["max"], c.count())
                        hold(sp, w)
                        sp.dma_start(at_rows(T.score2, p1, 4), kept[0:128:32, c.slot].rearrange("p k c -> p (k c)"))\
                          .then_inc(saved[c.slot], 16)
                run_chunks(sp, n, R, [0, 3], step)
                for s in range(R):
                    sp.wait_ge(saved[s], 48 * turns(n, s, R))

            @block.gpsimd
            def _(pool):
                bound = pool.to_reg(g.N - 1)

                def step(cs):
                    c = cs[0]
                    pool.wait_ge(S.ready, c.count())
                    hold(pool, w)
                    S.gather(pool, c, 0, xo, T.x2, bound, gathered)
                    S.gather(pool, c, 1, xt, T.x2, bound, gathered)
                run_chunks(pool, n, R, [0], step)

            @block.tensor
            def _(pe):
                mm = nc.tensor.matmul

                def step(cs):
                    a, b = cs
                    if a is not None:
                        pe.wait_ge(gathered[a.slot], a.landed(128))
                        if a.has(1):
                            pe.wait_ge(ac_["tr"], a.count(1))
                        transpose4(nc, ps[0], xo[:, a.slot], w["ident"])
                        transpose4(nc, ps[1], xt[:, a.slot], w["ident"]).then_inc(pe_["tr"], 1)
                        if a.has(1):
                            pe.wait_ge(ac_["m"], a.count(1))
                        spread(nc, ps[2], S.same[:, a.slot, 1, :], w["identb"]).then_inc(pe_["m"], 1)
                    if b is not None:
                        k = b.slot % 2
                        pe.wait_ge(ac_["tr"], b.count())
                        if b.has(1):
                            pe.wait_ge(ac_["s"], b.count(1))
                        mm(ps[3][:, :], w["Asrc"][:, :], xoT[:, k, :], start=True, stop=False)
                        mm(ps[3][:, :], w["Adst"][:, :], xtT[:, k, :], start=False, stop=True)
                        mm(ps[4][:, :], w["Aself"][:, :], xtT[:, k, :], start=True, stop=True).then_inc(pe_["s"], 1)
                        if b.has(1):
                            pe.wait_ge(ac_["p"], b.count(1))
                        mm(ps[5][:, :], w["W2"][:, :], xoT[:, k, :], start=True, stop=True).then_inc(pe_["p"], 1)
                run_chunks(pe, n, R, [0, 1], step)

            @block.scalar
            def _(act):
                nc.scalar.preload_act_table_set(ACT_SET)
                ac = nc.scalar.activation

                def step(cs):
                    a, b = cs
                    if a is not None:
                        k = a.slot % 2
                        act.wait_ge(pe_["tr"], a.count())
                        if a.has(2):
                            act.wait_ge(pe_["p"], a.count(2))
                        ac(xoT[:, k, :], ps[0][:, :], ACT.Copy)
                        ac(xtT[:, k, :], ps[1][:, :], ACT.Copy).then_inc(ac_["tr"], 1)
                        act.wait_ge(pe_["m"], a.count())
                        if a.has(2):
                            act.wait_ge(ve_["max"], a.count(2))
                        ac(fresh[:, k, :], ps[2][:, :], ACT.Copy).then_inc(ac_["m"], 1)
                    if b is not None:
                        k = b.slot % 2
                        act.wait_ge(pe_["s"], b.count())
                        if b.has(2):
                            act.wait_ge(ve_["s"], b.count(2))
                        ac(raw[:, k, 0, :], ps[3][:, :], ACT.Copy)
                        ac(raw[:, k, 1, :], ps[4][:, :], ACT.Copy).then_inc(ac_["s"], 1)
                        act.wait_ge(pe_["p"], b.count())
                        if b.slot_used():
                            act.wait_ge(saved[b.slot], b.landed(48, 1))
                        ac(proj[:, b.slot, :], ps[5][:, :], ACT.Copy).then_inc(ac_["p"], 1)
                run_chunks(act, n, R, [0, 1], step)

            @block.vector
            def _(dve):
                v = nc.vector

                def step(cs):
                    m, b = cs
                    dve.drain()
                    if m is not None:
                        S.index(dve, m)
                    if b is not None:
                        k = b.slot % 2
                        dve.wait_ge(ac_["s"], b.count())
                        dve.wait_ge(ac_["m"], b.count())
                        if b.slot_used():
                            dve.wait_ge(saved[b.slot], b.landed(48, 1))
                        v.scalar_tensor_tensor(kept[:, b.slot, 0:2, :], raw[:, k, :, :], 0.2, raw[:, k, :, :],
                                               ALU.mult, ALU.max).then_inc(ve_["s"], 1)
                        dve.drain()
                        v.tensor_tensor(high[:, :], kept[:, b.slot, 0, :], kept[:, b.slot, 1, :], ALU.max)
                        dve.drain()
                        first = isinstance(b.i, int) and b.i == 0
                        scan(nc, S, kept[:, b.slot, 2, :], fresh[:, k, :], high[:, :],
                             None if first else edge_col(S, kept[:, (b.slot - 1) % R, 2, :]), ALU.add, ALU.max)\
                            .then_inc(ve_["max"], 1)
                run_chunks(dve, n, R, [0, 3], step)
        end_phase(nc, P)


def at_rows(t, start, size):
    return t[start:start + size, :] if isinstance(start, int) else t[bass.ds(start, size), :]


def build_layer2_sums(nc, g, w, T, A):
    n = g.EC // CH
    x34 = T.x34.rearrange("n k d -> n (k d)")
    with ExitStack() as ctx:
        P = Phase(nc, ctx, "l2b")
        S = Slots(P, nc, g, w, T.rec_c, 2, n, True)
        R = S.RING
        proj = P.sb("proj", [128, R, CH])
        xt = P.sb("xt", [128, R, TPC, D])
        score = P.sb("score", [128, R, 3, CH])
        xtT = P.sb("xtT", [128, 2, CH])
        goes_on, fresh = P.sb("goes_on", [128, 2, CH]), P.sb("fresh", [128, 2, CH])
        top = P.sb("top", [128, 2, CH])
        exps = P.sb("exps", [128, 2, 2, CH])
        den, num = P.sb("den", [128, 2, CH]), P.sb("num", [128, 2, CH])
        weighted = P.sb("weighted", [128, CH])
        heads = P.sb("heads", [128, 2, TPC * 4])
        inv = P.sb("inv", [128, TPC * 4])
        z = P.sb("z", [128, TPC, D])
        low = P.sb("low", [128, TPC, D])
        y = P.sb("y", [128, TPC, D])
        out = P.sb("out", [128, R, TPC, 2 * D])
        stats, mv, rstd = P.sb("stats", [128, 4, 6]), P.sb("mv", [128, 4, 2]), P.sb("rstd", [128, 4])
        ps = [P.ps(f"ps{k}") for k in range(6)]
        pe_ = {k: P.sem("pe_" + k) for k in ("tr", "m", "rows")}
        ac_ = {k: P.sem("ac_" + k) for k in ("tr", "m", "exp", "heads", "elu", "rstd")}
        ve_ = {k: P.sem("ve_" + k) for k in ("diff", "num", "z", "low", "y", "stats", "out")}
        loaded, scattered = P.sems("loaded", R), P.sems("scattered", R)
        with nc.Block() as block:
            @block.sync
            def _(sp):
                def step(cs):
                    c = cs[0]
                    start = S.start(sp, c)
                    p = S.pos(c)
                    p0 = p * 128 if isinstance(p, int) else sp.snap(p * 128)
                    p1 = p * 4 if isinstance(p, int) else sp.snap(p * 4)
                    if c.slot_used():
                        sp.wait_ge(scattered[c.slot], c.landed(64, 1))
                    hold(sp, w)
                    S.load(sp, c, start)
                    sp.dma_start(proj[:, c.slot, :], at_rows(T.proj2, p0, 128)).then_inc(loaded[c.slot], 16)
                    sp.dma_start(xt[:, c.slot].rearrange("p t c -> p (t c)"), at_rows(T.row2, p0, 128))\
                      .then_inc(loaded[c.slot], 16)
                    for h in range(4):
                        src = T.score2[p1 + h] if isinstance(p1, int) else T.score2[bass.ds(p1 + h, 1), :].squeeze(0)
                        sp.dma_start(score[32 * h:32 * h + 32, c.slot].rearrange("p k c -> p (k c)"),
                                     src.partition_broadcast(32)).then_inc(loaded[c.slot], 16)
                run_chunks(sp, n, R, [0], step)

            @block.gpsimd
            def _(pool):
                bound = pool.to_reg(g.N - 1)

                def step(cs):
                    c = cs[0]
                    pool.wait_ge(ve_["out"], c.count())
                    hold(pool, w)
                    S.scatter(pool, c, out, x34, bound, scattered)
                run_chunks(pool, n, R, [0], step)
                for s in range(R):
                    pool.wait_ge(scattered[s], 64 * turns(n, s, R))

            @block.tensor
            def _(pe):
                mm = nc.tensor.matmul

                def step(cs):
                    a, b = cs
                    if a is not None:
                        pe.wait_ge(S.ready, a.count())
                        if a.has(1):
                            pe.wait_ge(ac_["m"], a.count(1))
                        spread(nc, ps[1], S.same[:, a.slot, 0, :], w["identb"])
                        spread(nc, ps[2], S.same[:, a.slot, 1, :], w["identb"]).then_inc(pe_["m"], 1)
                        pe.wait_ge(loaded[a.slot], a.landed(96))
                        if a.has(1):
                            pe.wait_ge(ac_["tr"], a.count(1))
                        transpose4(nc, ps[0], xt[:, a.slot], w["ident"]).then_inc(pe_["tr"], 1)
                    if b is not None:
                        k = b.slot % 2
                        pe.wait_ge(ve_["num"], b.count())
                        pe.wait_ge(ac_["tr"], b.count())
                        if b.has(1):
                            pe.wait_ge(ve_["z"], b.count(1))
                        for t in range(TPC):
                            ts = slice(t * TILE, (t + 1) * TILE)
                            nc.tensor.transpose(ps[3][:, ts], num[:, k, ts], w["ident"][:, :])
                            mm(ps[4][:, ts], xtT[:, k, ts], w["W2"][:, :], start=True, stop=True)
                            mm(ps[5][:, 4 * t:4 * t + 4], den[:, k, ts], w["pick32"][:, :], start=True, stop=True)
                            last = mm(ps[5][:, 16 + 4 * t:20 + 4 * t], exps[:, k, 1, ts], w["pick32"][:, :],
                                      start=True, stop=True)
                        last.then_inc(pe_["rows"], 1)
                run_chunks(pe, n, R, [0, 1], step)

            @block.scalar
            def _(act):
                nc.scalar.preload_act_table_set(ACT_SET)
                ac = nc.scalar.activation

                def step(cs):
                    a, b = cs
                    if a is not None:
                        k = a.slot % 2
                        act.wait_ge(pe_["m"], a.count())
                        if a.has(2):
                            act.wait_ge(ve_["num"], a.count(2))
                        ac(goes_on[:, k, :], ps[1][:, :], ACT.Copy)
                        ac(fresh[:, k, :], ps[2][:, :], ACT.Copy).then_inc(ac_["m"], 1)
                        act.wait_ge(pe_["tr"], a.count())
                        if a.has(2):
                            act.wait_ge(pe_["rows"], a.count(2))
                        ac(xtT[:, k, :], ps[0][:, :], ACT.Copy).then_inc(ac_["tr"], 1)
                        act.wait_ge(ve_["diff"], a.count())
                        ac(exps[:, k], exps[:, k], ACT.Exp).then_inc(ac_["exp"], 1)
                    if b is not None:
                        act.wait_ge(pe_["rows"], b.count())
                        if b.has(1):
                            act.wait_ge(ve_["z"], b.count(1))
                        ac(heads[:, :, :].rearrange("p k c -> p (k c)"), ps[5][:, 0:32], ACT.Copy)\
                            .then_inc(ac_["heads"], 1)
                        act.wait_ge(ve_["low"], b.count())
                        ac(low[:, :, :], low[:, :, :], ACT.Exp).then_inc(ac_["elu"], 1)
                        for i in range(2):
                            act.wait_ge(ve_["stats"], b.i * 2 + (i + 1))
                            ln_rstd(nc, act, mv[:, :, 1], rstd[:, :], w["eps"]).then_inc(ac_["rstd"], 1)
                run_chunks(act, n, R, [0, 1], step)

            @block.vector
            def _(dve):
                v = nc.vector

                def by_head(t):
                    return t.rearrange("p t (h d) -> p (t h) d", h=4)

                def widen(cols):
                    return cols.unsqueeze(2).to_broadcast([128, TPC * 4, 32])

                def step(cs):
                    m, a, b = cs
                    dve.drain()
                    if a is not None:
                        k = a.slot % 2
                        first = isinstance(a.i, int) and a.i == 0

                        def carry(t):
                            return None if first else edge_col(S, t[:, 1 - k, :])
                        dve.wait_ge(loaded[a.slot], a.landed(96))
                        dve.wait_ge(ac_["m"], a.count())
                        if a.has(2):
                            dve.wait_ge(pe_["rows"], a.count(2))
                        sc = score[:, a.slot]
                        scan(nc, S, top[:, k, :], fresh[:, k, :], sc[:, 2, :], carry(top), ALU.add, ALU.max)
                        dve.drain()
                        for i in range(2):
                            last = v.tensor_tensor(exps[:, k, i, :], sc[:, i, :], top[:, k, :], ALU.subtract)
                        last.then_inc(ve_["diff"], 1)
                    if b is not None:
                        dve.wait_ge(ac_["heads"], b.count())
                        v.tensor_tensor(inv[:, :], heads[:, 0, :], heads[:, 1, :], ALU.add)
                        v.tensor_tensor(by_head(z[:, :, :]), by_head(tiles(ps[4][:, :])), widen(heads[:, 1, :]), ALU.mult)
                        dve.drain()
                        v.tensor_scalar(inv[:, :], inv[:, :], 1e-12, None, ALU.max)
                        v.tensor_tensor(z[:, :, :], z[:, :, :], tiles(ps[3][:, :]), ALU.add)
                        dve.drain()
                        v.reciprocal(inv[:, :], inv[:, :])
                        dve.drain()
                        v.tensor_tensor(by_head(z[:, :, :]), by_head(z[:, :, :]), widen(inv[:, :]), ALU.mult)
                        dve.drain()
                        v.tensor_tensor(z[:, :, :], z[:, :, :], w["bias2r"][:, :].unsqueeze(1).to_broadcast([128, TPC, D]),
                                        ALU.add).then_inc(ve_["z"], 1)
                        dve.drain()
                        v.tensor_scalar(low[:, :, :], z[:, :, :], 0.0, None, ALU.min).then_inc(ve_["low"], 1)
                    if a is not None:
                        dve.wait_ge(ac_["exp"], a.count())
                        scan(nc, S, den[:, k, :], goes_on[:, k, :], exps[:, k, 0, :], carry(den), ALU.mult, ALU.add)
                        v.tensor_tensor(weighted[:, :], exps[:, k, 0, :], proj[:, a.slot, :], ALU.mult)
                    if b is not None:
                        v.scalar_tensor_tensor(y[:, :, :], z[:, :, :], 0.0, xt[:, b.slot], ALU.max, ALU.add)
                        dve.drain()
                        dve.wait_ge(ac_["elu"], b.count())
                        v.scalar_tensor_tensor(y[:, :, :], low[:, :, :], -1.0, y[:, :, :], ALU.add, ALU.add)
                        dve.drain()
                        ln_stats(nc, y, stats, mv)
                        dve.drain()
                        ln_aggregate(nc, stats, mv, TPC).then_inc(ve_["stats"], 1)
                    dve.drain()
                    if a is not None:
                        scan(nc, S, num[:, k, :], goes_on[:, k, :], weighted[:, :], carry(num), ALU.mult, ALU.add)\
                            .then_inc(ve_["num"], 1)
                    if b is not None:
                        x3, x4 = out[:, b.slot, :, 0:D], out[:, b.slot, :, D:2 * D]
                        dve.wait_ge(ac_["rstd"], b.i * 2 + 1)
                        ln_apply(nc, x3, y, mv, rstd)
                        dve.drain()
                        ln_stats(nc, x3, stats, mv)
                        dve.drain()
                        ln_aggregate(nc, stats, mv, TPC).then_inc(ve_["stats"], 1)
                    if m is not None:
                        S.index(dve, m)
                    if b is not None:
                        dve.drain()
                        dve.wait_ge(ac_["rstd"], b.i * 2 + 2)
                        ln_apply(nc, x4, x3, mv, rstd).then_inc(ve_["out"], 1)
                run_chunks(dve, n, R, [0, 2, 3], step)
        end_phase(nc, P)


def build_layer3_scores(nc, g, w, T, A):
    n = g.ED // CH
    x_rows = T.x34.rearrange("n k d -> (n k) d")
    with ExitStack() as ctx:
        P = Phase(nc, ctx, "l3a")
        S = Slots(P, nc, g, w, T.rec_d, REC, n, False)
        R = S.RING
        xs = P.sb("xs", [128, R, TPC, D])
        xd = P.sb("xd", [128, R, TPC, D])
        xsT = P.sb("xsT", [128, 2, CH])
        xdT = P.sb("xdT", [128, 2, CH])
        attr = P.sb("attr", [128, R, TPC, 3])
        attrT = P.sb("attrT", [3, CH])
        fresh = P.sb("fresh", [128, 2, CH])
        oh_type = P.sb("oh_type", [64, CH])
        tm = P.sb("tm", [128, CH])
        rel = P.sb("rel", [128, 2, CH])
        hT = P.sb("hT", [128, CH])
        dw = P.sb("dw", [128, CH])
        msg = P.sb("msg", [128, CH])
        qT = P.sb("qT", [128, CH])
        qk = P.sb("qk", [128, CH])
        value = P.sb("value", [128, R, CH])
        kept = P.sb("kept", [128, R, 2, CH])
        ps = [P.ps(f"ps{k}") for k in range(8)]
        pe_ = {k: P.sem("pe_" + k) for k in ("tr", "m", "sel", "rel", "h", "dw", "kvq", "s")}
        ac_ = {k: P.sem("ac_" + k) for k in ("tr", "m", "dt", "h", "dw", "q", "v", "s")}
        ve_ = {k: P.sem("ve_" + k) for k in ("attr", "type", "tm", "rel", "msg", "qk", "max")}
        gathered, saved = P.sems("gathered", R), P.sems("saved", R)
        with nc.Block() as block:
            @block.sync
            def _(sp):
                def step(cs):
                    c = cs[0]
                    if c is not None:
                        start = S.start(sp, c)
                        if c.slot_used():
                            sp.wait_ge(saved[c.slot], c.landed(48, 1))
                        hold(sp, w)
                        S.load(sp, c, start)
                    c = cs[1]
                    if c is not None:
                        p = S.pos(c)
                        p0 = p * 128 if isinstance(p, int) else sp.snap(p * 128)
                        p1 = p * 8 if isinstance(p, int) else sp.snap(p * 8)
                        sp.wait_ge(ac_["v"], c.count())
                        hold(sp, w)
                        sp.dma_start(at_rows(T.value3, p0, 128), value[:, c.slot, :]).then_inc(saved[c.slot], 16)
                        sp.dma_start(at_rows(T.row3, p0, 128), xd[:, c.slot].rearrange("p t c -> p (t c)"))\
                          .then_inc(saved[c.slot], 16)
                        sp.wait_ge(ve_["max"], c.count())
                        hold(sp, w)
                        sp.dma_start(at_rows(T.score3, p1, 8), kept[0:128:16, c.slot].rearrange("p k c -> p (k c)"))\
                          .then_inc(saved[c.slot], 16)
                run_chunks(sp, n, R, [0, 3], step)
                for s in range(R):
                    sp.wait_ge(saved[s], 48 * turns(n, s, R))

            @block.gpsimd
            def _(pool):
                bound = pool.to_reg(2 * g.N - 1)

                def step(cs):
                    c = cs[0]
                    pool.wait_ge(S.ready, c.count())
                    hold(pool, w)
                    S.gather(pool, c, 0, xs, x_rows, bound, gathered)
                    S.gather(pool, c, 1, xd, x_rows, bound, gathered)
                run_chunks(pool, n, R, [0], step)

            @block.tensor
            def _(pe):
                mm = nc.tensor.matmul

                def step(cs):
                    a, b = cs
                    if b is not None:
                        k = b.slot % 2
                        pe.wait_ge(ac_["h"], b.count())
                        if b.has(1):
                            pe.wait_ge(ve_["qk"], b.count(1))
                        mm(ps[5][:, :], w["R2"][:, :], hT[:, :], start=True, stop=True).then_inc(pe_["dw"], 1)
                    if a is not None:
                        k = a.slot % 2
                        pe.wait_ge(gathered[a.slot], a.landed(128))
                        if a.has(1):
                            pe.wait_ge(ac_["tr"], a.count(1))
                        transpose4(nc, ps[0], xs[:, a.slot], w["ident"])
                        transpose4(nc, ps[1], xd[:, a.slot], w["ident"])
                        if a.has(1):
                            pe.wait_ge(ac_["m"], a.count(1))
                        pe.wait_ge(ve_["attr"], a.count())
                        for t in range(TPC):
                            last = nc.tensor.transpose(ps[2][0:3, t * TILE:(t + 1) * TILE], attr[:, a.slot, t, :],
                                                       w["ident"][:, :])
                        last.then_inc(pe_["tr"], 1)
                        pe.wait_ge(ac_["tr"], a.count())
                        spread(nc, ps[2], S.same[:, a.slot, 1, :], w["identb"]).then_inc(pe_["m"], 1)
                        if a.has(1):
                            pe.wait_ge(ve_["rel"], a.count(1))
                        if a.has(1):
                            pe.wait_ge(ac_["h"], a.count(1))
                        mm(ps[3][0:64, :], w["sel_type"][:, :], attrT[:, :], start=True, stop=True)
                        mm(ps[4][:, :], w["sel_dt"][:, :], attrT[:, :], start=True, stop=True).then_inc(pe_["sel"], 1)
                    if b is not None:
                        k = b.slot % 2
                        pe.wait_ge(ve_["msg"], b.count())
                        if b.has(1):
                            pe.wait_ge(ac_["v"], b.count(1))
                        if b.has(1):
                            pe.wait_ge(ac_["s"], b.count(1))
                        mm(ps[5][:, :], w["Wq"][:, :], xdT[:, k, :], start=True, stop=True)
                        mm(ps[6][:, :], w["Wk"][:, :], msg[:, :], start=True, stop=True)
                        mm(ps[7][:, :], w["Wv"][:, :], msg[:, :], start=True, stop=True).then_inc(pe_["kvq"], 1)
                    if a is not None:
                        k = a.slot % 2
                        pe.wait_ge(ve_["type"], a.count())
                        mm(ps[3][:, :], w["rel"][:, :], oh_type[:, :], start=True, stop=True).then_inc(pe_["rel"], 1)
                        pe.wait_ge(ve_["rel"], a.count())
                        pe.wait_ge(ac_["dt"], a.count())
                        mm(ps[4][:, :], w["R1a"][:, :], xsT[:, k, :], start=True, stop=False)
                        mm(ps[4][:, :], w["R1b"][:, :], rel[:, k, :], start=False, stop=False)
                        mm(ps[4][:, :], w["W1c"][:, :], tm[0:1, :], start=False, stop=True).then_inc(pe_["h"], 1)
                    if b is not None:
                        pe.wait_ge(ve_["qk"], b.count())
                        mm(ps[6][:, :], w["heads16"][:, :], qk[:, :], start=True, stop=True).then_inc(pe_["s"], 1)
                run_chunks(pe, n, R, [0, 1], step)

            @block.scalar
            def _(act):
                nc.scalar.preload_act_table(ACT.Sigmoid)
                ac = nc.scalar.activation

                def step(cs):
                    a, b = cs
                    if b is not None:
                        act.wait_ge(pe_["dw"], b.count())
                        if b.has(1):
                            act.wait_ge(ve_["msg"], b.count(1))
                        ac(dw[:, :], ps[5][:, :], ACT.Sigmoid, bias=w["b2"][:, 0:1]).then_inc(ac_["dw"], 1)
                    if a is not None:
                        k = a.slot % 2
                        act.wait_ge(pe_["tr"], a.count())
                        if a.has(2):
                            act.wait_ge(pe_["kvq"], a.count(2))
                        if a.has(1):
                            act.wait_ge(pe_["sel"], a.count(1))
                        ac(xsT[:, k, :], ps[0][:, :], ACT.Copy)
                        ac(xdT[:, k, :], ps[1][:, :], ACT.Copy)
                        ac(attrT[:, :], ps[2][0:3, :], ACT.Copy).then_inc(ac_["tr"], 1)
                        act.wait_ge(pe_["m"], a.count())
                        if a.has(2):
                            act.wait_ge(ve_["max"], a.count(2))
                        ac(fresh[:, k, :], ps[2][:, :], ACT.Copy).then_inc(ac_["m"], 1)
                        act.wait_ge(pe_["sel"], a.count())
                        if a.has(1):
                            act.wait_ge(pe_["h"], a.count(1))
                        ac(tm[:, :], ps[4][:, :], ACT.Sigmoid, scale=w["inv_tc"][:, 0:1]).then_inc(ac_["dt"], 1)
                    if b is not None:
                        act.wait_ge(pe_["kvq"], b.count())
                        ac(qT[:, :], ps[5][:, :], ACT.Identity, bias=w["bq"][:, 0:1]).then_inc(ac_["q"], 1)
                        if b.slot_used():
                            act.wait_ge(saved[b.slot], b.landed(48, 1))
                        ac(value[:, b.slot, :], ps[7][:, :], ACT.Identity, bias=w["bias3v"][:, 0:1]).then_inc(ac_["v"], 1)
                    if a is not None:
                        act.wait_ge(pe_["h"], a.count())
                        ac(hT[:, :], ps[4][:, :], ACT.Relu, bias=w["b1"][:, 0:1]).then_inc(ac_["h"], 1)
                    if b is not None:
                        act.wait_ge(pe_["s"], b.count())
                        ac(kept[:, b.slot, 0, :], ps[6][:, :], ACT.Copy, scale=0.25).then_inc(ac_["s"], 1)
                run_chunks(act, n, R, [0, 1], step)

            @block.vector
            def _(dve):
                v = nc.vector

                def step(cs):
                    m, a, b = cs
                    dve.drain()
                    if m is not None:
                        S.index(dve, m, other_scale=2)
                        v.tensor_copy(attr[:, m.slot, :, 0], S.rec[:, m.slot, :, W_TYPE])
                        v.tensor_copy(attr[:, m.slot, :, 1:3], S.rec[:, m.slot, :, W_NV:W_NV + 2].bitcast(F32))\
                         .then_inc(ve_["attr"], 1)
                    if b is not None:
                        k = b.slot % 2
                        dve.wait_ge(ac_["dw"], b.count())
                        v.tensor_tensor(msg[:, :], xsT[:, k, :], rel[:, k, :], ALU.mult)
                        dve.drain()
                        v.tensor_tensor(msg[:, :], msg[:, :], dw[:, :], ALU.mult).then_inc(ve_["msg"], 1)
                    if a is not None:
                        k = a.slot % 2
                        dve.wait_ge(pe_["sel"], a.count())
                        v.tensor_scalar(oh_type[:, :], ps[3][0:64, :], w["iota64"][:, 0:1], None, ALU.is_equal)\
                         .then_inc(ve_["type"], 1)
                        dve.wait_ge(ac_["dt"], a.count())
                        dve.wait_ge(pe_["rel"], a.count())
                        v.tensor_tensor(rel[:, k, :], ps[3][:, :], tm[:, :], ALU.mult).then_inc(ve_["rel"], 1)
                    if b is not None:
                        k = b.slot % 2
                        dve.wait_ge(pe_["kvq"], b.count())
                        dve.wait_ge(ac_["q"], b.count())
                        v.scalar_tensor_tensor(qk[:, :], ps[6][:, :], w["bk"][:, 0:1], qT[:, :], ALU.add, ALU.mult)\
                         .then_inc(ve_["qk"], 1)
                        dve.wait_ge(ac_["s"], b.count())
                        dve.wait_ge(ac_["m"], b.count())
                        if b.slot_used():
                            dve.wait_ge(saved[b.slot], b.landed(48, 1))
                        first = isinstance(b.i, int) and b.i == 0
                        scan(nc, S, kept[:, b.slot, 1, :], fresh[:, k, :], kept[:, b.slot, 0, :],
                             None if first else edge_col(S, kept[:, (b.slot - 1) % R, 1, :]), ALU.add, ALU.max)\
                            .then_inc(ve_["max"], 1)
                run_chunks(dve, n, R, [0, 2, 3], step)
        end_phase(nc, P)


def build_layer3_sums(nc, g, w, T, A):
    n = g.ED // CH
    x_rows = T.x34.rearrange("n k d -> (n k) d")
    with ExitStack() as ctx:
        P = Phase(nc, ctx, "l3b")
        S = Slots(P, nc, g, w, T.rec_d, REC, n, True)
        R = S.RING
        value = P.sb("value", [128, R, CH])
        xd = P.sb("xd", [128, R, TPC, D])
        score = P.sb("score", [128, R, 2, CH])
        goes_on = P.sb("goes_on", [128, 2, CH])
        fresh = P.sb("fresh", [128, 2, CH])
        top = P.sb("top", [128, 2, CH])
        exps = P.sb("exps", [128, 2, CH])
        den, num = P.sb("den", [128, 2, CH]), P.sb("num", [128, 2, CH])
        weighted, inv = P.sb("weighted", [128, CH]), P.sb("inv", [128, TPC * 8])
        z = P.sb("z", [128, TPC, D])
        y = P.sb("y", [128, TPC, D])
        out = P.sb("out", [128, R, TPC, D])
        stats, mv, rstd = P.sb("stats", [128, 4, 6]), P.sb("mv", [128, 4, 2]), P.sb("rstd", [128, 4])
        ps = [P.ps(f"ps{k}") for k in range(4)]
        pe_ = {k: P.sem("pe_" + k) for k in ("m", "z")}
        ac_ = {k: P.sem("ac_" + k) for k in ("m", "exp", "rstd")}
        ve_ = {k: P.sem("ve_" + k) for k in ("diff", "num", "z", "stats", "out")}
        loaded, scattered = P.sems("loaded", R), P.sems("scattered", R)
        with nc.Block() as block:
            @block.sync
            def _(sp):
                def step(cs):
                    c = cs[0]
                    start = S.start(sp, c)
                    p = S.pos(c)
                    p0 = p * 128 if isinstance(p, int) else sp.snap(p * 128)
                    p1 = p * 8 if isinstance(p, int) else sp.snap(p * 8)
                    if c.slot_used():
                        sp.wait_ge(scattered[c.slot], c.landed(64, 1))
                    hold(sp, w)
                    S.load(sp, c, start)
                    sp.dma_start(value[:, c.slot, :], at_rows(T.value3, p0, 128)).then_inc(loaded[c.slot], 16)
                    sp.dma_start(xd[:, c.slot].rearrange("p t c -> p (t c)"), at_rows(T.row3, p0, 128))\
                      .then_inc(loaded[c.slot], 16)
                    for h in range(8):
                        src = T.score3[p1 + h] if isinstance(p1, int) else T.score3[bass.ds(p1 + h, 1), :].squeeze(0)
                        sp.dma_start(score[16 * h:16 * h + 16, c.slot].rearrange("p k c -> p (k c)"),
                                     src.partition_broadcast(16)).then_inc(loaded[c.slot], 16)
                run_chunks(sp, n, R, [0], step)

            @block.gpsimd
            def _(pool):
                bound = pool.to_reg(2 * g.N - 1)

                def step(cs):
                    c = cs[0]
                    pool.wait_ge(ve_["out"], c.count())
                    hold(pool, w)
                    S.scatter(pool, c, out, x_rows, bound, scattered)
                run_chunks(pool, n, R, [0], step)
                for s in range(R):
                    pool.wait_ge(scattered[s], 64 * turns(n, s, R))

            @block.tensor
            def _(pe):
                def step(cs):
                    a, b = cs
                    if a is not None:
                        pe.wait_ge(S.ready, a.count())
                        if a.has(1):
                            pe.wait_ge(ac_["m"], a.count(1))
                        spread(nc, ps[0], S.same[:, a.slot, 0, :], w["identb"])
                        spread(nc, ps[1], S.same[:, a.slot, 1, :], w["identb"]).then_inc(pe_["m"], 1)
                    if b is not None:
                        pe.wait_ge(ve_["num"], b.count())
                        if b.has(1):
                            pe.wait_ge(ve_["z"], b.count(1))
                        for t in range(TPC):
                            ts = slice(t * TILE, (t + 1) * TILE)
                            nc.tensor.transpose(ps[2][:, ts], num[:, b.slot % 2, ts], w["ident"][:, :])
                            last = nc.tensor.matmul(ps[3][:, 8 * t:8 * t + 8], den[:, b.slot % 2, ts],
                                                    w["pick16"][:, :], start=True, stop=True)
                        last.then_inc(pe_["z"], 1)
                run_chunks(pe, n, R, [0, 1], step)

            @block.scalar
            def _(act):
                nc.scalar.preload_act_table_set(ACT_SET)
                ac = nc.scalar.activation

                def step(cs):
                    a, b = cs
                    if a is not None:
                        k = a.slot % 2
                        act.wait_ge(pe_["m"], a.count())
                        if a.has(2):
                            act.wait_ge(ve_["num"], a.count(2))
                        ac(goes_on[:, k, :], ps[0][:, :], ACT.Copy)
                        ac(fresh[:, k, :], ps[1][:, :], ACT.Copy).then_inc(ac_["m"], 1)
                        act.wait_ge(ve_["diff"], a.count())
                        ac(exps[:, k, :], exps[:, k, :], ACT.Exp).then_inc(ac_["exp"], 1)
                    if b is not None:
                        act.wait_ge(ve_["stats"], b.count())
                        ln_rstd(nc, act, mv[:, :, 1], rstd[:, :], w["eps"]).then_inc(ac_["rstd"], 1)
                run_chunks(act, n, R, [0, 1], step)

            @block.vector
            def _(dve):
                v = nc.vector

                def by_head(t):
                    return t.rearrange("p t (h d) -> p (t h) d", h=8)

                def step(cs):
                    m, a, b = cs
                    dve.drain()
                    if a is not None:
                        k = a.slot % 2
                        first = isinstance(a.i, int) and a.i == 0
                        dve.wait_ge(loaded[a.slot], a.landed(160))
                        dve.wait_ge(ac_["m"], a.count())
                        scan(nc, S, top[:, k, :], fresh[:, k, :], score[:, a.slot, 1, :],
                             None if first else edge_col(S, top[:, 1 - k, :]), ALU.add, ALU.max)
                        dve.drain()
                        v.tensor_tensor(exps[:, k, :], score[:, a.slot, 0, :], top[:, k, :], ALU.subtract)\
                         .then_inc(ve_["diff"], 1)
                    if b is not None:
                        dve.wait_ge(pe_["z"], b.count())
                        v.reciprocal(inv[:, :], ps[3][:, 0:TPC * 8])
                        dve.drain()
                        v.tensor_tensor(by_head(z[:, :, :]), by_head(tiles(ps[2][:, :])),
                                        inv[:, :].unsqueeze(2).to_broadcast([128, TPC * 8, 16]), ALU.mult)\
                         .then_inc(ve_["z"], 1)
                        dve.drain()
                        v.tensor_tensor(y[:, :, :], z[:, :, :], xd[:, b.slot], ALU.add)
                    if a is not None:
                        dve.wait_ge(ac_["exp"], a.count())
                        if a.has(2):
                            dve.wait_ge(pe_["z"], a.count(2))
                        scan(nc, S, den[:, k, :], goes_on[:, k, :], exps[:, k, :],
                             None if first else edge_col(S, den[:, 1 - k, :]), ALU.mult, ALU.add)
                        v.tensor_tensor(weighted[:, :], exps[:, k, :], value[:, a.slot, :], ALU.mult)
                    if b is not None:
                        dve.drain()
                        ln_stats(nc, y, stats, mv)
                        dve.drain()
                        ln_aggregate(nc, stats, mv, TPC).then_inc(ve_["stats"], 1)
                    dve.drain()
                    if a is not None:
                        scan(nc, S, num[:, k, :], goes_on[:, k, :], weighted[:, :],
                             None if first else edge_col(S, num[:, 1 - k, :]), ALU.mult, ALU.add)\
                            .then_inc(ve_["num"], 1)
                    if m is not None:
                        S.index(dve, m, to_scale=2, to_plus=1)
                    if b is not None:
                        dve.wait_ge(ac_["rstd"], b.count())
                        ln_apply(nc, out[:, b.slot], y, mv, rstd).then_inc(ve_["out"], 1)
                run_chunks(dve, n, R, [0, 2, 3], step)
        end_phase(nc, P)


def build_program(nc, A, stage="all"):
    g = Sizes(A["x"].shape[0], A["src"].shape[0])
    T = Tables()
    T.x = A["x"]

    def table(name, shape, dt=F32):
        return A[name] if name in A else nc.dram_tensor(name, shape, dt).ap()
    T.x1, T.x2, T.x1_slot = table("x1", [g.N, D]), table("x2", [g.N, D]), table("x1_slot", [g.ED, D])
    T.x34 = A["x34"]
    T.rec_c = table("rec_c", [g.EC + 2, 2], I32)
    T.rec_d = table("rec_d", [g.ED + 2, REC], I32)
    nd, nC = g.ED // CH, g.EC // CH
    T.proj2, T.row2 = table("proj2", [nC * 128, CH]), table("row2", [nC * 128, TPC * D])
    T.score2 = table("score2", [nC * 4, 3 * CH])
    T.value3, T.row3 = table("value3", [nd * 128, CH]), table("row3", [nd * 128, TPC * D])
    T.score3 = table("score3", [nd * 8, 2 * CH])
    with ExitStack() as ctx:
        P = Phase(nc, ctx, "w")
        w = build_constants(nc, P, g, A)
        order = ["iso", "sort", "l0", "l1", "l2a", "l2b", "l3a", "l3b"]
        last = len(order) if stage == "all" else order.index(stage) + 1
        for s in order[:last]:
            {"iso": lambda: build_isolated(nc, g, w, T), "sort": lambda: build_sort(nc, g, w, T, A),
             "l0": lambda: build_layer0(nc, g, w, T, A), "l1": lambda: build_layer1(nc, g, w, T, A),
             "l2a": lambda: build_layer2_scores(nc, g, w, T, A), "l2b": lambda: build_layer2_sums(nc, g, w, T, A),
             "l3a": lambda: build_layer3_scores(nc, g, w, T, A), "l3b": lambda: build_layer3_sums(nc, g, w, T, A)}[s]()


_INS = ["x", "src", "dst", "edge_attr_10", "edge_attr_4", "edge_type_64", "edge_weight", "node_vec",
        "L0_gnn_W_si_0e", "L0_gnn_W_si_1o", "L0_gnn_W_l1_0e", "L0_gnn_W_l1_1o", "L0_gnn_W_fc1", "L0_gnn_W_fc2",
        "L0_gnn_W_l2_0e", "L0_gnn_W_l2_1o", "L1_gnn_W", "L1_gnn_b", "L2_gnn_W", "L2_gnn_attn_src",
        "L2_gnn_attn_dst", "L2_gnn_bias", "L3_gnn_rel_table", "L3_gnn_Wq", "L3_gnn_bq", "L3_gnn_Wk", "L3_gnn_bk",
        "L3_gnn_Wv", "L3_gnn_bv", "L3_gnn_W1", "L3_gnn_b1", "L3_gnn_W2", "L3_gnn_b2", "L3_gnn_time_coeff"]


def kernel(**inputs):
    import numpy as np
    import concourse.bacc as bacc
    from concourse import mybir as _mybir
    from concourse.bass_utils import run_bass_kernel_spmd

    nc = bacc.Bacc("TRN2", target_bir_lowering=False, num_devices=1)
    arrays, A = {}, {}
    for name in _INS:
        a = np.atleast_1d(np.ascontiguousarray(inputs[name]))
        arrays[name] = a
        A[name] = nc.dram_tensor(name, a.shape, _mybir.dt.from_np(a.dtype), kind="ExternalInput").ap()
    n, d = inputs["x"].shape
    A["x34"] = nc.dram_tensor("x34", [n, 2, d], _mybir.dt.float32, kind="ExternalOutput").ap()
    build_program(nc, A)
    result = run_bass_kernel_spmd(nc, [arrays], core_ids=[0])
    return result.results[0]["x34"].reshape(n, 2, d)[:, 1, :]
```

```python
import concourse.bass as bass
from concourse import mybir
from contextlib import ExitStack

F32 = mybir.dt.float32
I32 = mybir.dt.int32
BF16 = mybir.dt.bfloat16
F16 = mybir.dt.float16
ALU = mybir.AluOpType
ACT = mybir.ActivationFunctionType
AX_X = mybir.AxisListType.X

D = 128
MUL = 32
TILE = 128
TPC = 4
CH = TILE * TPC
LN_EPS = 1e-5
FAR = 1 << 20
ACT_SET = "natural_log_exp_and_others"
NEG = -1e30

W_DST, W_SRC, W_TYPE, W_NV, W_EW, W_SH, W_LEN = 0, 1, 2, 3, 4, 5, 9
N_SH, N_LEN = 4, 10
N_ATTR = N_SH + N_LEN
REC = 20


class Chunk:

    def __init__(self, i, slot, turn, ring):
        self.i, self.slot, self.turn, self.ring = i, slot, turn, ring

    def has(self, back):
        return not isinstance(self.i, int) or self.i >= back

    def count(self, back=0):
        return self.i + (1 - back)

    def slot_used(self):
        return not isinstance(self.turn, int) or self.turn > 0

    def landed(self, amount, back=0):
        return (self.turn + (1 - back)) * amount


def run_chunks(eng, n, ring, lags, body, base=0):
    deep = max(lags)
    before = base // ring

    def at(i):
        return [Chunk(i - k + base, (i - k) % ring, (i - k) // ring + before, ring) if 0 <= i - k < n else None
                for k in lags]

    lo = -(-(deep + ring) // ring)
    hi = max(lo, (n - 1) // ring)
    for i in range(min(lo * ring, n + deep)):
        body(at(i))
    if hi > lo:
        with eng.Fori(lo, hi) as turn:
            for p in range(ring):
                body([Chunk(turn * ring + (p - k + base), (p - k) % ring, turn + ((p - k) // ring + before), ring)
                      for k in lags])
    for i in range(hi * ring, n + deep):
        body(at(i))


def hold(eng, w):
    eng.sem_inc(w["held"], 1)


class Phase:

    def __init__(self, nc, ctx, tag):
        self.nc, self.ctx, self.tag, self.taken = nc, ctx, tag, []

    def sb(self, name, shape, dt=F32):
        return self.ctx.enter_context(self.nc.sbuf_tensor(f"{self.tag}_{name}", shape, dt))

    def ps(self, name, shape=(128, 512), dt=F32):
        return self.ctx.enter_context(self.nc.psum_tensor(f"{self.tag}_{name}", list(shape), dt))

    def sem(self, name):
        s = self.nc.alloc_semaphore(f"{self.tag}_{name}")
        self.taken.append(s)
        return s

    def sems(self, name, n):
        return [self.sem(f"{name}{k}") for k in range(n)]


def end_phase(nc, P):
    nc.all_engine_barrier()
    nc.clear_and_free_semaphores(P.taken)
    nc.all_engine_barrier()


def tiles(t):
    return t.rearrange("p (t c) -> p t c", t=TPC)



def ln_stats(nc, y, stats, mv, tiles_of=range(TPC), at=0):
    for t in tiles_of:
        nc.vector.bn_stats(stats[:, at + t, :], y[:, t, :])


def ln_aggregate(nc, stats, mv, n):
    last = None
    for t in range(n):
        last = nc.vector.bn_aggr(mv[:, t, :], stats[:, t, :])
    return last


def ln_rstd(nc, act, mv, rstd, eps):
    nc.scalar.activation(rstd, mv, ACT.Ln, bias=eps[:, 0:1])
    act.drain()
    return nc.scalar.activation(rstd, rstd, ACT.Exp, scale=-0.5)


def ln_twice_rstd(nc, act, var, rstd, w):
    nc.scalar.activation(rstd[:, 0, :], var, ACT.Ln, bias=w["eps"][:, 0:1])
    nc.scalar.activation(rstd[:, 1, :], var, ACT.Ln, bias=w["eps2"][:, 0:1], scale=1.0 + LN_EPS)
    act.drain()
    return nc.scalar.activation(rstd[:, :, :], rstd[:, :, :], ACT.Exp, scale=-0.5)


def ln_apply(nc, out, y, mv, rstd):
    last = None
    for t in range(TPC):
        last = nc.vector.tensor_scalar(out[:, t, :], y[:, t, :], mv[:, t, 0:1], rstd[:, t:t + 1],
                                       ALU.subtract, ALU.mult)
    return last


def transpose4(nc, out, rows, ident):
    last = None
    for t in range(TPC):
        last = nc.tensor.transpose(out[:, t * TILE:(t + 1) * TILE], rows[:, t, :], ident[:, :])
    return last


def spread(nc, out, cols, ident):
    last = None
    for t in range(TPC):
        last = nc.tensor.matmul(out[:, t * TILE:(t + 1) * TILE], cols[:, t:t + 1].to_broadcast([128, 128]),
                                ident[:, :], start=True, stop=True)
    return last


def add_bias(nc, out, w, name):
    return nc.tensor.matmul(out[:, :], w["ones3"][:, :], w[name][:, :], start=True, stop=False)


def build_constants(nc, P, g, A):
    w = {}
    for n in ("ident", "Wsi", "WsiI", "W1a", "W1b", "W1sum", "W2", "Asrc", "Adst", "Aself", "g1", "g2",
              "o1", "o2", "o3", "R1a", "R1b", "R2", "Wq", "Wk", "Wv", "heads16", "heads32"):
        w[n] = P.sb(n, [128, 128])
    w["held"] = P.sem("held")
    w["identb"] = P.sb("identb", [128, 128], BF16)
    w["eps"], w["eps2"] = P.sb("eps", [128, 1]), P.sb("eps2", [128, 1])
    w["ones3"] = P.sb("ones3", [3, 128], BF16)
    w["bias1"], w["bias2"] = P.sb("bias1", [3, CH], BF16), P.sb("bias2", [3, CH], BF16)
    w["bias2c"] = P.sb("bias2c", [128, 1])
    w["bias3v"] = P.sb("bias3v", [128, 1])
    w["bq"] = P.sb("bq", [128, 1])
    w["bk"] = P.sb("bk", [128, 1])
    w["b1"] = P.sb("b1", [128, 1])
    w["b2"] = P.sb("b2", [128, 1])
    w["inv_tc"] = P.sb("inv_tc", [128, 1])
    w["fc1"] = P.sb("fc1", [N_ATTR, 100])
    for n in ("h1", "h2", "h3"):
        w[n] = P.sb(n, [100, 128])
    w["sel_sh"] = P.sb("sel_sh", [N_ATTR, 128])
    w["sel_sh0"] = P.sb("sel_sh0", [N_ATTR, 128])
    w["rel"] = P.sb("rel", [64, 128])
    w["W1c"] = P.sb("W1c", [1, 128])
    w["sel_type"] = P.sb("sel_type", [3, 64])
    w["sel_dt"] = P.sb("sel_dt", [3, 128])
    w["iota64"] = P.sb("iota64", [64, 1])
    w["pick16"] = P.sb("pick16", [128, 8])
    with ExitStack() as ctx:
        Q = Phase(nc, ctx, "prep")
        l1w = Q.sb("l1w", [128, 256])
        acol = Q.sb("acol", [128, 2])
        asel = Q.sb("asel", [128, 2, 128])
        w2t = Q.sb("w2t", [128, 128])
        r2c = Q.sb("r2c", [128, 1])
        bias = Q.sb("bias", [3, 2, TPC, D])
        parts = Q.sb("parts", [3, 3, 2, TPC, D], BF16)
        tcn = Q.sb("tcn", [128, 1])
        ones = Q.sb("ones", [128, 128])
        pt = Q.ps("pt")
        pa = Q.ps("pa")
        zeroed, made, loaded, transposed, turned, combined = (
            Q.sem(n) for n in ("zeroed", "made", "loaded", "transposed", "turned", "combined"))
        n_loads = [0]
        zero_first = ("Wsi", "g1", "g2", "o1", "o2", "o3", "fc1", "h1", "h2", "h3")
        with nc.Block() as block:
            @block.vector
            def _(dve):
                for n in zero_first:
                    last = nc.vector.memset(w[n][:, :], 0.0)
                nc.vector.memset(w["eps"][:, :], LN_EPS)
                nc.vector.memset(w["eps2"][:, :], LN_EPS ** 2)
                last = nc.vector.memset(w["ones3"][:, :], 1.0)
                last.then_inc(zeroed, 1)

            @block.sync
            def _(sp):
                sp.wait_ge(zeroed, 1)

                def load(dst, src):
                    sp.dma_start(dst, src, allow_slow_non_contiguous=True).then_inc(loaded, 16)
                    n_loads[0] += 1

                def col(v):
                    return v.rearrange("(p a) -> p a", a=1)

                def row(v):
                    return v.rearrange("(a n) -> a n", a=1)

                def vec(mat, m, cols_from=MUL):
                    return mat[MUL + m:128:3, cols_from + m:128:3]

                load(w["Wsi"][0:MUL, 0:MUL], A["L0_gnn_W_si_0e"])
                load(w["g1"][0:MUL, 0:MUL], A["L0_gnn_W_l1_0e"])
                load(w["o1"][0:MUL, 0:MUL], A["L0_gnn_W_l2_0e"][0:MUL, :])
                load(w["h1"][:, 0:MUL], A["L0_gnn_W_fc2"][:, 0:MUL])
                for m in range(3):
                    load(vec(w["Wsi"], m), A["L0_gnn_W_si_1o"])
                    load(w["g1"][0:MUL, MUL + m:128:3], A["L0_gnn_W_l1_0e"])
                    load(vec(w["g2"], m), A["L0_gnn_W_l1_1o"])
                    load(w["o3"][MUL + m:128:3, 0:MUL], A["L0_gnn_W_l2_0e"][MUL:2 * MUL, :])
                    load(vec(w["o1"], m), A["L0_gnn_W_l2_1o"][0:MUL, :])
                    load(vec(w["o2"], m), A["L0_gnn_W_l2_1o"][MUL:2 * MUL, :])
                    for k in range(3):
                        load(w[f"h{k + 1}"][:, MUL + m:128:3], A["L0_gnn_W_fc2"][:, (k + 1) * MUL:(k + 2) * MUL])
                load(w["fc1"][N_SH:N_ATTR, :], A["L0_gnn_W_fc1"])
                load(l1w[:, :], A["L1_gnn_W"])
                for t in range(TPC):
                    load(bias[:, 0, t, :], A["L1_gnn_b"].partition_broadcast(3))
                    load(bias[:, 1, t, :], A["L2_gnn_bias"].partition_broadcast(3))
                load(w["bias2c"][:, :], col(A["L2_gnn_bias"]))
                load(w["W2"][:, :], A["L2_gnn_W"])
                load(acol[:, 0:1], A["L2_gnn_attn_src"].rearrange("h (d a) -> (h d) a", a=1))
                load(acol[:, 1:2], A["L2_gnn_attn_dst"].rearrange("h (d a) -> (h d) a", a=1))
                load(w["rel"][:, :], A["L3_gnn_rel_table"])
                load(w["Wq"][:, :], A["L3_gnn_Wq"])
                load(w["Wk"][:, :], A["L3_gnn_Wk"])
                load(w["Wv"][:, :], A["L3_gnn_Wv"])
                load(w["bq"][:, :], col(A["L3_gnn_bq"]))
                load(w["bk"][:, :], col(A["L3_gnn_bk"]))
                load(w["bias3v"][:, :], col(A["L3_gnn_bv"]))
                load(w["b1"][:, :], col(A["L3_gnn_b1"]))
                load(w["R1a"][:, :], A["L3_gnn_W1"][0:128, :])
                load(w["R1b"][:, :], A["L3_gnn_W1"][128:256, :])
                load(w["W1c"][:, :], A["L3_gnn_W1"][256:257, :])
                load(r2c[:, :], A["L3_gnn_W2"])
                load(w["b2"][:, :], A["L3_gnn_b2"].partition_broadcast(128))
                load(tcn[:, :], A["L3_gnn_time_coeff"].partition_broadcast(128))

            @block.gpsimd
            def _(pool):
                for n in ("ident", "identb", "heads16", "heads32", "sel_sh", "sel_sh0", "sel_type", "pick16"):
                    nc.gpsimd.memset(w[n][:, :], 1.0)
                nc.gpsimd.memset(ones[:, :], 1.0)
                nc.gpsimd.memset(w["sel_dt"][:, :], 0.0)
                pool.drain()

                def keep(t, pattern, base, cm, op):
                    return nc.gpsimd.affine_select(out=t, in_=t, compare_op=op, fill=0.0, base=base,
                                                   pattern=pattern, channel_multiplier=cm)

                for n in ("ident", "identb"):
                    keep(w[n][:, :], [[-1, 128]], 0, 1, ALU.is_equal)
                for n, size in (("heads16", 16), ("heads32", 32)):
                    v = w[n][:, :].rearrange("p (h d) -> p h d", d=size)
                    keep(v, [[-size, 128 // size], [0, size]], 0, 1, ALU.is_ge)
                    pool.drain()
                    keep(v, [[size, 128 // size], [0, size]], size - 1, -1, ALU.is_ge)
                keep(w["sel_sh"][:, 0:MUL], [[0, MUL]], 0, 1, ALU.is_equal)
                keep(w["sel_sh"][:, MUL:128].rearrange("p (u m) -> p u m", m=3), [[0, MUL], [-1, 3]], -1, 1,
                     ALU.is_equal)
                keep(w["pick16"][:, :], [[-16, 8]], 0, 1, ALU.is_equal)
                keep(w["sel_sh0"][:, :], [[0, 128]], 0, 1, ALU.is_equal)
                keep(w["sel_type"][:, :], [[0, 64]], 0, 1, ALU.is_equal)
                s = w["sel_dt"]
                nc.gpsimd.affine_select(out=s[:, :], in_=s[:, :], compare_op=ALU.not_equal, fill=1.0, base=-1,
                                        pattern=[[0, 128]], channel_multiplier=1)
                pool.drain()
                nc.gpsimd.affine_select(out=s[:, :], in_=s[:, :], compare_op=ALU.not_equal, fill=-1.0, base=-2,
                                        pattern=[[0, 128]], channel_multiplier=1)
                nc.gpsimd.iota(w["iota64"][:, :], pattern=[[0, 1]], base=0, channel_multiplier=1,
                               allow_small_or_imprecise_dtypes=True)
                pool.drain()
                nc.gpsimd.memset(ones[:, 0:1], 1.0).then_inc(made, 1)

            @block.tensor
            def _(pe):
                pe.wait_ge(made, 1)
                pe.wait_ge(loaded, 16 * n_loads[0])
                nc.tensor.transpose(pt[:, 0:128], l1w[:, 0:128], w["ident"][:, :])
                nc.tensor.transpose(pt[:, 128:256], l1w[:, 128:256], w["ident"][:, :])
                nc.tensor.transpose(pt[:, 256:384], w["W2"][:, :], w["ident"][:, :]).then_inc(transposed, 1)
                pe.wait_ge(turned, 1)
                nc.tensor.matmul(pa[:, 0:128], w2t[:, :], asel[:, 0, :], start=True, stop=True)
                nc.tensor.matmul(pa[:, 128:256], w2t[:, :], asel[:, 1, :], start=True, stop=True).then_inc(combined, 1)

            @block.vector
            def _(dve):
                dve.wait_ge(made, 1)
                dve.wait_ge(loaded, 16 * n_loads[0])
                dve.wait_ge(transposed, 1)
                v = nc.vector
                v.tensor_copy(w["W1a"][:, :], pt[:, 0:128])
                v.tensor_copy(w["W1b"][:, :], pt[:, 128:256])
                v.tensor_copy(w2t[:, :], pt[:, 256:384])
                for k in range(2):
                    v.tensor_scalar(asel[:, k, :], w["heads32"][:, :], acol[:, k:k + 1], None, ALU.mult)
                for k in range(3):
                    v.tensor_copy(parts[:, k], bias[:, :])
                    dve.drain()
                    if k < 2:
                        v.tensor_tensor(bias[:, :], bias[:, :], parts[:, k], ALU.subtract)
                        dve.drain()
                for i, n in enumerate(("bias1", "bias2")):
                    for k in range(3):
                        part = parts[:, k, i].rearrange("p t c -> p (t c)")
                        if k == 0:
                            v.tensor_scalar(w[n][:, :], part, w["ident"][0:3, 0:1], None, ALU.mult)
                        else:
                            v.scalar_tensor_tensor(w[n][:, :], part, w["ident"][0:3, k:k + 1], w[n][:, :],
                                                   ALU.mult, ALU.add)
                        dve.drain()
                v.tensor_scalar(w["R2"][:, :], ones[:, :], r2c[:, 0:1], None, ALU.mult)
                for n, s in (("Wsi", MUL ** -0.5), ("g1", MUL ** -0.5), ("g2", MUL ** -0.5),
                             ("o1", 0.5 / 4 / 8), ("o2", 0.5 / 4 / 8), ("o3", 0.5 / 4 / 8),
                             ("h1", 0.1), ("h2", 0.1), ("h3", 0.1), ("fc1", N_LEN ** -0.5)):
                    v.tensor_scalar(w[n][:, :], w[n][:, :], s, None, ALU.mult)
                v.tensor_scalar(w["inv_tc"][:, :], tcn[:, :], -1.0, None, ALU.mult)
                dve.drain()
                v.tensor_tensor(w["W1sum"][:, :], w["W1a"][:, :], w["W1b"][:, :], ALU.add).then_inc(turned, 1)
                v.tensor_tensor(w["WsiI"][:, :], w["Wsi"][:, :], w["ident"][:, :], ALU.add)
                v.tensor_scalar(w["o3"][:, 0:MUL], w["o3"][:, 0:MUL], 3.0 ** -0.5, None, ALU.mult)
                v.tensor_tensor(w["inv_tc"][:, :], w["inv_tc"][:, :], tcn[:, :], ALU.max)
                dve.drain()
                v.tensor_scalar(w["inv_tc"][:, :], w["inv_tc"][:, :], 1e-9, None, ALU.add)
                dve.drain()
                v.reciprocal(w["inv_tc"][:, :], w["inv_tc"][:, :])
                dve.wait_ge(combined, 1)
                v.tensor_copy(w["Asrc"][:, :], pa[:, 0:128])
                v.tensor_copy(w["Adst"][:, :], pa[:, 128:256])
                dve.drain()
                v.tensor_tensor(w["Aself"][:, :], w["Asrc"][:, :], w["Adst"][:, :], ALU.add)
        end_phase(nc, Q)
    return w


def build_isolated(nc, g, w, T):
    N = g.N
    n = -(-N // CH)
    with ExitStack() as ctx:
        P = Phase(nc, ctx, "iso")
        R = 4
        x_in = P.sb("x_in", [128, R, TPC, D])
        normed = P.sb("normed", [128, 4, R, TPC, D])
        xT = P.sb("xT", [128, 3, 2, CH])
        y = P.sb("y", [128, 3, 2, TPC, D])
        low = P.sb("low", [128, TPC, D])
        stats = P.sb("stats", [128, 16, 6])
        mv = P.sb("mv", [128, 16, 2])
        rstd, shift = P.sb("rstd", [128, 16]), P.sb("shift", [128, 16])
        psT = [P.ps(f"psT{k}") for k in range(3)]
        psZ = [[P.ps("psZ00"), P.ps("psZ01")], [P.ps("psZ1")], [P.ps("psZ2")]]
        x_loaded = P.sems("x_loaded", R)
        stored = [P.sems(f"stored{k}_", R) for k in range(4)]
        transposed, xT_copied, z_done, y_done = (P.sems(s, 3) for s in ("transposed", "xT_copied", "z_done", "y_done"))
        elu_done, stats_done, rstd_done, shift_done = (
            P.sem(s) for s in ("elu_done", "stats_done", "rstd_done", "shift_done"))
        applied = P.sems("applied", 4)
        T_LAGS, A_LAGS = [0, 3, 6], [1, 4, 7, 8]
        B_LAGS = [k + 1 for k in A_LAGS]
        weights = [w["WsiI"], w["W1sum"], w["W2"]]
        targets = [T.x1, T.x2, T.x34[:, 0, :], T.x34[:, 1, :]]
        BY_ACT = (0, 1, 3)

        def rows(table, c):
            start = N - CH if isinstance(c.i, int) and c.i == n - 1 else c.i * CH
            part = table[start:start + CH, :] if isinstance(start, int) else table[bass.ds(start, CH), :]
            return part.rearrange("(p t) c -> p t c", t=TPC)

        def source(l, c):
            return x_in[:, c.slot] if l == 0 else normed[:, l - 1, c.slot]

        def present(cs, lags):
            ls = [l for l in range(len(lags)) if cs[l] is not None]
            if not ls:
                return None
            return ls[0], ls[-1] + 1, cs[ls[0]].i + lags[ls[0]]

        def before_norm(l, c):
            return tiles(psZ[0][c.slot % 2][:, :]) if l == 0 else source(3, c) if l == 3 else y[:, l, c.slot % 2]

        with nc.Block() as block:
            @block.sync
            def _(sp):
                def step(cs):
                    c = cs[0]
                    if c is not None:
                        if c.has(R):
                            sp.wait_ge(transposed[0], c.count(R))
                        sp.dma_start(x_in[:, c.slot], rows(T.x, c)).then_inc(x_loaded[c.slot], 16)
                    for l in range(4):
                        c = cs[l + 1]
                        if c is not None:
                            sp.wait_ge(applied[l], c.count())
                            if isinstance(c.i, int) and c.i == n - 1:
                                sp.wait_ge(stored[l][(n - 2) % R], 16 * turns(n - 1, (n - 2) % R, R))
                            sp.dma_start(rows(targets[l], c), normed[:, l, c.slot]).then_inc(stored[l][c.slot], 16)
                run_chunks(sp, n, R, [0] + [k + 1 for k in B_LAGS], step)
                for l in range(4):
                    for s in range(R):
                        sp.wait_ge(stored[l][s], 16 * turns(n, s, R))

            @block.tensor
            def _(pe):
                def step(cs):
                    for l in range(3):
                        c = cs[l + 3]
                        if c is None:
                            continue
                        pe.wait_ge(xT_copied[l], c.count())
                        if l == 0:
                            if c.has(2):
                                pe.wait_ge(applied[0], c.count(2))
                        elif c.has(1):
                            pe.wait_ge(y_done[1] if l == 1 else elu_done, c.count(1))
                        z = psZ[l][c.slot % len(psZ[l])]
                        if l > 0:
                            add_bias(nc, z, w, f"bias{l}")
                        for t in range(TPC):
                            last = nc.tensor.matmul(z[:, t * D:(t + 1) * D], xT[:, l, c.slot % 2, t * D:(t + 1) * D],
                                                    weights[l][:, :], start=l == 0, stop=l == 0 or t == TPC - 1)
                        last.then_inc(z_done[l], 1)
                    for l in range(3):
                        c = cs[l]
                        if c is None:
                            continue
                        if l == 0:
                            pe.wait_ge(x_loaded[c.slot], c.landed(16))
                        else:
                            pe.wait_ge(applied[l - 1], c.count())
                        if c.has(1):
                            pe.wait_ge(xT_copied[l], c.count(1))
                        transpose4(nc, psT[l], source(l, c), w["ident"]).then_inc(transposed[l], 1)
                run_chunks(pe, n, R, T_LAGS + A_LAGS[:3], step)

            @block.scalar
            def _(act):
                nc.scalar.preload_act_table_set(ACT_SET)
                def step(cs):
                    now = present(cs[7:], B_LAGS)
                    if now is not None:
                        lo, hi, t = now
                        act.wait_ge(shift_done, t - 1)
                        for l in range(lo, hi):
                            if l not in BY_ACT:
                                continue
                            c = cs[7 + l]
                            if c.slot_used():
                                act.wait_ge(stored[l][c.slot], c.landed(16, 1))
                            for k in range(TPC):
                                j = 4 * l + k
                                last = nc.scalar.activation(normed[:, l, c.slot, k, :], before_norm(l, c)[:, k, :],
                                                            ACT.Identity, bias=shift[:, j:j + 1], scale=rstd[:, j:j + 1])
                            last.then_inc(applied[l], 1)
                    c = cs[3 + 2]
                    if c is not None:
                        act.wait_ge(y_done[2], c.count())
                        nc.scalar.activation(low[:, :, :], tiles(psZ[2][0][:, :]), ACT.Relu, scale=-1.0)
                        act.drain()
                        nc.scalar.activation(low[:, :, :], low[:, :, :], ACT.Exp, scale=-1.0).then_inc(elu_done, 1)
                    for l in range(3):
                        c = cs[l]
                        if c is None:
                            continue
                        act.wait_ge(transposed[l], c.count())
                        if c.has(2):
                            act.wait_ge(z_done[l], c.count(2))
                        nc.scalar.activation(xT[:, l, c.slot % 2, :], psT[l][:, :], ACT.Copy).then_inc(xT_copied[l], 1)
                    now = present(cs[3:7], A_LAGS)
                    if now is not None:
                        lo, hi, t = now
                        act.drain()
                        act.wait_ge(stats_done, t)
                        ln_rstd(nc, act, mv[:, lo * 4:hi * 4, 1], rstd[:, lo * 4:hi * 4], w["eps"]).then_inc(rstd_done, 1)
                run_chunks(act, n, R, T_LAGS + A_LAGS + B_LAGS, step)

            @block.vector
            def _(dve):
                def step(cs):
                    a, b = cs[0:4], cs[4:8]
                    now_b = present(b, B_LAGS)
                    if now_b is not None:
                        lo, hi, t = now_b
                        dve.wait_ge(rstd_done, t - 1)
                        for l in BY_ACT:
                            if b[l] is not None and b[l].has(1):
                                dve.wait_ge(applied[l], b[l].count(1))
                        nc.vector.scalar_tensor_tensor(shift[:, lo * 4:hi * 4], mv[:, lo * 4:hi * 4, 0], -1.0,
                                                       rstd[:, lo * 4:hi * 4], ALU.mult, ALU.mult).then_inc(shift_done, 1)
                        if b[2] is not None:
                            if b[2].slot_used():
                                dve.wait_ge(stored[2][b[2].slot], b[2].landed(16, 1))
                            ln_apply(nc, normed[:, 2, b[2].slot], y[:, 2, b[2].slot % 2], mv[:, 8:12], rstd[:, 8:12])\
                                .then_inc(applied[2], 1)
                    now_a = present(a, A_LAGS)
                    if now_a is None:
                        return
                    lo, hi, t = now_a
                    early = [l for l in range(lo, hi) if l != 2]

                    def add_x(l):
                        if a[l] is not None:
                            dve.wait_ge(z_done[l], a[l].count())
                            nc.vector.scalar_tensor_tensor(y[:, l, a[l].slot % 2], tiles(psZ[l][0][:, :]), 0.0,
                                                           source(l, a[l]), ALU.max, ALU.add).then_inc(y_done[l], 1)

                    def measure(l):
                        if a[l] is not None:
                            ln_stats(nc, before_norm(l, a[l]), stats, mv, at=4 * l)

                    def aggregate(l):
                        for k in range(4 * l, 4 * l + 4):
                            last = nc.vector.bn_aggr(mv[:, k, :], stats[:, k, :])
                        return last

                    if a[0] is not None:
                        dve.wait_ge(z_done[0], a[0].count())
                    measure(0)
                    add_x(1)
                    dve.drain()
                    measure(3)
                    add_x(2)
                    measure(1)
                    dve.drain()
                    for l in early:
                        last = aggregate(l)
                    if a[2] is not None:
                        dve.wait_ge(elu_done, a[2].count())
                        nc.vector.scalar_tensor_tensor(y[:, 2, a[2].slot % 2], low[:, :, :], -1.0,
                                                       y[:, 2, a[2].slot % 2], ALU.add, ALU.add)
                        dve.drain()
                        measure(2)
                        dve.drain()
                        last = aggregate(2)
                    last.then_inc(stats_done, 1)
                    dve.drain()
                run_chunks(dve, n, R, A_LAGS + B_LAGS, step)
        end_phase(nc, P)


class Sizes:
    def __init__(self, N, E):
        self.N, self.E = N, E
        self.NQ = -(-N // 128)
        self.LE = 125
        self.GT = 4
        self.TT = E // self.LE
        assert E % self.LE == 0 and self.TT % (2 * self.GT) == 0
        self.ED = -(-E // CH) * CH
        self.EC = -(-2 * E // CH) * CH


class Tables:
    pass


def build_sort(nc, g, w, T, A):
    N, E, NQ, LE, GT, TT = g.N, g.E, g.NQ, g.LE, g.GT, g.TT
    GE = GT * LE
    RING = 2 * GT
    with ExitStack() as ctx:
        P = Phase(nc, ctx, "sort")
        ends = P.sb("ends", [LE, 2, TT], I32)
        kind = P.sb("kind", [LE, TT], I32)
        ew = P.sb("ew", [LE, TT])
        part = P.sb("part", [LE, 2 * TT], I32)
        key = P.sb("key", [LE, 2 * TT])
        lane = P.sb("lane", [LE, 2 * TT])
        quot = P.sb("quot", [LE, 2 * TT])
        iota_q = P.sb("iota_q", [128, NQ], F16)
        iota_l = P.sb("iota_l", [128, 128], F16)
        iota_p = P.sb("iota_p", [128, 1])
        earlier = P.sb("earlier", [LE, LE])
        below = P.sb("below", [128, 128])
        zeros = P.sb("zeros", [128, NQ])
        hist = P.sb("hist", [128, 2, NQ])
        base = P.sb("base", [128, 2, NQ])
        nv_tab = P.sb("nv_tab", [128, NQ])
        row_sum = P.sb("row_sum", [128, 2])
        row_pre = P.sb("row_pre", [128, 2])
        running = P.sb("running", [128, 2, NQ])
        oh_lane = P.sb("oh_lane", [LE, 2, 128], BF16)
        oh_quot = P.sb("oh_quot", [LE, 2, NQ], BF16)
        key_row = P.sb("key_row", [128, 2, GE], I32)
        lane_row = P.sb("lane_row", [128, GE], I32)
        oh_row = P.sb("oh_row", [128, 2, GE])
        junk = P.sb("junk", [LE, 3, NQ])
        junk2 = P.sb("junk2", [LE, LE])
        rank = P.sb("rank", [LE, 2])
        found = P.sb("found", [LE, 3, GT])
        at_c = P.sb("at_c", [LE, 2, GT], I32)
        at_d = P.sb("at_d", [LE, 2, GT], I32)
        out_c = P.sb("out_c", [LE, 2, GT, 2], I32)
        out_d = P.sb("out_d", [LE, 2, GT, REC], I32)
        pad = P.sb("pad", [128, REC], I32)
        ps_look = [[P.ps(f"look{k}{s}") for s in range(2)] for k in range(3)]
        ps_run = P.ps("run")
        loaded, made, cols_ready = P.sem("loaded"), P.sem("made"), P.sem("cols_ready")
        oh1, hist_done = P.sem("oh1"), P.sem("hist_done")
        sums_ready, pre_done, base_ready = P.sem("sums_ready"), P.sem("pre_done"), P.sem("base_ready")
        oh_ready, updated, run_copied, looked, selected = (
            P.sem(s) for s in ("oh_ready", "updated", "run_copied", "looked", "selected"))
        row_ready, row_used, rec_ready = P.sem("row_ready"), P.sem("row_used"), P.sem("rec_ready")
        keys_landed, attrs_landed, scattered = (P.sems(s, 2) for s in ("keys_landed", "attrs_landed", "scattered"))
        padded = P.sem("padded")
        A_keys = [A["dst"], A["src"]]
        full_q = N // 128

        def col(t, c):
            return t[:, c.i:c.i + 1] if isinstance(c.i, int) else t[:, bass.ds(c.i, 1)]

        def group(c):
            s = c.slot // GT
            return Chunk(c.turn * 2 + s, s, c.turn, 2)

        def seg(t, start, size):
            return t[start:start + size] if isinstance(start, int) else t[bass.ds(start, size)]

        with nc.Block() as block:
            @block.sync
            def _(sp):
                with nc.allow_non_contiguous_dma(reason="one word per edge"):
                    for k in range(2):
                        sp.dma_start(ends[:, k, :], A_keys[k].rearrange("(j p) -> p j", p=LE)).then_inc(loaded, 16)
                    sp.dma_start(kind[:, :], A["edge_type_64"].rearrange("(j p) -> p j", p=LE)).then_inc(loaded, 16)
                    sp.dma_start(ew[:, :], A["edge_weight"].rearrange("(j p) -> p j", p=LE)).then_inc(loaded, 16)
                    sp.wait_ge(made, 1)
                    sp.dma_start(nv_tab[:, 0:full_q],
                                 A["node_vec"][0:128 * full_q].rearrange("(q p) -> p q", p=128)).then_inc(loaded, 16)
                    if N % 128:
                        sp.dma_start(nv_tab[0:N % 128, full_q:NQ],
                                     A["node_vec"][128 * full_q:N].rearrange("(p q) -> p q", q=1)).then_inc(loaded, 16)
                n_pads = 0
                for table, width, used, slots in ((T.rec_c, 2, 2 * E, g.EC), (T.rec_d, REC, E, g.ED)):
                    sp.dma_start(table[0:1, :], pad[0:1, 0:width]).then_inc(padded, 16)
                    n_pads += 1
                    at = 1 + used
                    while at < slots + 2:
                        k = min(128, slots + 2 - at)
                        sp.dma_start(table[at:at + k, :], pad[0:k, 0:width]).then_inc(padded, 16)
                        at += k
                        n_pads += 1

                def step(cs):
                    c = cs[0]
                    k = step.k
                    first = c.i - k * (TT // GT)
                    if not isinstance(first, int):
                        first = sp.snap(first)
                    start = first * GE if isinstance(first, int) else sp.snap(first * GE)
                    if c.has(2):
                        sp.wait_ge(row_used, c.count(2))
                    sp.dma_start(key_row[:, c.slot, :], seg(A_keys[k], start, GE).partition_broadcast(128))\
                      .then_inc(keys_landed[c.slot], 16)
                    if k == 0:
                        if c.slot_used():
                            sp.wait_ge(scattered[c.slot], c.landed(16 * 2 * GT, 1))
                        hold(sp, w)
                        for lo, hi, name in ((W_SH, W_SH + N_SH, "edge_attr_4"), (W_LEN, W_LEN + N_LEN, "edge_attr_10")):
                            src = seg(A[name], start, GE)
                            sp.dma_start(out_d[:, c.slot, :, lo:hi], src.rearrange("(j p) c -> p j c", p=LE).bitcast(I32))\
                              .then_inc(attrs_landed[c.slot], 16)
                for step.k in range(2):
                    run_chunks(sp, TT // GT, 2, [0], step, base=step.k * (TT // GT))
                sp.wait_ge(padded, 16 * n_pads)

            @block.gpsimd
            def _(pool):
                nc.gpsimd.memset(nv_tab[:, :], 0.0)
                nc.gpsimd.memset(zeros[:, :], 0.0)
                nc.gpsimd.memset(pad[:, :], 0)
                nc.gpsimd.memset(out_d[:, :, :, :], 0)
                nc.gpsimd.memset(earlier[:, :], 1.0)
                nc.gpsimd.memset(below[:, :], 1.0)
                nc.gpsimd.iota(iota_q[:, :], pattern=[[1, NQ]], base=0, channel_multiplier=0,
                               allow_small_or_imprecise_dtypes=True)
                nc.gpsimd.iota(iota_l[:, :], pattern=[[1, 128]], base=0, channel_multiplier=0,
                               allow_small_or_imprecise_dtypes=True)
                nc.gpsimd.iota(iota_p[:, :], pattern=[[0, 1]], base=0, channel_multiplier=1,
                               allow_small_or_imprecise_dtypes=True)
                pool.drain()
                nc.gpsimd.affine_select(out=earlier[:, :], in_=earlier[:, :], compare_op=ALU.is_gt, fill=0.0, base=0,
                                        pattern=[[-1, LE]], channel_multiplier=1)
                nc.gpsimd.affine_select(out=below[:, :], in_=below[:, :], compare_op=ALU.is_gt, fill=0.0, base=0,
                                        pattern=[[1, 128]], channel_multiplier=-1)
                nc.gpsimd.memset(pad[:, 0:1], N)
                pool.drain()
                nc.gpsimd.memset(zeros[:, 0:1], 0.0).then_inc(made, 1)
                bound_c, bound_d = pool.to_reg(g.EC + 1), pool.to_reg(g.ED + 1)

                def step(cs):
                    c = cs[0]
                    pool.wait_ge(rec_ready, c.count())
                    hold(pool, w)
                    for t in range(GT):
                        pool.indirect_dma_start(T.rec_c, bass.IndirectOffsetOnAxis(ap=at_c[:, c.slot, t:t + 1], axis=0),
                                                out_c[:, c.slot, t, :], None, bounds_check=bound_c, oob_is_err=False)\
                            .then_inc(scattered[c.slot], 16)
                        if step.k == 0:
                            pool.indirect_dma_start(T.rec_d, bass.IndirectOffsetOnAxis(ap=at_d[:, c.slot, t:t + 1], axis=0),
                                                    out_d[:, c.slot, t, :], None, bounds_check=bound_d, oob_is_err=False)\
                                .then_inc(scattered[c.slot], 16)
                for step.k in range(2):
                    run_chunks(pool, TT // GT, 2, [0], step, base=step.k * (TT // GT))
                for s in range(2):
                    pool.wait_ge(scattered[s], 16 * 3 * GT * (TT // GT) // 2)

            @block.tensor
            def _(pe):
                pe.wait_ge(made, 1)
                for k in range(2):
                    def step(cs):
                        c = cs[0]
                        pe.wait_ge(oh1, c.count())
                        nc.tensor.matmul(ps_look[k][0][:, 0:NQ], oh_lane[:, c.slot, :], oh_quot[:, c.slot, :],
                                         start=isinstance(c.i, int) and c.i == k * TT,
                                         stop=isinstance(c.i, int) and c.i == k * TT + TT - 1).then_inc(hist_done, 1)
                    run_chunks(pe, TT, 2, [0], step, base=k * TT)
                pe.wait_ge(sums_ready, 1)
                nc.tensor.matmul(ps_look[2][0][:, 0:2], below[:, :], row_sum[:, :], start=True, stop=True).then_inc(pre_done, 1)
                pe.wait_ge(base_ready, 1)
                pe.wait_ge(loaded, 16 * (6 if N % 128 else 5))
                nc.tensor.matmul(ps_run[:, 0:NQ], w["ident"][:, :], base[:, 0, :], start=True, stop=True).then_inc(updated, 1)
                for k in range(2):
                    def step(cs):
                        c = cs[0]
                        pe.wait_ge(oh_ready, c.count())
                        pe.wait_ge(run_copied, c.count())
                        nc.tensor.matmul(ps_run[:, 0:NQ], oh_lane[:, c.slot % 2, :], oh_quot[:, c.slot % 2, :],
                                         start=False, stop=True, skip_group_check=True).then_inc(updated, 1)
                        gr = group(c)
                        pe.wait_ge(row_ready, gr.count())
                        if c.has(2):
                            pe.wait_ge(selected, c.count(2))
                        t = c.slot % GT
                        oh = oh_row[:, gr.slot, t * LE:(t + 1) * LE]
                        tabs = [running[:, c.slot % 2, :]] + ([base[:, 1, :], nv_tab[:, :]] if k == 0 else [])
                        for i, tab in enumerate(tabs):
                            ins = nc.tensor.matmul(ps_look[i][c.slot % 2][0:LE, 0:NQ], oh, tab, start=True, stop=True)
                        ins.then_inc(looked, 1)
                    run_chunks(pe, TT, RING, [0], step, base=k * TT)

            @block.scalar
            def _(act):
                nc.scalar.preload_act_table_set(ACT_SET)
                act.wait_ge(updated, 1)
                nc.scalar.activation(running[:, 0, :], ps_run[:, 0:NQ], ACT.Copy).then_inc(run_copied, 1)

                def step(cs):
                    c = cs[0]
                    if isinstance(c.i, int) and c.i == 2 * TT - 1:
                        return
                    act.wait_ge(updated, c.i + 2)
                    if c.has(1):
                        act.wait_ge(looked, c.count(1))
                    nc.scalar.activation(running[:, (c.slot + 1) % 2, :], ps_run[:, 0:NQ], ACT.Copy).then_inc(run_copied, 1)
                run_chunks(act, 2 * TT, RING, [0], step)

            @block.vector
            def _(dve):
                v = nc.vector
                dve.wait_ge(made, 1)
                dve.wait_ge(loaded, 16 * (6 if N % 128 else 5))
                both = ends[:, :, :].rearrange("p k j -> p (k j)")
                v.tensor_copy(key[:, :], both)
                v.tensor_scalar(part[:, :], both, 127, None, ALU.bitwise_and)
                dve.drain()
                v.tensor_copy(lane[:, :], part[:, :])
                dve.drain()
                v.tensor_scalar(part[:, :], both, 7, None, ALU.logical_shift_right)
                dve.drain()
                v.tensor_copy(quot[:, :], part[:, :])
                dve.drain()

                def one_hots(c, s, sem):
                    v.tensor_scalar(oh_lane[:, s, :], iota_l[0:LE, :], col(lane, c), None, ALU.is_equal)
                    v.tensor_scalar(oh_quot[:, s, :], iota_q[0:LE, :], col(quot, c), None, ALU.is_equal)\
                     .then_inc(sem, 1)

                def step(cs):
                    if cs[0].has(2):
                        dve.wait_ge(hist_done, cs[0].count(2))
                    one_hots(cs[0], cs[0].slot, oh1)
                run_chunks(dve, 2 * TT, 2, [0], step)
                dve.wait_ge(hist_done, 2 * TT)
                for k in range(2):
                    v.tensor_copy(hist[:, k, :], ps_look[k][0][:, 0:NQ])
                dve.drain()
                v.tensor_reduce(row_sum[:, :], hist[:, :, :], AX_X, ALU.add).then_inc(sums_ready, 1)
                dve.wait_ge(pre_done, 1)
                v.tensor_copy(row_pre[:, :], ps_look[2][0][:, 0:2])
                dve.drain()
                for k in range(2):
                    v.tensor_tensor_scan(base[:, k, :], hist[:, k, :], zeros[:, :], row_pre[:, k:k + 1], ALU.add, ALU.add)
                dve.drain()
                v.tensor_tensor(base[:, :, :], base[:, :, :], hist[:, :, :], ALU.subtract)
                dve.drain()
                v.scalar_tensor_tensor(base[:, 0, :], base[:, 0, :], 1.0, base[:, 1, :], ALU.add, ALU.add).then_inc(base_ready, 1)

                for k in range(2):
                    def step(cs):
                        c = cs[0]
                        dve.drain()
                        if c is not None:
                            gr = group(c)
                            if c.slot % GT == 0:
                                dve.wait_ge(keys_landed[gr.slot], gr.landed(16))
                                if c.has(GT + 1):
                                    dve.wait_ge(looked, c.count(GT + 1))
                                v.tensor_scalar(lane_row[:, :], key_row[:, gr.slot, :], 127, None, ALU.bitwise_and)
                                dve.drain()
                                v.tensor_scalar(oh_row[:, gr.slot, :], lane_row[:, :], iota_p[:, 0:1], None,
                                                ALU.is_equal).then_inc(row_ready, 1)
                            if c.has(1):
                                dve.wait_ge(updated, c.count(1))
                            one_hots(c, c.slot % 2, oh_ready)
                            t = c.slot % GT
                            ins = v.scalar_tensor_tensor(junk2[:, :], key_row[0:LE, gr.slot, t * LE:(t + 1) * LE],
                                                         col(key, c), earlier[:, :], ALU.is_equal, ALU.mult,
                                                         accum_out=rank[:, c.slot % 2:c.slot % 2 + 1])
                            if t == GT - 1:
                                ins.then_inc(row_used, 1)
                        c = cs[1]
                        if c is None:
                            return
                        gr = group(c)
                        t = c.slot % GT
                        dve.wait_ge(looked, c.count())
                        for i in range(3 if k == 0 else 1):
                            first = rank[:, c.slot % 2:c.slot % 2 + 1] if i == 0 else 0.0
                            ins = v.tensor_tensor_reduce(junk[:, i, :], ps_look[i][c.slot % 2][0:LE, 0:NQ],
                                                         oh_quot[:, c.slot % 2, :], 1.0, first, ALU.mult, ALU.add,
                                                         found[:, i, t:t + 1])
                        ins.then_inc(selected, 1)
                        if t != GT - 1:
                            return
                        rel = c.i - (GT - 1 + k * TT)
                        dve.drain()
                        wait_scattered(gr, k)
                        def cols(tab, start):
                            return tab[:, start:start + GT] if isinstance(start, int) else tab[:, bass.ds(start, GT)]
                        v.tensor_copy(at_c[:, gr.slot, :], found[:, 0, :])
                        v.tensor_copy(out_c[:, gr.slot, :, 0], cols(ends[:, k, :], rel))
                        if k == 0:
                            dve.wait_ge(attrs_landed[gr.slot], gr.landed(32))
                            v.tensor_copy(out_c[:, gr.slot, :, 1], cols(ends[:, 1, :], rel))
                            v.tensor_tensor(at_d[:, gr.slot, :], found[:, 0, :], found[:, 1, :], ALU.subtract)
                            v.tensor_copy(out_d[:, gr.slot, :, W_DST], cols(ends[:, 0, :], rel))
                            v.tensor_copy(out_d[:, gr.slot, :, W_SRC], cols(ends[:, 1, :], rel))
                            v.tensor_copy(out_d[:, gr.slot, :, W_TYPE], cols(kind[:, :], rel))
                            v.tensor_copy(out_d[:, gr.slot, :, W_EW], cols(ew[:, :].bitcast(I32), rel))
                            v.tensor_copy(out_d[:, gr.slot, :, W_NV], found[:, 2, :].bitcast(I32))
                        else:
                            v.tensor_copy(out_c[:, gr.slot, :, 1], cols(ends[:, 0, :], rel))
                        dve.drain().then_inc(rec_ready, 1)

                    def wait_scattered(gr, k):
                        half = TT // GT // 2
                        if k == 0:
                            if gr.slot_used():
                                dve.wait_ge(scattered[gr.slot], gr.landed(16 * 2 * GT, 1))
                        else:
                            dve.wait_ge(scattered[gr.slot], (gr.turn - half) * (16 * GT) + 16 * 2 * GT * half)
                    run_chunks(dve, TT, RING, [0, 1], step, base=k * TT)
        end_phase(nc, P)


class Slots:

    RING = 8

    def __init__(self, P, nc, g, w, table, width, n, backwards):
        self.nc, self.g, self.w, self.table, self.width, self.n, self.back = nc, g, w, table, width, n, backwards
        R = self.RING
        self.rec = P.sb("rec", [128, R, TPC, width], I32)
        self.near = P.sb("near", [128, R, 2, TPC], I32)
        self.same = P.sb("same", [128, R, 2, TPC], BF16)
        self.inner = P.sb("inner", [128, R, TPC])
        self.row = P.sb("row", [128, R, TPC])
        self.to = P.sb("to", [128, R, TPC], I32)
        self.of = P.sb("of", [128, R, 2, TPC], I32)
        self.landed = P.sems("rec_landed", R)
        self.ready = P.sem("idx_ready")

    def pos(self, c):
        return self.n - 1 - c.i if self.back else c.i

    def start(self, eng, c):
        p = self.pos(c)
        return p * CH if isinstance(p, int) else eng.snap(p * CH)

    def rows(self, t, start, off=0):
        part = t[start + off:start + off + CH] if isinstance(start, int) else t[bass.ds(start + off, CH)]
        return part

    def load(self, sp, c, start):
        R = self.rows
        with self.nc.allow_non_contiguous_dma(reason="one word per slot"):
            sp.dma_start(self.rec[:, c.slot], R(self.table, start, 1).rearrange("(t p) w -> p t w", p=128))\
              .then_inc(self.landed[c.slot], 16)
            for k in range(2):
                sp.dma_start(self.near[:, c.slot, k, :],
                             R(self.table, start, 2 * k)[:, 0].rearrange("(t p) -> p t", p=128))\
                  .then_inc(self.landed[c.slot], 16)

    def index(self, dve, c, other_scale=1, to_scale=1, to_plus=0):
        v = self.nc.vector
        dve.wait_ge(self.landed[c.slot], c.landed(48))
        s = c.slot
        node = self.rec[:, s, :, 0]
        first, last = (1, 0) if self.back else (0, 1)
        v.tensor_tensor(self.same[:, s, 0, :], node, self.near[:, s, first, :], ALU.is_equal)
        v.tensor_tensor(self.inner[:, s, :], node, self.near[:, s, last, :], ALU.is_equal)
        v.tensor_scalar(self.of[:, s, 1, :], node, self.g.N - 1, other_scale, ALU.min, ALU.mult)
        v.tensor_scalar(self.of[:, s, 0, :], self.rec[:, s, :, 1], other_scale, None, ALU.mult)
        if to_scale != 1:
            v.tensor_scalar(self.row[:, s, :], node, to_scale, to_plus, ALU.mult, ALU.add)
            node = self.row[:, s, :]
        dve.drain()
        v.tensor_scalar(self.same[:, s, 1, :], self.same[:, s, 0, :], -1.0, -NEG, ALU.add, ALU.mult)
        v.scalar_tensor_tensor(self.to[:, s, :], self.inner[:, s, :], float(FAR), node, ALU.mult, ALU.add)
        dve.drain().then_inc(self.ready, 1)

    def gather(self, pool, c, which, out, table, bound, sem):
        for t in range(TPC):
            pool.indirect_dma_start(out[:, c.slot, t, :], None, table,
                                    bass.IndirectOffsetOnAxis(ap=self.of[:, c.slot, which, t:t + 1], axis=0),
                                    bounds_check=bound, oob_is_err=False).then_inc(sem[c.slot], 16)

    def scatter(self, pool, c, rows, table, bound, sem):
        for t in range(TPC):
            pool.indirect_dma_start(table, bass.IndirectOffsetOnAxis(ap=self.to[:, c.slot, t:t + 1], axis=0),
                                    rows[:, c.slot, t, :], None,
                                    bounds_check=bound, oob_is_err=False).then_inc(sem[c.slot], 16)


def scan(nc, S, out, mask, data, carry, op0, op1):
    if S.back:
        out, mask, data = out[:, ::-1], mask[:, ::-1], data[:, ::-1]
    return nc.vector.tensor_tensor_scan(out, mask, data, carry if carry is not None else 0.0, op0, op1)


def edge_col(S, t):
    return t[:, 0:1] if S.back else t[:, CH - 1:CH]


def turns(n, slot, ring):
    return (n - slot + ring - 1) // ring


def build_layer0(nc, g, w, T, A):
    n = g.ED // CH
    with ExitStack() as ctx:
        P = Phase(nc, ctx, "l0")
        S = Slots(P, nc, g, w, T.rec_d, REC, n, False)
        R = S.RING
        xs = P.sb("xs", [128, R, TPC, D])
        xd = P.sb("xd", [128, R, TPC, D])
        out = P.sb("out", [128, R, TPC, D])
        xsT = P.sb("xsT", [128, CH])
        xdT = P.sb("xdT", [128, 2, CH])
        attrT = P.sb("attrT", [N_ATTR, CH])
        hT = P.sb("hT", [100, CH])
        mask = P.sb("mask", [128, 2, CH])
        sh = P.sb("sh", [128, 2, CH])
        part = P.sb("part", [128, 3, CH])
        msg = P.sb("msg", [128, 3, CH])
        agg = P.sb("agg", [128, 2, CH])
        y = P.sb("y", [128, TPC, D])
        stats, mv, rstd = P.sb("stats", [128, 4, 6]), P.sb("mv", [128, 4, 2]), P.sb("rstd", [128, 4])
        ps = [P.ps(f"ps{k}") for k in range(8)]
        names = ("tr", "trd", "h", "m", "s1", "s2", "g", "w", "o", "z")
        pe_ = {k: P.sem("pe_" + k) for k in names}
        ac_ = {k: P.sem("ac_" + k) for k in ("tr", "trd", "h", "m", "s1", "s2", "rstd")}
        ve_ = {k: P.sem("ve_" + k) for k in ("part", "msg", "agg", "y", "stats", "out")}
        gathered, scattered, saved = P.sems("gathered", R), P.sems("scattered", R), P.sems("saved", R)
        lags = [0, 2, 3]
        with nc.Block() as block:
            @block.sync
            def _(sp):
                def step(cs):
                    c = cs[0]
                    if c is not None:
                        start = S.start(sp, c)
                        if c.slot_used():
                            sp.wait_ge(scattered[c.slot], c.landed(64, 1))
                        hold(sp, w)
                        if c.slot_used():
                            sp.wait_ge(saved[c.slot], c.landed(16, 1))
                        hold(sp, w)
                        S.load(sp, c, start)
                    c = cs[1]
                    if c is not None:
                        start = S.start(sp, c)
                        sp.wait_ge(ve_["out"], c.count())
                        hold(sp, w)
                        sp.dma_start(S.rows(T.x1_slot, start).rearrange("(t p) c -> p t c", p=128), out[:, c.slot])\
                          .then_inc(saved[c.slot], 16)
                run_chunks(sp, n, R, [0, 3], step)
                for s in range(R):
                    sp.wait_ge(saved[s], 16 * turns(n, s, R))

            @block.gpsimd
            def _(pool):
                bound = pool.to_reg(g.N - 1)

                def step(cs):
                    c = cs[0]
                    if c is not None:
                        pool.wait_ge(S.ready, c.count())
                        hold(pool, w)
                        S.gather(pool, c, 0, xs, T.x, bound, gathered)
                        S.gather(pool, c, 1, xd, T.x, bound, gathered)
                    c = cs[1]
                    if c is not None:
                        pool.wait_ge(ve_["out"], c.count())
                        hold(pool, w)
                        S.scatter(pool, c, out, T.x1, bound, scattered)
                run_chunks(pool, n, R, [0, 2], step)
                for s in range(R):
                    pool.wait_ge(scattered[s], 64 * turns(n, s, R))

            @block.tensor
            def _(pe):
                mm = nc.tensor.matmul

                def step(cs):
                    a, b = cs
                    if a is not None:
                        pe.wait_ge(gathered[a.slot], a.landed(128))
                        if a.has(1):
                            pe.wait_ge(ac_["trd"], a.count(1))
                        if a.has(1):
                            pe.wait_ge(ac_["s1"], a.count(1))
                        transpose4(nc, ps[0], xs[:, a.slot], w["ident"])
                        for t in range(TPC):
                            last = nc.tensor.transpose(ps[1][0:N_ATTR, t * TILE:(t + 1) * TILE],
                                                       S.rec[:, a.slot, t, W_SH:W_SH + N_ATTR].bitcast(F32),
                                                       w["ident"][:, :])
                        last.then_inc(pe_["tr"], 1)
                        if a.has(1):
                            pe.wait_ge(ac_["m"], a.count(1))
                        spread(nc, ps[2], S.same[:, a.slot, 0, :], w["identb"]).then_inc(pe_["m"], 1)
                        pe.wait_ge(ac_["tr"], a.count())
                        transpose4(nc, ps[0], xd[:, a.slot], w["ident"]).then_inc(pe_["trd"], 1)
                        mm(ps[1][0:100, :], w["fc1"][:, :], attrT[:, :], start=True, stop=True).then_inc(pe_["h"], 1)
                        if a.has(1):
                            pe.wait_ge(ve_["msg"], a.count(1))
                        mm(ps[3][:, :], w["g1"][:, :], xsT[:, :], start=True, stop=True)
                        mm(ps[4][:, :], w["g2"][:, :], xsT[:, :], start=True, stop=True).then_inc(pe_["g"], 1)
                        pe.wait_ge(ac_["h"], a.count())
                        mm(ps[1][:, :], w["sel_sh"][:, :], attrT[:, :], start=True, stop=True).then_inc(pe_["s1"], 1)
                        if a.has(2):
                            pe.wait_ge(ve_["agg"], a.count(2))
                        mm(ps[6][:, :], w["sel_sh0"][:, :], attrT[:, :], start=True, stop=True).then_inc(pe_["s2"], 1)
                    if b is not None:
                        if a is not None:
                            pe.wait_ge(ac_["s2"], a.count())
                        pe.wait_ge(ve_["msg"], b.count())
                        for k in range(3):
                            last = mm(ps[6][:, :], w[f"o{k + 1}"][:, :], msg[:, k, :], start=k == 0, stop=k == 2)
                        last.then_inc(pe_["o"], 1)
                    if a is not None:
                        pe.wait_ge(ve_["part"], a.count())
                        mm(ps[5][:, :], w["h1"][:, :], hT[:, :], start=True, stop=True)
                        mm(ps[3][:, :], w["h2"][:, :], hT[:, :], start=True, stop=True)
                        mm(ps[4][:, :], w["h3"][:, :], hT[:, :], start=True, stop=True).then_inc(pe_["w"], 1)
                    if b is not None:
                        pe.wait_ge(ve_["agg"], b.count())
                        if b.has(1):
                            pe.wait_ge(ve_["y"], b.count(1))
                        for t in range(TPC):
                            ts = slice(t * TILE, (t + 1) * TILE)
                            mm(ps[7][:, ts], agg[:, b.slot % 2, ts], w["ident"][:, :], start=True, stop=False)
                            last = mm(ps[7][:, ts], xdT[:, b.slot % 2, ts], w["Wsi"][:, :], start=False, stop=True)
                        last.then_inc(pe_["z"], 1)
                run_chunks(pe, n, R, [0, 1], step)

            @block.scalar
            def _(act):
                nc.scalar.preload_act_table_set(ACT_SET)
                ac = nc.scalar.activation

                def step(cs):
                    a, b = cs
                    if a is not None:
                        act.wait_ge(pe_["tr"], a.count())
                        if a.has(1):
                            act.wait_ge(pe_["g"], a.count(1))
                        if a.has(1):
                            act.wait_ge(pe_["s2"], a.count(1))
                        ac(xsT[:, :], ps[0][:, :], ACT.Copy)
                        ac(attrT[:, :], ps[1][0:N_ATTR, :], ACT.Copy).then_inc(ac_["tr"], 1)
                        act.wait_ge(pe_["h"], a.count())
                        if a.has(1):
                            act.wait_ge(pe_["w"], a.count(1))
                        ac(hT[:, :], ps[1][0:100, :], ACT.Relu).then_inc(ac_["h"], 1)
                        act.wait_ge(pe_["trd"], a.count())
                        if a.has(2):
                            act.wait_ge(pe_["z"], a.count(2))
                        ac(xdT[:, a.slot % 2, :], ps[0][:, :], ACT.Copy).then_inc(ac_["trd"], 1)
                        act.wait_ge(pe_["s1"], a.count())
                        if a.has(1):
                            act.wait_ge(ve_["part"], a.count(1))
                        ac(sh[:, 0, :], ps[1][:, :], ACT.Copy).then_inc(ac_["s1"], 1)
                        act.wait_ge(pe_["s2"], a.count())
                        ac(sh[:, 1, :], ps[6][:, :], ACT.Copy).then_inc(ac_["s2"], 1)
                        act.wait_ge(pe_["m"], a.count())
                        if a.has(2):
                            act.wait_ge(ve_["agg"], a.count(2))
                        ac(mask[:, a.slot % 2, :], ps[2][:, :], ACT.Copy).then_inc(ac_["m"], 1)
                    if b is not None:
                        act.wait_ge(ve_["stats"], b.count())
                        ln_rstd(nc, act, mv[:, :, 1], rstd[:, :], w["eps"]).then_inc(ac_["rstd"], 1)
                run_chunks(act, n, R, [0, 1], step)

            @block.vector
            def _(dve):
                v = nc.vector

                def step(cs):
                    m, a, b = cs
                    dve.drain()
                    if m is not None:
                        S.index(dve, m)
                    if a is not None:
                        dve.wait_ge(pe_["g"], a.count())
                        dve.wait_ge(ac_["s2"], a.count())
                        v.tensor_tensor(part[:, 0, :], ps[3][:, :], sh[:, 0, :], ALU.mult)
                        v.tensor_tensor(part[:, 1, :], ps[4][:, :], sh[:, 1, :], ALU.mult)
                        v.tensor_tensor(part[:, 2, :], ps[4][:, :], sh[:, 0, :], ALU.mult).then_inc(ve_["part"], 1)
                    if b is not None:
                        dve.wait_ge(pe_["o"], b.count())
                        dve.wait_ge(ac_["m"], b.count())
                        if b.has(2):
                            dve.wait_ge(pe_["z"], b.count(2))
                        k = b.slot % 2
                        carry = None if isinstance(b.i, int) and b.i == 0 else edge_col(S, agg[:, 1 - k, :])
                        scan(nc, S, agg[:, k, :], mask[:, k, :], ps[6][:, :], carry, ALU.mult, ALU.add)\
                            .then_inc(ve_["agg"], 1)
                    dve.drain()
                    if a is not None:
                        dve.wait_ge(pe_["w"], a.count())
                        if a.has(1):
                            dve.wait_ge(pe_["o"], a.count(1))
                        for k, bank in enumerate((5, 3, 4)):
                            last = v.tensor_tensor(msg[:, k, :], ps[bank][:, :], part[:, k, :], ALU.mult)
                        last.then_inc(ve_["msg"], 1)
                    if b is not None:
                        dve.wait_ge(pe_["z"], b.count())
                        v.tensor_tensor(y[:, :, :], tiles(ps[7][:, :]), xd[:, b.slot], ALU.add).then_inc(ve_["y"], 1)
                        finish_rows(nc, dve, b, y, stats, mv, rstd, out, ve_, ac_["rstd"])
                run_chunks(dve, n, R, lags, step)
        end_phase(nc, P)


def finish_rows(nc, dve, b, y, stats, mv, rstd, out, ve_, rstd_done):
    dve.drain()
    ln_stats(nc, y, stats, mv)
    dve.drain()
    ln_aggregate(nc, stats, mv, TPC).then_inc(ve_["stats"], 1)
    dve.drain()
    dve.wait_ge(rstd_done, b.count())
    ln_apply(nc, out[:, b.slot], y, mv, rstd).then_inc(ve_["out"], 1)


def build_layer1(nc, g, w, T, A):
    n = g.ED // CH
    with ExitStack() as ctx:
        P = Phase(nc, ctx, "l1")
        S = Slots(P, nc, g, w, T.rec_d, REC, n, False)
        R = S.RING
        xs = P.sb("xs", [128, R, TPC, D])
        xd = P.sb("xd", [128, R, TPC, D])
        out = P.sb("out", [128, R, TPC, D])
        xsT = P.sb("xsT", [128, CH])
        xdT = P.sb("xdT", [128, 2, CH])
        mask = P.sb("mask", [128, CH])
        ones = P.sb("ones", [128, CH])
        sums, degree = P.sb("sums", [128, 2, CH]), P.sb("degree", [128, 2, CH])
        inv = P.sb("inv", [128, CH])
        mean = P.sb("mean", [128, 2, CH])
        y = P.sb("y", [128, TPC, D])
        stats, mv, rstd = P.sb("stats", [128, 4, 6]), P.sb("mv", [128, 4, 2]), P.sb("rstd", [128, 4])
        ps = [P.ps(f"ps{k}") for k in range(4)]
        pe_ = {k: P.sem("pe_" + k) for k in ("tr", "trd", "m", "z")}
        ac_ = {k: P.sem("ac_" + k) for k in ("tr", "trd", "m", "inv", "rstd")}
        ve_ = {k: P.sem("ve_" + k) for k in ("sum", "mean", "y", "stats", "out", "ones")}
        gathered, scattered, loaded = P.sems("gathered", R), P.sems("scattered", R), P.sems("loaded", R)
        with nc.Block() as block:
            @block.sync
            def _(sp):
                def step(cs):
                    c = cs[0]
                    start = S.start(sp, c)
                    if c.slot_used():
                        sp.wait_ge(scattered[c.slot], c.landed(64, 1))
                    hold(sp, w)
                    S.load(sp, c, start)
                    sp.dma_start(xd[:, c.slot], S.rows(T.x1_slot, start).rearrange("(t p) c -> p t c", p=128))\
                      .then_inc(loaded[c.slot], 16)
                run_chunks(sp, n, R, [0], step)

            @block.gpsimd
            def _(pool):
                bound = pool.to_reg(g.N - 1)

                def step(cs):
                    c = cs[0]
                    if c is not None:
                        pool.wait_ge(S.ready, c.count())
                        hold(pool, w)
                        S.gather(pool, c, 0, xs, T.x1, bound, gathered)
                    c = cs[1]
                    if c is not None:
                        pool.wait_ge(ve_["out"], c.count())
                        hold(pool, w)
                        S.scatter(pool, c, out, T.x2, bound, scattered)
                run_chunks(pool, n, R, [0, 2], step)
                for s in range(R):
                    pool.wait_ge(scattered[s], 64 * turns(n, s, R))

            @block.tensor
            def _(pe):
                mm = nc.tensor.matmul

                def step(cs):
                    a, b = cs
                    if a is not None:
                        pe.wait_ge(gathered[a.slot], a.landed(64))
                        if a.has(1):
                            pe.wait_ge(ac_["tr"], a.count(1))
                        transpose4(nc, ps[0], xs[:, a.slot], w["ident"]).then_inc(pe_["tr"], 1)
                        if a.has(1):
                            pe.wait_ge(ac_["m"], a.count(1))
                        spread(nc, ps[2], S.same[:, a.slot, 0, :], w["identb"]).then_inc(pe_["m"], 1)
                        pe.wait_ge(loaded[a.slot], a.landed(16))
                        if a.has(1):
                            pe.wait_ge(ac_["trd"], a.count(1))
                        transpose4(nc, ps[1], xd[:, a.slot], w["ident"]).then_inc(pe_["trd"], 1)
                    if b is not None:
                        pe.wait_ge(ve_["mean"], b.count())
                        pe.wait_ge(ac_["trd"], b.count())
                        if b.has(1):
                            pe.wait_ge(ve_["y"], b.count(1))
                        add_bias(nc, ps[3], w, "bias1")
                        for t in range(TPC):
                            ts = slice(t * TILE, (t + 1) * TILE)
                            mm(ps[3][:, ts], xdT[:, b.slot % 2, ts], w["W1a"][:, :], start=False, stop=False)
                            last = mm(ps[3][:, ts], mean[:, b.slot % 2, ts], w["W1b"][:, :], start=False,
                                      stop=t == TPC - 1)
                        last.then_inc(pe_["z"], 1)
                run_chunks(pe, n, R, [0, 1], step)

            @block.scalar
            def _(act):
                nc.scalar.preload_act_table_set(ACT_SET)
                ac = nc.scalar.activation

                def step(cs):
                    a, b = cs
                    if a is not None:
                        act.wait_ge(pe_["tr"], a.count())
                        if a.has(1):
                            act.wait_ge(ve_["sum"], a.count(1))
                        ac(xsT[:, :], ps[0][:, :], ACT.Copy).then_inc(ac_["tr"], 1)
                        act.wait_ge(pe_["m"], a.count())
                        ac(mask[:, :], ps[2][:, :], ACT.Copy).then_inc(ac_["m"], 1)
                        act.wait_ge(ve_["sum"], a.count())
                        ac(inv[:, :], degree[:, a.slot % 2, :], ACT.Ln)
                        act.drain()
                        ac(inv[:, :], inv[:, :], ACT.Exp, scale=-1.0).then_inc(ac_["inv"], 1)
                        act.wait_ge(pe_["trd"], a.count())
                        if a.has(2):
                            act.wait_ge(pe_["z"], a.count(2))
                        ac(xdT[:, a.slot % 2, :], ps[1][:, :], ACT.Copy).then_inc(ac_["trd"], 1)
                    if b is not None:
                        act.wait_ge(ve_["stats"], b.count())
                        ln_rstd(nc, act, mv[:, :, 1], rstd[:, :], w["eps"]).then_inc(ac_["rstd"], 1)
                run_chunks(act, n, R, [0, 1], step)

            @block.vector
            def _(dve):
                v = nc.vector
                v.memset(ones[:, :], 1.0)

                def step(cs):
                    m, a, b = cs
                    dve.drain()
                    if m is not None:
                        S.index(dve, m)
                    if a is not None:
                        k = a.slot % 2
                        first = isinstance(a.i, int) and a.i == 0
                        dve.wait_ge(ac_["tr"], a.count())
                        dve.wait_ge(ac_["m"], a.count())
                        scan(nc, S, degree[:, k, :], mask[:, :], ones[:, :],
                             None if first else edge_col(S, degree[:, 1 - k, :]), ALU.mult, ALU.add)
                        scan(nc, S, sums[:, k, :], mask[:, :], xsT[:, :],
                             None if first else edge_col(S, sums[:, 1 - k, :]), ALU.mult, ALU.add)\
                            .then_inc(ve_["sum"], 1)
                        dve.drain()
                        dve.wait_ge(ac_["inv"], a.count())
                        if a.has(2):
                            dve.wait_ge(pe_["z"], a.count(2))
                        v.tensor_tensor(mean[:, k, :], sums[:, k, :], inv[:, :], ALU.mult).then_inc(ve_["mean"], 1)
                    if b is not None:
                        dve.wait_ge(pe_["z"], b.count())
                        v.scalar_tensor_tensor(y[:, :, :], tiles(ps[3][:, :]), 0.0, xd[:, b.slot], ALU.max, ALU.add)\
                            .then_inc(ve_["y"], 1)
                        finish_rows(nc, dve, b, y, stats, mv, rstd, out, ve_, ac_["rstd"])
                run_chunks(dve, n, R, [0, 2, 3], step)
        end_phase(nc, P)


def build_layer2_scores(nc, g, w, T, A):
    n = g.EC // CH
    with ExitStack() as ctx:
        P = Phase(nc, ctx, "l2a")
        S = Slots(P, nc, g, w, T.rec_c, 2, n, False)
        R = S.RING
        xo = P.sb("xo", [128, R, TPC, D])
        xt = P.sb("xt", [128, R, TPC, D])
        xoT = P.sb("xoT", [128, 2, CH])
        xtT = P.sb("xtT", [128, 2, CH])
        fresh = P.sb("fresh", [128, 2, CH])
        raw = P.sb("raw", [128, 2, 2, CH])
        proj = P.sb("proj", [128, R, CH])
        kept = P.sb("kept", [128, R, 3, CH])
        high = P.sb("high", [128, CH])
        ps = [P.ps(f"ps{k}") for k in range(6)]
        pe_ = {k: P.sem("pe_" + k) for k in ("tr", "m", "s", "p")}
        ac_ = {k: P.sem("ac_" + k) for k in ("tr", "m", "s", "p")}
        ve_ = {k: P.sem("ve_" + k) for k in ("s", "max")}
        gathered, saved = P.sems("gathered", R), P.sems("saved", R)
        with nc.Block() as block:
            @block.sync
            def _(sp):
                def step(cs):
                    c = cs[0]
                    if c is not None:
                        start = S.start(sp, c)
                        if c.slot_used():
                            sp.wait_ge(saved[c.slot], c.landed(48, 1))
                        hold(sp, w)
                        S.load(sp, c, start)
                    c = cs[1]
                    if c is not None:
                        p = S.pos(c)
                        p0 = p * 128 if isinstance(p, int) else sp.snap(p * 128)
                        p1 = p * 4 if isinstance(p, int) else sp.snap(p * 4)
                        sp.wait_ge(ac_["p"], c.count())
                        hold(sp, w)
                        sp.dma_start(at_rows(T.proj2, p0, 128), proj[:, c.slot, :]).then_inc(saved[c.slot], 16)
                        sp.dma_start(at_rows(T.row2, p0, 128), xt[:, c.slot].rearrange("p t c -> p (t c)"))\
                          .then_inc(saved[c.slot], 16)
                        sp.wait_ge(ve_["max"], c.count())
                        hold(sp, w)
                        sp.dma_start(at_rows(T.score2, p1, 4), kept[0:128:32, c.slot].rearrange("p k c -> p (k c)"))\
                          .then_inc(saved[c.slot], 16)
                run_chunks(sp, n, R, [0, 3], step)
                for s in range(R):
                    sp.wait_ge(saved[s], 48 * turns(n, s, R))

            @block.gpsimd
            def _(pool):
                bound = pool.to_reg(g.N - 1)

                def step(cs):
                    c = cs[0]
                    pool.wait_ge(S.ready, c.count())
                    hold(pool, w)
                    S.gather(pool, c, 0, xo, T.x2, bound, gathered)
                    S.gather(pool, c, 1, xt, T.x2, bound, gathered)
                run_chunks(pool, n, R, [0], step)

            @block.tensor
            def _(pe):
                mm = nc.tensor.matmul

                def step(cs):
                    a, b = cs
                    if a is not None:
                        pe.wait_ge(gathered[a.slot], a.landed(128))
                        if a.has(1):
                            pe.wait_ge(ac_["tr"], a.count(1))
                        transpose4(nc, ps[0], xo[:, a.slot], w["ident"])
                        transpose4(nc, ps[1], xt[:, a.slot], w["ident"]).then_inc(pe_["tr"], 1)
                        if a.has(1):
                            pe.wait_ge(ac_["m"], a.count(1))
                        spread(nc, ps[2], S.same[:, a.slot, 1, :], w["identb"]).then_inc(pe_["m"], 1)
                    if b is not None:
                        k = b.slot % 2
                        pe.wait_ge(ac_["tr"], b.count())
                        if b.has(1):
                            pe.wait_ge(ac_["s"], b.count(1))
                        mm(ps[3][:, :], w["Asrc"][:, :], xoT[:, k, :], start=True, stop=False)
                        mm(ps[3][:, :], w["Adst"][:, :], xtT[:, k, :], start=False, stop=True)
                        mm(ps[4][:, :], w["Aself"][:, :], xtT[:, k, :], start=True, stop=True).then_inc(pe_["s"], 1)
                        if b.has(1):
                            pe.wait_ge(ac_["p"], b.count(1))
                        mm(ps[5][:, :], w["W2"][:, :], xoT[:, k, :], start=True, stop=True).then_inc(pe_["p"], 1)
                run_chunks(pe, n, R, [0, 1], step)

            @block.scalar
            def _(act):
                nc.scalar.preload_act_table_set(ACT_SET)
                ac = nc.scalar.activation

                def step(cs):
                    a, b = cs
                    if a is not None:
                        k = a.slot % 2
                        act.wait_ge(pe_["tr"], a.count())
                        if a.has(2):
                            act.wait_ge(pe_["p"], a.count(2))
                        ac(xoT[:, k, :], ps[0][:, :], ACT.Copy)
                        ac(xtT[:, k, :], ps[1][:, :], ACT.Copy).then_inc(ac_["tr"], 1)
                        act.wait_ge(pe_["m"], a.count())
                        if a.has(2):
                            act.wait_ge(ve_["max"], a.count(2))
                        ac(fresh[:, k, :], ps[2][:, :], ACT.Copy).then_inc(ac_["m"], 1)
                    if b is not None:
                        k = b.slot % 2
                        act.wait_ge(pe_["s"], b.count())
                        if b.has(2):
                            act.wait_ge(ve_["s"], b.count(2))
                        ac(raw[:, k, 0, :], ps[3][:, :], ACT.Copy)
                        ac(raw[:, k, 1, :], ps[4][:, :], ACT.Copy).then_inc(ac_["s"], 1)
                        act.wait_ge(pe_["p"], b.count())
                        if b.slot_used():
                            act.wait_ge(saved[b.slot], b.landed(48, 1))
                        ac(proj[:, b.slot, :], ps[5][:, :], ACT.Identity, bias=w["bias2c"][:, 0:1]).then_inc(ac_["p"], 1)
                run_chunks(act, n, R, [0, 1], step)

            @block.vector
            def _(dve):
                v = nc.vector

                def step(cs):
                    m, b = cs
                    dve.drain()
                    if m is not None:
                        S.index(dve, m)
                    if b is not None:
                        k = b.slot % 2
                        dve.wait_ge(ac_["s"], b.count())
                        dve.wait_ge(ac_["m"], b.count())
                        if b.slot_used():
                            dve.wait_ge(saved[b.slot], b.landed(48, 1))
                        v.scalar_tensor_tensor(kept[:, b.slot, 0:2, :], raw[:, k, :, :], 0.2, raw[:, k, :, :],
                                               ALU.mult, ALU.max).then_inc(ve_["s"], 1)
                        dve.drain()
                        v.tensor_tensor(high[:, :], kept[:, b.slot, 0, :], kept[:, b.slot, 1, :], ALU.max)
                        dve.drain()
                        first = isinstance(b.i, int) and b.i == 0
                        scan(nc, S, kept[:, b.slot, 2, :], fresh[:, k, :], high[:, :],
                             None if first else edge_col(S, kept[:, (b.slot - 1) % R, 2, :]), ALU.add, ALU.max)\
                            .then_inc(ve_["max"], 1)
                run_chunks(dve, n, R, [0, 3], step)
        end_phase(nc, P)


def at_rows(t, start, size):
    return t[start:start + size, :] if isinstance(start, int) else t[bass.ds(start, size), :]


def build_layer2_sums(nc, g, w, T, A):
    n = g.EC // CH
    x34 = T.x34.rearrange("n k d -> n (k d)")
    with ExitStack() as ctx:
        P = Phase(nc, ctx, "l2b")
        S = Slots(P, nc, g, w, T.rec_c, 2, n, True)
        R = S.RING
        proj = P.sb("proj", [128, R, CH])
        xt = P.sb("xt", [128, R, TPC, D])
        score = P.sb("score", [128, R, 3, CH])
        xtT = P.sb("xtT", [128, 2, CH])
        top = P.sb("top", [128, 2, CH])
        exps = P.sb("exps", [128, CH])
        den, num = P.sb("den", [128, 2, CH]), P.sb("num", [128, 2, CH])
        weighted = P.sb("weighted", [128, CH])
        on = P.sb("on", [128, 2, CH])
        share = P.sb("share", [128, 2, TPC * 4])
        inv = P.sb("inv", [128, TPC * 4])
        z = P.sb("z", [128, TPC, D])
        low = P.sb("low", [128, TPC, D])
        y = P.sb("y", [128, 2, TPC, D])
        out = P.sb("out", [128, R, TPC, 2 * D])
        stats, mv = P.sb("stats", [128, 4, 6]), P.sb("mv", [128, 4, 2])
        rstd, shift = P.sb("rstd", [128, 2, TPC]), P.sb("shift", [128, 2, TPC])
        ps_on, ps_new, ps_xt, ps_num, ps_den, ps_self, ps_score, ps_top = (
            P.ps("ps_" + k) for k in ("on", "new", "xt", "num", "den", "self", "score", "top"))
        pe_ = {k: P.sem("pe_" + k) for k in ("tr", "m", "score", "self", "rows")}
        ac_ = {k: P.sem("ac_" + k) for k in ("tr", "on", "exp", "share", "elu", "rstd", "out")}
        ve_ = {k: P.sem("ve_" + k) for k in ("top", "diff", "less", "num", "z", "stats", "shift")}
        loaded, scattered = P.sems("loaded", R), P.sems("scattered", R)
        with nc.Block() as block:
            @block.sync
            def _(sp):
                def step(cs):
                    c = cs[0]
                    start = S.start(sp, c)
                    p = S.pos(c)
                    p0 = p * 128 if isinstance(p, int) else sp.snap(p * 128)
                    p1 = p * 4 if isinstance(p, int) else sp.snap(p * 4)
                    if c.slot_used():
                        sp.wait_ge(scattered[c.slot], c.landed(64, 1))
                    hold(sp, w)
                    S.load(sp, c, start)
                    sp.dma_start(proj[:, c.slot, :], at_rows(T.proj2, p0, 128)).then_inc(loaded[c.slot], 16)
                    sp.dma_start(xt[:, c.slot].rearrange("p t c -> p (t c)"), at_rows(T.row2, p0, 128))\
                      .then_inc(loaded[c.slot], 16)
                    for h in range(4):
                        src = T.score2[p1 + h] if isinstance(p1, int) else T.score2[bass.ds(p1 + h, 1), :].squeeze(0)
                        sp.dma_start(score[32 * h:32 * h + 32, c.slot].rearrange("p k c -> p (k c)"),
                                     src.partition_broadcast(32)).then_inc(loaded[c.slot], 16)
                run_chunks(sp, n, R, [0], step)

            @block.gpsimd
            def _(pool):
                bound = pool.to_reg(g.N - 1)

                def step(cs):
                    c = cs[0]
                    pool.wait_ge(ac_["out"], c.count())
                    hold(pool, w)
                    S.scatter(pool, c, out, x34, bound, scattered)
                run_chunks(pool, n, R, [0], step)
                for s in range(R):
                    pool.wait_ge(scattered[s], 64 * turns(n, s, R))

            @block.tensor
            def _(pe):
                mm = nc.tensor.matmul

                def step(cs):
                    p, a, b = cs
                    if b is not None:
                        k = b.slot % 2
                        pe.wait_ge(ve_["num"], b.count())
                        if b.has(1):
                            pe.wait_ge(ve_["z"], b.count(1))
                        for t in range(TPC):
                            ts = slice(t * TILE, (t + 1) * TILE)
                            nc.tensor.transpose(ps_num[:, ts], num[:, k, ts], w["ident"][:, :])
                            last = nc.tensor.transpose(ps_den[:, ts], den[:, k, ts], w["ident"][:, :])
                        last.then_inc(pe_["rows"], 1)
                    if p is not None:
                        pe.wait_ge(S.ready, p.count())
                        if p.has(1):
                            pe.wait_ge(ac_["on"], p.count(1))
                            pe.wait_ge(ve_["top"], p.count(1))
                        spread(nc, ps_on, S.same[:, p.slot, 0, :], w["identb"])
                        spread(nc, ps_new, S.same[:, p.slot, 1, :], w["identb"]).then_inc(pe_["m"], 1)
                        pe.wait_ge(loaded[p.slot], p.landed(96))
                        if p.has(1):
                            pe.wait_ge(ac_["tr"], p.count(1))
                        transpose4(nc, ps_xt, xt[:, p.slot], w["ident"]).then_inc(pe_["tr"], 1)
                    if a is not None:
                        k = a.slot % 2
                        pe.wait_ge(ve_["top"], a.count())
                        if a.has(1):
                            pe.wait_ge(ve_["less"], a.count(1))
                        for t in range(TPC):
                            ts = slice(t * TILE, (t + 1) * TILE)
                            nc.tensor.transpose(ps_score[:, ts], score[:, a.slot, 1, ts], w["ident"][:, :])
                            last = nc.tensor.transpose(ps_top[:, ts], top[:, k, ts], w["ident"][:, :])
                        last.then_inc(pe_["score"], 1)
                        pe.wait_ge(ac_["tr"], a.count())
                        if a.has(1):
                            pe.wait_ge(ve_["z"], a.count(1))
                        add_bias(nc, ps_self, w, "bias2")
                        for t in range(TPC):
                            ts = slice(t * TILE, (t + 1) * TILE)
                            last = mm(ps_self[:, ts], xtT[:, k, ts], w["W2"][:, :], start=False, stop=t == TPC - 1)
                        last.then_inc(pe_["self"], 1)
                run_chunks(pe, n, R, [1, 2, 3], step)

            @block.scalar
            def _(act):
                nc.scalar.preload_act_table_set(ACT_SET)
                ac = nc.scalar.activation

                def step(cs):
                    p, a, b, d = cs
                    if a is not None:
                        act.wait_ge(ve_["diff"], a.count())
                        ac(exps[:, :], exps[:, :], ACT.Exp).then_inc(ac_["exp"], 1)
                    if d is not None:
                        act.wait_ge(ve_["shift"], d.count())
                        for i in range(2):
                            for t in range(TPC):
                                last = ac(out[:, d.slot, t, i * D:(i + 1) * D], y[:, d.slot % 2, t, :], ACT.Identity,
                                          bias=shift[:, i, t:t + 1], scale=rstd[:, i, t:t + 1])
                        last.then_inc(ac_["out"], 1)
                    if b is not None:
                        act.wait_ge(ve_["z"], b.count())
                        ac(low[:, :, :], z[:, :, :], ACT.Relu, scale=-1.0)
                        act.drain()
                        ac(low[:, :, :], low[:, :, :], ACT.Exp, scale=-1.0).then_inc(ac_["elu"], 1)
                    if a is not None:
                        act.wait_ge(ve_["less"], a.count())
                        ac(share[:, a.slot % 2, :], share[:, a.slot % 2, :], ACT.Exp).then_inc(ac_["share"], 1)
                    if p is not None:
                        act.wait_ge(pe_["m"], p.count())
                        if p.has(2):
                            act.wait_ge(ve_["num"], p.count(2))
                        ac(on[:, p.slot % 2, :], ps_on[:, :], ACT.Copy).then_inc(ac_["on"], 1)
                        act.wait_ge(pe_["tr"], p.count())
                        if p.has(2):
                            act.wait_ge(pe_["self"], p.count(2))
                        ac(xtT[:, p.slot % 2, :], ps_xt[:, :], ACT.Copy).then_inc(ac_["tr"], 1)
                    if b is not None:
                        act.wait_ge(ve_["stats"], b.count())
                        ln_twice_rstd(nc, act, mv[:, :, 1], rstd, w).then_inc(ac_["rstd"], 1)
                run_chunks(act, n, R, [1, 2, 3, 4], step)

            @block.vector
            def _(dve):
                v = nc.vector

                def by_head(t):
                    return t.rearrange("p t (h d) -> p (t h) d", h=4)

                def widen(cols):
                    return cols.unsqueeze(2).to_broadcast([128, TPC * 4, 32])

                def step(cs):
                    m, a, b, d = cs
                    dve.drain()
                    if a is not None:
                        k = a.slot % 2
                        first = isinstance(a.i, int) and a.i == 0

                        def carry(t):
                            return None if first else edge_col(S, t[:, 1 - k, :])
                        dve.wait_ge(loaded[a.slot], a.landed(96))
                        dve.wait_ge(pe_["m"], a.count())
                        sc = score[:, a.slot]
                        scan(nc, S, top[:, k, :], ps_new[:, :], sc[:, 2, :], carry(top), ALU.add, ALU.max)\
                            .then_inc(ve_["top"], 1)
                    if d is not None:
                        dve.wait_ge(ac_["rstd"], d.count())
                        if d.has(1):
                            dve.wait_ge(ac_["out"], d.count(1))
                        for i in range(2):
                            last = v.scalar_tensor_tensor(shift[:, i, :], mv[:, :, 0], -1.0, rstd[:, i, :],
                                                          ALU.mult, ALU.mult)
                        last.then_inc(ve_["shift"], 1)
                    dve.drain()
                    if a is not None:
                        v.tensor_tensor(exps[:, :], sc[:, 0, :], top[:, k, :], ALU.subtract).then_inc(ve_["diff"], 1)
                    if b is not None:
                        dve.wait_ge(ac_["share"], b.count())
                        dve.wait_ge(pe_["rows"], b.count())
                        mine = share[:, b.slot % 2, :]
                        v.tensor_tensor(inv[:, :], ps_den[:, 0:CH:32], mine, ALU.add)
                        v.tensor_tensor(by_head(z[:, :, :]), by_head(tiles(ps_self[:, :])), widen(mine), ALU.mult)
                        dve.drain()
                        v.tensor_scalar(inv[:, :], inv[:, :], 1e-12, None, ALU.max)
                        v.tensor_tensor(z[:, :, :], z[:, :, :], tiles(ps_num[:, :]), ALU.add)
                        dve.drain()
                        v.reciprocal(inv[:, :], inv[:, :])
                    dve.drain()
                    if a is not None:
                        dve.wait_ge(ac_["exp"], a.count())
                        dve.wait_ge(ac_["on"], a.count())
                        v.tensor_tensor(weighted[:, :], exps[:, :], proj[:, a.slot, :], ALU.mult)
                    if b is not None:
                        v.tensor_tensor(by_head(z[:, :, :]), by_head(z[:, :, :]), widen(inv[:, :]), ALU.mult)\
                         .then_inc(ve_["z"], 1)
                    if a is not None:
                        scan(nc, S, den[:, k, :], on[:, k, :], exps[:, :], carry(den), ALU.mult, ALU.add)
                    dve.drain()
                    if b is not None:
                        v.scalar_tensor_tensor(y[:, b.slot % 2], z[:, :, :], 0.0, xt[:, b.slot], ALU.max, ALU.add)
                    if a is not None:
                        scan(nc, S, num[:, k, :], on[:, k, :], weighted[:, :], carry(num), ALU.mult, ALU.add)\
                            .then_inc(ve_["num"], 1)
                    if m is not None:
                        S.index(dve, m)
                    if a is not None:
                        dve.wait_ge(pe_["score"], a.count())
                        v.tensor_copy(share[:, k, :], ps_top[:, 0:CH:32])
                        dve.drain()
                        v.tensor_tensor(share[:, k, :], ps_score[:, 0:CH:32], share[:, k, :], ALU.subtract)\
                         .then_inc(ve_["less"], 1)
                    if b is not None:
                        dve.drain()
                        dve.wait_ge(ac_["elu"], b.count())
                        yb = y[:, b.slot % 2]
                        v.scalar_tensor_tensor(yb, low[:, :, :], -1.0, yb, ALU.add, ALU.add)
                        dve.drain()
                        ln_stats(nc, yb, stats, mv)
                        dve.drain()
                        ln_aggregate(nc, stats, mv, TPC).then_inc(ve_["stats"], 1)
                run_chunks(dve, n, R, [0, 2, 3, 4], step)
        end_phase(nc, P)


def build_layer3_scores(nc, g, w, T, A):
    n = g.ED // CH
    x_rows = T.x34.rearrange("n k d -> (n k) d")
    IDX, TURN, SEL, REL, HID, WGT, KVQ, MAX, SAVE = 0, 2, 3, 4, 5, 6, 7, 8, 9
    with ExitStack() as ctx:
        P = Phase(nc, ctx, "l3a")
        S = Slots(P, nc, g, w, T.rec_d, REC, n, False)
        R = S.RING
        xs, xd = P.sb("xs", [128, R, TPC, D]), P.sb("xd", [128, R, TPC, D])
        xsT, xdT = P.sb("xsT", [128, R, CH]), P.sb("xdT", [128, R, CH])
        fresh = P.sb("fresh", [128, R, CH])
        attr = P.sb("attr", [128, R, TPC, 3])
        attrT = P.sb("attrT", [3, CH])
        oh_type = P.sb("oh_type", [64, 2, CH])
        tm, rel = P.sb("tm", [128, 4, CH]), P.sb("rel", [128, 4, CH])
        hT, dw = P.sb("hT", [128, CH]), P.sb("dw", [128, CH])
        msg = P.sb("msg", [128, 2, CH])
        qT, qk = P.sb("qT", [128, CH]), P.sb("qk", [128, 2, CH])
        value = P.sb("value", [128, R, CH])
        kept = P.sb("kept", [128, R, 2, CH])
        ps_type, ps_dt, ps_rel_h, ps_wgt_attr, ps_v, ps_s_xs, ps_k_xd, ps_q_mask = (
            P.ps(k) for k in ("type", "dt", "rel_h", "wgt_attr", "v", "s_xs", "k_xd", "q_mask"))
        pe_ = {k: P.sem("pe_" + k) for k in ("tr", "sel", "rel", "h", "dw", "kvq", "s")}
        ac_ = {k: P.sem("ac_" + k) for k in ("tr", "dt", "h", "dw", "q", "s")}
        ve_ = {k: P.sem("ve_" + k) for k in ("attr", "type", "rel", "msg", "qk", "max")}
        gathered, saved, row_saved = P.sems("gathered", R), P.sems("saved", R), P.sems("row_saved", R)
        with nc.Block() as block:
            @block.sync
            def _(sp):
                def step(cs):
                    load, row, done = cs
                    if load is not None:
                        start = S.start(sp, load)
                        if load.slot_used():
                            sp.wait_ge(row_saved[load.slot], load.landed(16, 1))
                            hold(sp, w)
                            sp.wait_ge(pe_["tr"], load.count(R))
                            hold(sp, w)
                        S.load(sp, load, start)
                    if row is not None:
                        p = S.pos(row)
                        p0 = p * 128 if isinstance(p, int) else sp.snap(p * 128)
                        sp.wait_ge(gathered[row.slot], row.landed(128))
                        hold(sp, w)
                        sp.dma_start(at_rows(T.row3, p0, 128), xd[:, row.slot].rearrange("p t c -> p (t c)"))\
                          .then_inc(row_saved[row.slot], 16)
                    if done is not None:
                        p = S.pos(done)
                        p0 = p * 128 if isinstance(p, int) else sp.snap(p * 128)
                        p1 = p * 8 if isinstance(p, int) else sp.snap(p * 8)
                        sp.wait_ge(ve_["max"], done.count())
                        hold(sp, w)
                        sp.dma_start(at_rows(T.value3, p0, 128), value[:, done.slot, :]).then_inc(saved[done.slot], 16)
                        sp.dma_start(at_rows(T.score3, p1, 8), kept[0:128:16, done.slot].rearrange("p k c -> p (k c)"))\
                          .then_inc(saved[done.slot], 16)
                run_chunks(sp, n, R, [IDX, TURN, SAVE], step)
                for s in range(R):
                    sp.wait_ge(saved[s], 32 * turns(n, s, R))
                    sp.wait_ge(row_saved[s], 16 * turns(n, s, R))

            @block.gpsimd
            def _(pool):
                bound = pool.to_reg(2 * g.N - 1)

                def step(cs):
                    c = cs[0]
                    pool.wait_ge(S.ready, c.count())
                    hold(pool, w)
                    S.gather(pool, c, 0, xs, x_rows, bound, gathered)
                    S.gather(pool, c, 1, xd, x_rows, bound, gathered)
                run_chunks(pool, n, R, [0], step)

            @block.tensor
            def _(pe):
                mm = nc.tensor.matmul

                def step(cs):
                    turn, sel, relc, hid, wgt, kvq, mx = cs
                    if hid is not None:
                        pe.wait_ge(ve_["rel"], hid.count())
                        mm(ps_rel_h[:, :], w["R1a"][:, :], xsT[:, hid.slot, :], start=True, stop=False)
                        mm(ps_rel_h[:, :], w["R1b"][:, :], rel[:, hid.slot % 4, :], start=False, stop=False)
                        mm(ps_rel_h[:, :], w["W1c"][:, :], tm[0:1, hid.slot % 4, :], start=False, stop=True)\
                            .then_inc(pe_["h"], 1)
                    if sel is not None:
                        pe.wait_ge(ac_["tr"], sel.count())
                        if sel.has(1):
                            pe.wait_ge(ve_["type"], sel.count(1))
                            pe.wait_ge(ac_["dt"], sel.count(1))
                        mm(ps_type[0:64, :], w["sel_type"][:, :], attrT[:, :], start=True, stop=True)
                        mm(ps_dt[:, :], w["sel_dt"][:, :], attrT[:, :], start=True, stop=True).then_inc(pe_["sel"], 1)
                    if wgt is not None:
                        pe.wait_ge(ac_["h"], wgt.count())
                        if wgt.has(1):
                            pe.wait_ge(ac_["dw"], wgt.count(1))
                        mm(ps_wgt_attr[:, :], w["R2"][:, :], hT[:, :], start=True, stop=True).then_inc(pe_["dw"], 1)
                    if kvq is not None:
                        pe.wait_ge(ve_["msg"], kvq.count())
                        if kvq.has(1):
                            pe.wait_ge(ve_["qk"], kvq.count(1))
                            pe.wait_ge(ac_["q"], kvq.count(1))
                        mm(ps_q_mask[:, :], w["Wq"][:, :], xdT[:, kvq.slot, :], start=True, stop=True)
                        mm(ps_k_xd[:, :], w["Wk"][:, :], msg[:, kvq.slot % 2, :], start=True, stop=True)
                        mm(ps_v[:, :], w["Wv"][:, :], msg[:, kvq.slot % 2, :], start=True, stop=True)\
                            .then_inc(pe_["kvq"], 1)
                    if relc is not None:
                        pe.wait_ge(ve_["type"], relc.count())
                        if relc.has(1):
                            pe.wait_ge(ac_["h"], relc.count(1))
                        mm(ps_rel_h[:, :], w["rel"][:, :], oh_type[:, relc.slot % 2, :], start=True, stop=True)\
                            .then_inc(pe_["rel"], 1)
                    if mx is not None:
                        pe.wait_ge(ve_["qk"], mx.count())
                        if mx.has(1):
                            pe.wait_ge(ac_["s"], mx.count(1))
                        mm(ps_s_xs[:, :], w["heads16"][:, :], qk[:, mx.slot % 2, :], start=True, stop=True)\
                            .then_inc(pe_["s"], 1)
                    if turn is not None:
                        pe.wait_ge(gathered[turn.slot], turn.landed(128))
                        if turn.has(1):
                            pe.wait_ge(ac_["tr"], turn.count(1))
                        if turn.has(KVQ - TURN):
                            pe.wait_ge(ve_["qk"], turn.count(KVQ - TURN))
                            pe.wait_ge(ac_["q"], turn.count(KVQ - TURN))
                        if turn.has(WGT - TURN):
                            pe.wait_ge(ac_["dw"], turn.count(WGT - TURN))
                        pe.wait_ge(ve_["attr"], turn.count())
                        transpose4(nc, ps_k_xd, xd[:, turn.slot], w["ident"])
                        for t in range(TPC):
                            nc.tensor.transpose(ps_wgt_attr[0:3, t * TILE:(t + 1) * TILE], attr[:, turn.slot, t, :],
                                                w["ident"][:, :])
                        spread(nc, ps_q_mask, S.same[:, turn.slot, 1, :], w["identb"])
                        if turn.has(MAX - TURN):
                            pe.wait_ge(ac_["s"], turn.count(MAX - TURN))
                        transpose4(nc, ps_s_xs, xs[:, turn.slot], w["ident"]).then_inc(pe_["tr"], 1)
                run_chunks(pe, n, R, [TURN, SEL, REL, HID, WGT, KVQ, MAX], step)

            @block.scalar
            def _(act):
                nc.scalar.preload_act_table(ACT.Sigmoid)
                ac = nc.scalar.activation

                def step(cs):
                    turn, sel, hid, wgt, kvq, mx = cs
                    if hid is not None:
                        act.wait_ge(pe_["h"], hid.count())
                        if hid.has(1):
                            act.wait_ge(pe_["dw"], hid.count(1))
                        ac(hT[:, :], ps_rel_h[:, :], ACT.Relu, bias=w["b1"][:, 0:1]).then_inc(ac_["h"], 1)
                    if sel is not None:
                        act.wait_ge(pe_["sel"], sel.count())
                        if sel.has(4):
                            act.wait_ge(pe_["h"], sel.count(4))
                        ac(tm[:, sel.slot % 4, :], ps_dt[:, :], ACT.Sigmoid, scale=w["inv_tc"][:, 0:1])\
                            .then_inc(ac_["dt"], 1)
                    if wgt is not None:
                        act.wait_ge(pe_["dw"], wgt.count())
                        if wgt.has(1):
                            act.wait_ge(ve_["msg"], wgt.count(1))
                        ac(dw[:, :], ps_wgt_attr[:, :], ACT.Sigmoid, bias=w["b2"][:, 0:1]).then_inc(ac_["dw"], 1)
                    if kvq is not None:
                        act.wait_ge(pe_["kvq"], kvq.count())
                        if kvq.has(1):
                            act.wait_ge(ve_["qk"], kvq.count(1))
                        if kvq.slot_used():
                            act.wait_ge(saved[kvq.slot], kvq.landed(32, 1))
                        ac(qT[:, :], ps_q_mask[:, :], ACT.Identity, bias=w["bq"][:, 0:1])
                        ac(value[:, kvq.slot, :], ps_v[:, :], ACT.Identity, bias=w["bias3v"][:, 0:1])\
                            .then_inc(ac_["q"], 1)
                    if mx is not None:
                        act.wait_ge(pe_["s"], mx.count())
                        ac(kept[:, mx.slot, 0, :], ps_s_xs[:, :], ACT.Copy, scale=0.25).then_inc(ac_["s"], 1)
                    if turn is not None:
                        act.wait_ge(pe_["tr"], turn.count())
                        if turn.slot_used():
                            act.wait_ge(ve_["max"], turn.count(R))
                        ac(xdT[:, turn.slot, :], ps_k_xd[:, :], ACT.Copy)
                        ac(attrT[:, :], ps_wgt_attr[0:3, :], ACT.Copy)
                        ac(fresh[:, turn.slot, :], ps_q_mask[:, :], ACT.Copy)
                        ac(xsT[:, turn.slot, :], ps_s_xs[:, :], ACT.Copy).then_inc(ac_["tr"], 1)
                run_chunks(act, n, R, [TURN, SEL, HID, WGT, KVQ, MAX], step)

            @block.vector
            def _(dve):
                v = nc.vector

                def step(cs):
                    m, sel, relc, wgt, kvq, mx = cs
                    dve.drain()
                    if sel is not None:
                        dve.wait_ge(pe_["sel"], sel.count())
                        if sel.has(2):
                            dve.wait_ge(pe_["rel"], sel.count(2))
                        v.tensor_scalar(oh_type[:, sel.slot % 2, :], ps_type[0:64, :], w["iota64"][:, 0:1], None,
                                        ALU.is_equal).then_inc(ve_["type"], 1)
                    if wgt is not None:
                        if wgt.has(2):
                            dve.wait_ge(pe_["kvq"], wgt.count(2))
                        mine = msg[:, wgt.slot % 2, :]
                        v.tensor_tensor(mine, xsT[:, wgt.slot, :], rel[:, wgt.slot % 4, :], ALU.mult)
                        dve.drain()
                        dve.wait_ge(ac_["dw"], wgt.count())
                        v.tensor_tensor(mine, mine, dw[:, :], ALU.mult).then_inc(ve_["msg"], 1)
                    if kvq is not None:
                        dve.wait_ge(ac_["q"], kvq.count())
                        if kvq.has(2):
                            dve.wait_ge(pe_["s"], kvq.count(2))
                        v.scalar_tensor_tensor(qk[:, kvq.slot % 2, :], ps_k_xd[:, :], w["bk"][:, 0:1], qT[:, :],
                                               ALU.add, ALU.mult).then_inc(ve_["qk"], 1)
                    if relc is not None:
                        dve.wait_ge(pe_["rel"], relc.count())
                        dve.wait_ge(ac_["dt"], relc.count())
                        v.tensor_tensor(rel[:, relc.slot % 4, :], ps_rel_h[:, :], tm[:, relc.slot % 4, :], ALU.mult)\
                         .then_inc(ve_["rel"], 1)
                    if mx is not None:
                        dve.wait_ge(ac_["s"], mx.count())
                        first = isinstance(mx.i, int) and mx.i == 0
                        scan(nc, S, kept[:, mx.slot, 1, :], fresh[:, mx.slot, :], kept[:, mx.slot, 0, :],
                             None if first else edge_col(S, kept[:, (mx.slot - 1) % R, 1, :]), ALU.add, ALU.max)\
                            .then_inc(ve_["max"], 1)
                    if m is not None:
                        S.index(dve, m, other_scale=2)
                        v.tensor_copy(attr[:, m.slot, :, 0], S.rec[:, m.slot, :, W_TYPE])
                        v.tensor_copy(attr[:, m.slot, :, 1:3], S.rec[:, m.slot, :, W_NV:W_NV + 2].bitcast(F32))\
                         .then_inc(ve_["attr"], 1)
                run_chunks(dve, n, R, [IDX, SEL, REL, WGT, KVQ, MAX], step)
        end_phase(nc, P)


def build_layer3_sums(nc, g, w, T, A):
    n = g.ED // CH
    x_rows = T.x34.rearrange("n k d -> (n k) d")
    with ExitStack() as ctx:
        P = Phase(nc, ctx, "l3b")
        S = Slots(P, nc, g, w, T.rec_d, REC, n, True)
        R = S.RING
        value = P.sb("value", [128, R, CH])
        xd = P.sb("xd", [128, R, TPC, D])
        score = P.sb("score", [128, R, 2, CH])
        goes_on = P.sb("goes_on", [128, 2, CH])
        fresh = P.sb("fresh", [128, 2, CH])
        top = P.sb("top", [128, 2, CH])
        exps = P.sb("exps", [128, 2, CH])
        den, num = P.sb("den", [128, 2, CH]), P.sb("num", [128, 2, CH])
        weighted, inv = P.sb("weighted", [128, CH]), P.sb("inv", [128, TPC * 8])
        z = P.sb("z", [128, TPC, D])
        y = P.sb("y", [128, TPC, D])
        out = P.sb("out", [128, R, TPC, D])
        stats, mv, rstd = P.sb("stats", [128, 4, 6]), P.sb("mv", [128, 4, 2]), P.sb("rstd", [128, 4])
        ps = [P.ps(f"ps{k}") for k in range(4)]
        pe_ = {k: P.sem("pe_" + k) for k in ("m", "z")}
        ac_ = {k: P.sem("ac_" + k) for k in ("m", "exp", "rstd")}
        ve_ = {k: P.sem("ve_" + k) for k in ("diff", "num", "z", "stats", "out")}
        loaded, scattered = P.sems("loaded", R), P.sems("scattered", R)
        with nc.Block() as block:
            @block.sync
            def _(sp):
                def step(cs):
                    c = cs[0]
                    start = S.start(sp, c)
                    p = S.pos(c)
                    p0 = p * 128 if isinstance(p, int) else sp.snap(p * 128)
                    p1 = p * 8 if isinstance(p, int) else sp.snap(p * 8)
                    if c.slot_used():
                        sp.wait_ge(scattered[c.slot], c.landed(64, 1))
                    hold(sp, w)
                    S.load(sp, c, start)
                    sp.dma_start(value[:, c.slot, :], at_rows(T.value3, p0, 128)).then_inc(loaded[c.slot], 16)
                    sp.dma_start(xd[:, c.slot].rearrange("p t c -> p (t c)"), at_rows(T.row3, p0, 128))\
                      .then_inc(loaded[c.slot], 16)
                    for h in range(8):
                        src = T.score3[p1 + h] if isinstance(p1, int) else T.score3[bass.ds(p1 + h, 1), :].squeeze(0)
                        sp.dma_start(score[16 * h:16 * h + 16, c.slot].rearrange("p k c -> p (k c)"),
                                     src.partition_broadcast(16)).then_inc(loaded[c.slot], 16)
                run_chunks(sp, n, R, [0], step)

            @block.gpsimd
            def _(pool):
                bound = pool.to_reg(2 * g.N - 1)

                def step(cs):
                    c = cs[0]
                    pool.wait_ge(ve_["out"], c.count())
                    hold(pool, w)
                    S.scatter(pool, c, out, x_rows, bound, scattered)
                run_chunks(pool, n, R, [0], step)
                for s in range(R):
                    pool.wait_ge(scattered[s], 64 * turns(n, s, R))

            @block.tensor
            def _(pe):
                def step(cs):
                    a, b = cs
                    if a is not None:
                        pe.wait_ge(S.ready, a.count())
                        if a.has(1):
                            pe.wait_ge(ac_["m"], a.count(1))
                        spread(nc, ps[0], S.same[:, a.slot, 0, :], w["identb"])
                        spread(nc, ps[1], S.same[:, a.slot, 1, :], w["identb"]).then_inc(pe_["m"], 1)
                    if b is not None:
                        pe.wait_ge(ve_["num"], b.count())
                        if b.has(1):
                            pe.wait_ge(ve_["z"], b.count(1))
                        for t in range(TPC):
                            ts = slice(t * TILE, (t + 1) * TILE)
                            nc.tensor.transpose(ps[2][:, ts], num[:, b.slot % 2, ts], w["ident"][:, :])
                            last = nc.tensor.matmul(ps[3][:, 8 * t:8 * t + 8], den[:, b.slot % 2, ts],
                                                    w["pick16"][:, :], start=True, stop=True)
                        last.then_inc(pe_["z"], 1)
                run_chunks(pe, n, R, [0, 1], step)

            @block.scalar
            def _(act):
                nc.scalar.preload_act_table_set(ACT_SET)
                ac = nc.scalar.activation

                def step(cs):
                    a, b = cs
                    if a is not None:
                        k = a.slot % 2
                        act.wait_ge(pe_["m"], a.count())
                        if a.has(2):
                            act.wait_ge(ve_["num"], a.count(2))
                        ac(goes_on[:, k, :], ps[0][:, :], ACT.Copy)
                        ac(fresh[:, k, :], ps[1][:, :], ACT.Copy).then_inc(ac_["m"], 1)
                        act.wait_ge(ve_["diff"], a.count())
                        ac(exps[:, k, :], exps[:, k, :], ACT.Exp).then_inc(ac_["exp"], 1)
                    if b is not None:
                        act.wait_ge(ve_["stats"], b.count())
                        ln_rstd(nc, act, mv[:, :, 1], rstd[:, :], w["eps"]).then_inc(ac_["rstd"], 1)
                run_chunks(act, n, R, [0, 1], step)

            @block.vector
            def _(dve):
                v = nc.vector

                def by_head(t):
                    return t.rearrange("p t (h d) -> p (t h) d", h=8)

                def step(cs):
                    m, a, b = cs
                    dve.drain()
                    if a is not None:
                        k = a.slot % 2
                        first = isinstance(a.i, int) and a.i == 0
                        dve.wait_ge(loaded[a.slot], a.landed(160))
                        dve.wait_ge(ac_["m"], a.count())
                        scan(nc, S, top[:, k, :], fresh[:, k, :], score[:, a.slot, 1, :],
                             None if first else edge_col(S, top[:, 1 - k, :]), ALU.add, ALU.max)
                        dve.drain()
                        v.tensor_tensor(exps[:, k, :], score[:, a.slot, 0, :], top[:, k, :], ALU.subtract)\
                         .then_inc(ve_["diff"], 1)
                    if b is not None:
                        dve.wait_ge(pe_["z"], b.count())
                        v.reciprocal(inv[:, :], ps[3][:, 0:TPC * 8])
                        dve.drain()
                        v.tensor_tensor(by_head(z[:, :, :]), by_head(tiles(ps[2][:, :])),
                                        inv[:, :].unsqueeze(2).to_broadcast([128, TPC * 8, 16]), ALU.mult)\
                         .then_inc(ve_["z"], 1)
                        dve.drain()
                        v.tensor_tensor(y[:, :, :], z[:, :, :], xd[:, b.slot], ALU.add)
                    if a is not None:
                        dve.wait_ge(ac_["exp"], a.count())
                        if a.has(2):
                            dve.wait_ge(pe_["z"], a.count(2))
                        scan(nc, S, den[:, k, :], goes_on[:, k, :], exps[:, k, :],
                             None if first else edge_col(S, den[:, 1 - k, :]), ALU.mult, ALU.add)
                        v.tensor_tensor(weighted[:, :], exps[:, k, :], value[:, a.slot, :], ALU.mult)
                    if b is not None:
                        dve.drain()
                        ln_stats(nc, y, stats, mv)
                        dve.drain()
                        ln_aggregate(nc, stats, mv, TPC).then_inc(ve_["stats"], 1)
                    dve.drain()
                    if a is not None:
                        scan(nc, S, num[:, k, :], goes_on[:, k, :], weighted[:, :],
                             None if first else edge_col(S, num[:, 1 - k, :]), ALU.mult, ALU.add)\
                            .then_inc(ve_["num"], 1)
                    if m is not None:
                        S.index(dve, m, to_scale=2, to_plus=1)
                    if b is not None:
                        dve.wait_ge(ac_["rstd"], b.count())
                        ln_apply(nc, out[:, b.slot], y, mv, rstd).then_inc(ve_["out"], 1)
                run_chunks(dve, n, R, [0, 2, 3], step)
        end_phase(nc, P)


def build_program(nc, A, stage="all"):
    g = Sizes(A["x"].shape[0], A["src"].shape[0])
    T = Tables()
    T.x = A["x"]

    def table(name, shape, dt=F32):
        return A[name] if name in A else nc.dram_tensor(name, shape, dt).ap()
    T.x1, T.x2, T.x1_slot = table("x1", [g.N, D]), table("x2", [g.N, D]), table("x1_slot", [g.ED, D])
    T.x34 = A["x34"]
    T.rec_c = table("rec_c", [g.EC + 2, 2], I32)
    T.rec_d = table("rec_d", [g.ED + 2, REC], I32)
    nd, nC = g.ED // CH, g.EC // CH
    T.proj2, T.row2 = table("proj2", [nC * 128, CH]), table("row2", [nC * 128, TPC * D])
    T.score2 = table("score2", [nC * 4, 3 * CH])
    T.value3, T.row3 = table("value3", [nd * 128, CH]), table("row3", [nd * 128, TPC * D])
    T.score3 = table("score3", [nd * 8, 2 * CH])
    with ExitStack() as ctx:
        P = Phase(nc, ctx, "w")
        w = build_constants(nc, P, g, A)
        order = ["iso", "sort", "l0", "l1", "l2a", "l2b", "l3a", "l3b"]
        last = len(order) if stage == "all" else order.index(stage) + 1
        for s in order[:last]:
            {"iso": lambda: build_isolated(nc, g, w, T), "sort": lambda: build_sort(nc, g, w, T, A),
             "l0": lambda: build_layer0(nc, g, w, T, A), "l1": lambda: build_layer1(nc, g, w, T, A),
             "l2a": lambda: build_layer2_scores(nc, g, w, T, A), "l2b": lambda: build_layer2_sums(nc, g, w, T, A),
             "l3a": lambda: build_layer3_scores(nc, g, w, T, A), "l3b": lambda: build_layer3_sums(nc, g, w, T, A)}[s]()


_INS = ["x", "src", "dst", "edge_attr_10", "edge_attr_4", "edge_type_64", "edge_weight", "node_vec",
        "L0_gnn_W_si_0e", "L0_gnn_W_si_1o", "L0_gnn_W_l1_0e", "L0_gnn_W_l1_1o", "L0_gnn_W_fc1", "L0_gnn_W_fc2",
        "L0_gnn_W_l2_0e", "L0_gnn_W_l2_1o", "L1_gnn_W", "L1_gnn_b", "L2_gnn_W", "L2_gnn_attn_src",
        "L2_gnn_attn_dst", "L2_gnn_bias", "L3_gnn_rel_table", "L3_gnn_Wq", "L3_gnn_bq", "L3_gnn_Wk", "L3_gnn_bk",
        "L3_gnn_Wv", "L3_gnn_bv", "L3_gnn_W1", "L3_gnn_b1", "L3_gnn_W2", "L3_gnn_b2", "L3_gnn_time_coeff"]


def kernel(**inputs):
    import numpy as np
    import concourse.bacc as bacc
    from concourse import mybir as _mybir
    from concourse.bass_utils import run_bass_kernel_spmd

    nc = bacc.Bacc("TRN2", target_bir_lowering=False, num_devices=1)
    arrays, A = {}, {}
    for name in _INS:
        a = np.atleast_1d(np.ascontiguousarray(inputs[name]))
        arrays[name] = a
        A[name] = nc.dram_tensor(name, a.shape, _mybir.dt.from_np(a.dtype), kind="ExternalInput").ap()
    n, d = inputs["x"].shape
    A["x34"] = nc.dram_tensor("x34", [n, 2, d], _mybir.dt.float32, kind="ExternalOutput").ap()
    build_program(nc, A)
    result = run_bass_kernel_spmd(nc, [arrays], core_ids=[0])
    return result.results[0]["x34"].reshape(n, 2, d)[:, 1, :]
```

```python
import concourse.bass as bass
from concourse import mybir
from contextlib import ExitStack

F32 = mybir.dt.float32
I32 = mybir.dt.int32
BF16 = mybir.dt.bfloat16
F16 = mybir.dt.float16
ALU = mybir.AluOpType
ACT = mybir.ActivationFunctionType
AX_X = mybir.AxisListType.X

D = 128
MUL = 32
TILE = 128
TPC = 4
CH = TILE * TPC
LN_EPS = 1e-5
FAR = 1 << 20
ACT_SET = "natural_log_exp_and_others"
NEG = -1e30

W_DST, W_SRC, W_TYPE, W_NV, W_EW, W_SH, W_LEN = 0, 1, 2, 3, 4, 5, 9
N_SH, N_LEN = 4, 10
N_ATTR = N_SH + N_LEN
REC = 20


class Chunk:

    def __init__(self, i, slot, turn, ring):
        self.i, self.slot, self.turn, self.ring = i, slot, turn, ring

    def has(self, back):
        return not isinstance(self.i, int) or self.i >= back

    def count(self, back=0):
        return self.i + (1 - back)

    def slot_used(self):
        return not isinstance(self.turn, int) or self.turn > 0

    def landed(self, amount, back=0):
        return (self.turn + (1 - back)) * amount


def run_chunks(eng, n, ring, lags, body, base=0):
    deep = max(lags)
    before = base // ring

    def at(i):
        return [Chunk(i - k + base, (i - k) % ring, (i - k) // ring + before, ring) if 0 <= i - k < n else None
                for k in lags]

    lo = -(-(deep + ring) // ring)
    hi = max(lo, (n - 1) // ring)
    for i in range(min(lo * ring, n + deep)):
        body(at(i))
    if hi > lo:
        with eng.Fori(lo, hi) as turn:
            for p in range(ring):
                body([Chunk(turn * ring + (p - k + base), (p - k) % ring, turn + ((p - k) // ring + before), ring)
                      for k in lags])
    for i in range(hi * ring, n + deep):
        body(at(i))


def hold(eng, w):
    eng.sem_inc(w["held"], 1)


class Phase:

    def __init__(self, nc, ctx, tag):
        self.nc, self.ctx, self.tag, self.taken = nc, ctx, tag, []

    def sb(self, name, shape, dt=F32):
        return self.ctx.enter_context(self.nc.sbuf_tensor(f"{self.tag}_{name}", shape, dt))

    def ps(self, name, shape=(128, 512), dt=F32):
        return self.ctx.enter_context(self.nc.psum_tensor(f"{self.tag}_{name}", list(shape), dt))

    def sem(self, name):
        s = self.nc.alloc_semaphore(f"{self.tag}_{name}")
        self.taken.append(s)
        return s

    def sems(self, name, n):
        return [self.sem(f"{name}{k}") for k in range(n)]


def end_phase(nc, P):
    nc.all_engine_barrier()
    nc.clear_and_free_semaphores(P.taken)
    nc.all_engine_barrier()


def tiles(t):
    return t.rearrange("p (t c) -> p t c", t=TPC)



def ln_stats(nc, y, stats, mv, tiles_of=range(TPC), at=0):
    for t in tiles_of:
        nc.vector.bn_stats(stats[:, at + t, :], y[:, t, :])


def ln_aggregate(nc, stats, mv, n):
    last = None
    for t in range(n):
        last = nc.vector.bn_aggr(mv[:, t, :], stats[:, t, :])
    return last


def ln_rstd(nc, act, mv, rstd, eps):
    nc.scalar.activation(rstd, mv, ACT.Ln, bias=eps[:, 0:1])
    act.drain()
    return nc.scalar.activation(rstd, rstd, ACT.Exp, scale=-0.5)


def ln_twice_rstd(nc, act, var, rstd, w):
    nc.scalar.activation(rstd[:, 0, :], var, ACT.Ln, bias=w["eps"][:, 0:1])
    nc.scalar.activation(rstd[:, 1, :], var, ACT.Ln, bias=w["eps2"][:, 0:1], scale=1.0 + LN_EPS)
    act.drain()
    return nc.scalar.activation(rstd[:, :, :], rstd[:, :, :], ACT.Exp, scale=-0.5)


def ln_apply(nc, out, y, mv, rstd):
    last = None
    for t in range(TPC):
        last = nc.vector.tensor_scalar(out[:, t, :], y[:, t, :], mv[:, t, 0:1], rstd[:, t:t + 1],
                                       ALU.subtract, ALU.mult)
    return last


def transpose4(nc, out, rows, ident):
    last = None
    for t in range(TPC):
        last = nc.tensor.transpose(out[:, t * TILE:(t + 1) * TILE], rows[:, t, :], ident[:, :])
    return last


def spread(nc, out, cols, ident):
    last = None
    for t in range(TPC):
        last = nc.tensor.matmul(out[:, t * TILE:(t + 1) * TILE], cols[:, t:t + 1].to_broadcast([128, 128]),
                                ident[:, :], start=True, stop=True)
    return last


def add_bias(nc, out, w, name):
    return nc.tensor.matmul(out[:, :], w["ones3"][:, :], w[name][:, :], start=True, stop=False)


def build_constants(nc, P, g, A):
    w = {}
    for n in ("ident", "Wsi", "WsiI", "W1a", "W1b", "W1sum", "W2", "Asrc", "Adst", "Aself", "g1", "g2",
              "o1", "o2", "o3", "R1a", "R1b", "R2", "Wq", "Wk", "Wv", "heads16", "heads32"):
        w[n] = P.sb(n, [128, 128])
    w["held"] = P.sem("held")
    w["identb"] = P.sb("identb", [128, 128], BF16)
    w["eps"], w["eps2"] = P.sb("eps", [128, 1]), P.sb("eps2", [128, 1])
    w["ones3"] = P.sb("ones3", [3, 128], BF16)
    w["bias1"], w["bias2"] = P.sb("bias1", [3, CH], BF16), P.sb("bias2", [3, CH], BF16)
    w["bias2c"] = P.sb("bias2c", [128, 1])
    w["bias3v"] = P.sb("bias3v", [128, 1])
    w["bq"] = P.sb("bq", [128, 1])
    w["bk"] = P.sb("bk", [128, 1])
    w["b1"] = P.sb("b1", [128, 1])
    w["b2"] = P.sb("b2", [128, 1])
    w["inv_tc"] = P.sb("inv_tc", [128, 1])
    w["fc1"] = P.sb("fc1", [N_ATTR, 100])
    for n in ("h1", "h2", "h3"):
        w[n] = P.sb(n, [100, 128])
    w["sel_sh"] = P.sb("sel_sh", [N_ATTR, 128])
    w["sel_sh0"] = P.sb("sel_sh0", [N_ATTR, 128])
    w["rel"] = P.sb("rel", [64, 128])
    w["W1c"] = P.sb("W1c", [1, 128])
    w["sel_type"] = P.sb("sel_type", [3, 64])
    w["sel_dt"] = P.sb("sel_dt", [3, 128])
    w["iota64"] = P.sb("iota64", [64, 1])
    w["pick16"] = P.sb("pick16", [128, 8])
    with ExitStack() as ctx:
        Q = Phase(nc, ctx, "prep")
        l1w = Q.sb("l1w", [128, 256])
        acol = Q.sb("acol", [128, 2])
        asel = Q.sb("asel", [128, 2, 128])
        w2t = Q.sb("w2t", [128, 128])
        r2c = Q.sb("r2c", [128, 1])
        bias = Q.sb("bias", [3, 2, TPC, D])
        parts = Q.sb("parts", [3, 3, 2, TPC, D], BF16)
        tcn = Q.sb("tcn", [128, 1])
        ones = Q.sb("ones", [128, 128])
        pt = Q.ps("pt")
        pa = Q.ps("pa")
        zeroed, made, loaded, transposed, turned, combined = (
            Q.sem(n) for n in ("zeroed", "made", "loaded", "transposed", "turned", "combined"))
        n_loads = [0]
        zero_first = ("Wsi", "g1", "g2", "o1", "o2", "o3", "fc1", "h1", "h2", "h3")
        with nc.Block() as block:
            @block.vector
            def _(dve):
                for n in zero_first:
                    last = nc.vector.memset(w[n][:, :], 0.0)
                nc.vector.memset(w["eps"][:, :], LN_EPS)
                nc.vector.memset(w["eps2"][:, :], LN_EPS ** 2)
                last = nc.vector.memset(w["ones3"][:, :], 1.0)
                last.then_inc(zeroed, 1)

            @block.sync
            def _(sp):
                sp.wait_ge(zeroed, 1)

                def load(dst, src):
                    sp.dma_start(dst, src, allow_slow_non_contiguous=True).then_inc(loaded, 16)
                    n_loads[0] += 1

                def col(v):
                    return v.rearrange("(p a) -> p a", a=1)

                def row(v):
                    return v.rearrange("(a n) -> a n", a=1)

                def vec(mat, m, cols_from=MUL):
                    return mat[MUL + m:128:3, cols_from + m:128:3]

                load(w["Wsi"][0:MUL, 0:MUL], A["L0_gnn_W_si_0e"])
                load(w["g1"][0:MUL, 0:MUL], A["L0_gnn_W_l1_0e"])
                load(w["o1"][0:MUL, 0:MUL], A["L0_gnn_W_l2_0e"][0:MUL, :])
                load(w["h1"][:, 0:MUL], A["L0_gnn_W_fc2"][:, 0:MUL])
                for m in range(3):
                    load(vec(w["Wsi"], m), A["L0_gnn_W_si_1o"])
                    load(w["g1"][0:MUL, MUL + m:128:3], A["L0_gnn_W_l1_0e"])
                    load(vec(w["g2"], m), A["L0_gnn_W_l1_1o"])
                    load(w["o3"][MUL + m:128:3, 0:MUL], A["L0_gnn_W_l2_0e"][MUL:2 * MUL, :])
                    load(vec(w["o1"], m), A["L0_gnn_W_l2_1o"][0:MUL, :])
                    load(vec(w["o2"], m), A["L0_gnn_W_l2_1o"][MUL:2 * MUL, :])
                    for k in range(3):
                        load(w[f"h{k + 1}"][:, MUL + m:128:3], A["L0_gnn_W_fc2"][:, (k + 1) * MUL:(k + 2) * MUL])
                load(w["fc1"][N_SH:N_ATTR, :], A["L0_gnn_W_fc1"])
                load(l1w[:, :], A["L1_gnn_W"])
                for t in range(TPC):
                    load(bias[:, 0, t, :], A["L1_gnn_b"].partition_broadcast(3))
                    load(bias[:, 1, t, :], A["L2_gnn_bias"].partition_broadcast(3))
                load(w["bias2c"][:, :], col(A["L2_gnn_bias"]))
                load(w["W2"][:, :], A["L2_gnn_W"])
                load(acol[:, 0:1], A["L2_gnn_attn_src"].rearrange("h (d a) -> (h d) a", a=1))
                load(acol[:, 1:2], A["L2_gnn_attn_dst"].rearrange("h (d a) -> (h d) a", a=1))
                load(w["rel"][:, :], A["L3_gnn_rel_table"])
                load(w["Wq"][:, :], A["L3_gnn_Wq"])
                load(w["Wk"][:, :], A["L3_gnn_Wk"])
                load(w["Wv"][:, :], A["L3_gnn_Wv"])
                load(w["bq"][:, :], col(A["L3_gnn_bq"]))
                load(w["bk"][:, :], col(A["L3_gnn_bk"]))
                load(w["bias3v"][:, :], col(A["L3_gnn_bv"]))
                load(w["b1"][:, :], col(A["L3_gnn_b1"]))
                load(w["R1a"][:, :], A["L3_gnn_W1"][0:128, :])
                load(w["R1b"][:, :], A["L3_gnn_W1"][128:256, :])
                load(w["W1c"][:, :], A["L3_gnn_W1"][256:257, :])
                load(r2c[:, :], A["L3_gnn_W2"])
                load(w["b2"][:, :], A["L3_gnn_b2"].partition_broadcast(128))
                load(tcn[:, :], A["L3_gnn_time_coeff"].partition_broadcast(128))

            @block.gpsimd
            def _(pool):
                for n in ("ident", "identb", "heads16", "heads32", "sel_sh", "sel_sh0", "sel_type", "pick16"):
                    nc.gpsimd.memset(w[n][:, :], 1.0)
                nc.gpsimd.memset(ones[:, :], 1.0)
                nc.gpsimd.memset(w["sel_dt"][:, :], 0.0)
                pool.drain()

                def keep(t, pattern, base, cm, op):
                    return nc.gpsimd.affine_select(out=t, in_=t, compare_op=op, fill=0.0, base=base,
                                                   pattern=pattern, channel_multiplier=cm)

                for n in ("ident", "identb"):
                    keep(w[n][:, :], [[-1, 128]], 0, 1, ALU.is_equal)
                for n, size in (("heads16", 16), ("heads32", 32)):
                    v = w[n][:, :].rearrange("p (h d) -> p h d", d=size)
                    keep(v, [[-size, 128 // size], [0, size]], 0, 1, ALU.is_ge)
                    pool.drain()
                    keep(v, [[size, 128 // size], [0, size]], size - 1, -1, ALU.is_ge)
                keep(w["sel_sh"][:, 0:MUL], [[0, MUL]], 0, 1, ALU.is_equal)
                keep(w["sel_sh"][:, MUL:128].rearrange("p (u m) -> p u m", m=3), [[0, MUL], [-1, 3]], -1, 1,
                     ALU.is_equal)
                keep(w["pick16"][:, :], [[-16, 8]], 0, 1, ALU.is_equal)
                keep(w["sel_sh0"][:, :], [[0, 128]], 0, 1, ALU.is_equal)
                keep(w["sel_type"][:, :], [[0, 64]], 0, 1, ALU.is_equal)
                s = w["sel_dt"]
                nc.gpsimd.affine_select(out=s[:, :], in_=s[:, :], compare_op=ALU.not_equal, fill=1.0, base=-1,
                                        pattern=[[0, 128]], channel_multiplier=1)
                pool.drain()
                nc.gpsimd.affine_select(out=s[:, :], in_=s[:, :], compare_op=ALU.not_equal, fill=-1.0, base=-2,
                                        pattern=[[0, 128]], channel_multiplier=1)
                nc.gpsimd.iota(w["iota64"][:, :], pattern=[[0, 1]], base=0, channel_multiplier=1,
                               allow_small_or_imprecise_dtypes=True)
                pool.drain()
                nc.gpsimd.memset(ones[:, 0:1], 1.0).then_inc(made, 1)

            @block.tensor
            def _(pe):
                pe.wait_ge(made, 1)
                pe.wait_ge(loaded, 16 * n_loads[0])
                nc.tensor.transpose(pt[:, 0:128], l1w[:, 0:128], w["ident"][:, :])
                nc.tensor.transpose(pt[:, 128:256], l1w[:, 128:256], w["ident"][:, :])
                nc.tensor.transpose(pt[:, 256:384], w["W2"][:, :], w["ident"][:, :]).then_inc(transposed, 1)
                pe.wait_ge(turned, 1)
                nc.tensor.matmul(pa[:, 0:128], w2t[:, :], asel[:, 0, :], start=True, stop=True)
                nc.tensor.matmul(pa[:, 128:256], w2t[:, :], asel[:, 1, :], start=True, stop=True).then_inc(combined, 1)

            @block.vector
            def _(dve):
                dve.wait_ge(made, 1)
                dve.wait_ge(loaded, 16 * n_loads[0])
                dve.wait_ge(transposed, 1)
                v = nc.vector
                v.tensor_copy(w["W1a"][:, :], pt[:, 0:128])
                v.tensor_copy(w["W1b"][:, :], pt[:, 128:256])
                v.tensor_copy(w2t[:, :], pt[:, 256:384])
                for k in range(2):
                    v.tensor_scalar(asel[:, k, :], w["heads32"][:, :], acol[:, k:k + 1], None, ALU.mult)
                for k in range(3):
                    v.tensor_copy(parts[:, k], bias[:, :])
                    dve.drain()
                    if k < 2:
                        v.tensor_tensor(bias[:, :], bias[:, :], parts[:, k], ALU.subtract)
                        dve.drain()
                for i, n in enumerate(("bias1", "bias2")):
                    for k in range(3):
                        part = parts[:, k, i].rearrange("p t c -> p (t c)")
                        if k == 0:
                            v.tensor_scalar(w[n][:, :], part, w["ident"][0:3, 0:1], None, ALU.mult)
                        else:
                            v.scalar_tensor_tensor(w[n][:, :], part, w["ident"][0:3, k:k + 1], w[n][:, :],
                                                   ALU.mult, ALU.add)
                        dve.drain()
                v.tensor_scalar(w["R2"][:, :], ones[:, :], r2c[:, 0:1], None, ALU.mult)
                for n, s in (("Wsi", MUL ** -0.5), ("g1", MUL ** -0.5), ("g2", MUL ** -0.5),
                             ("o1", 0.5 / 4 / 8), ("o2", 0.5 / 4 / 8), ("o3", 0.5 / 4 / 8),
                             ("h1", 0.1), ("h2", 0.1), ("h3", 0.1), ("fc1", N_LEN ** -0.5)):
                    v.tensor_scalar(w[n][:, :], w[n][:, :], s, None, ALU.mult)
                v.tensor_scalar(w["inv_tc"][:, :], tcn[:, :], -1.0, None, ALU.mult)
                dve.drain()
                v.tensor_tensor(w["W1sum"][:, :], w["W1a"][:, :], w["W1b"][:, :], ALU.add).then_inc(turned, 1)
                v.tensor_tensor(w["WsiI"][:, :], w["Wsi"][:, :], w["ident"][:, :], ALU.add)
                v.tensor_scalar(w["o3"][:, 0:MUL], w["o3"][:, 0:MUL], 3.0 ** -0.5, None, ALU.mult)
                v.tensor_tensor(w["inv_tc"][:, :], w["inv_tc"][:, :], tcn[:, :], ALU.max)
                dve.drain()
                v.tensor_scalar(w["inv_tc"][:, :], w["inv_tc"][:, :], 1e-9, None, ALU.add)
                dve.drain()
                v.reciprocal(w["inv_tc"][:, :], w["inv_tc"][:, :])
                dve.wait_ge(combined, 1)
                v.tensor_copy(w["Asrc"][:, :], pa[:, 0:128])
                v.tensor_copy(w["Adst"][:, :], pa[:, 128:256])
                dve.drain()
                v.tensor_tensor(w["Aself"][:, :], w["Asrc"][:, :], w["Adst"][:, :], ALU.add)
        end_phase(nc, Q)
    return w


def build_isolated(nc, g, w, T):
    N = g.N
    n = -(-N // CH)
    with ExitStack() as ctx:
        P = Phase(nc, ctx, "iso")
        R = 4
        x_in = P.sb("x_in", [128, R, TPC, D])
        normed = P.sb("normed", [128, 2, R, TPC, D])
        xT = P.sb("xT", [128, 2, 2, CH])
        y = P.sb("y", [128, 2, TPC, D])
        stats = P.sb("stats", [128, 8, 6])
        mv = P.sb("mv", [128, 8, 2])
        rstd, shift = P.sb("rstd", [128, 8]), P.sb("shift", [128, 8])
        psT = [P.ps(f"psT{k}") for k in range(2)]
        psZ = [[P.ps("psZ00"), P.ps("psZ01")], [P.ps("psZ10"), P.ps("psZ11")]]
        x_loaded = P.sems("x_loaded", R)
        stored = [P.sems(f"stored{k}_", R) for k in range(2)]
        transposed, xT_copied, z_done = (P.sems(s, 2) for s in ("transposed", "xT_copied", "z_done"))
        y_done, stats_done, rstd_done, shift_done = (
            P.sem(s) for s in ("y_done", "stats_done", "rstd_done", "shift_done"))
        applied = P.sems("applied", 2)
        T_LAGS, A_LAGS = [0, 3], [1, 4]
        B_LAGS = [k + 1 for k in A_LAGS]
        weights = [w["WsiI"], w["W1sum"]]
        targets = [T.x1, T.x2]

        def rows(table, c):
            start = N - CH if isinstance(c.i, int) and c.i == n - 1 else c.i * CH
            part = table[start:start + CH, :] if isinstance(start, int) else table[bass.ds(start, CH), :]
            return part.rearrange("(p t) c -> p t c", t=TPC)

        def source(l, c):
            return x_in[:, c.slot] if l == 0 else normed[:, l - 1, c.slot]

        def present(cs, lags):
            ls = [l for l in range(len(lags)) if cs[l] is not None]
            if not ls:
                return None
            return ls[0], ls[-1] + 1, cs[ls[0]].i + lags[ls[0]]

        def before_norm(l, c):
            return tiles(psZ[0][c.slot % 2][:, :]) if l == 0 else y[:, c.slot % 2]

        with nc.Block() as block:
            @block.sync
            def _(sp):
                def step(cs):
                    c = cs[0]
                    if c is not None:
                        if c.has(R):
                            sp.wait_ge(transposed[0], c.count(R))
                        sp.dma_start(x_in[:, c.slot], rows(T.x, c)).then_inc(x_loaded[c.slot], 16)
                    for l in range(2):
                        c = cs[l + 1]
                        if c is not None:
                            sp.wait_ge(applied[l], c.count())
                            if isinstance(c.i, int) and c.i == n - 1:
                                sp.wait_ge(stored[l][(n - 2) % R], 16 * turns(n - 1, (n - 2) % R, R))
                            sp.dma_start(rows(targets[l], c), normed[:, l, c.slot]).then_inc(stored[l][c.slot], 16)
                run_chunks(sp, n, R, [0] + [k + 1 for k in B_LAGS], step)
                for l in range(2):
                    for s in range(R):
                        sp.wait_ge(stored[l][s], 16 * turns(n, s, R))

            @block.tensor
            def _(pe):
                def step(cs):
                    for l in range(2):
                        c = cs[l + 2]
                        if c is None:
                            continue
                        pe.wait_ge(xT_copied[l], c.count())
                        if c.has(2):
                            pe.wait_ge(applied[0] if l == 0 else y_done, c.count(2))
                        z = psZ[l][c.slot % 2]
                        if l > 0:
                            add_bias(nc, z, w, f"bias{l}")
                        for t in range(TPC):
                            last = nc.tensor.matmul(z[:, t * D:(t + 1) * D], xT[:, l, c.slot % 2, t * D:(t + 1) * D],
                                                    weights[l][:, :], start=l == 0, stop=l == 0 or t == TPC - 1)
                        last.then_inc(z_done[l], 1)
                    for l in range(2):
                        c = cs[l]
                        if c is None:
                            continue
                        if l == 0:
                            pe.wait_ge(x_loaded[c.slot], c.landed(16))
                        else:
                            pe.wait_ge(applied[l - 1], c.count())
                        if c.has(1):
                            pe.wait_ge(xT_copied[l], c.count(1))
                        transpose4(nc, psT[l], source(l, c), w["ident"]).then_inc(transposed[l], 1)
                run_chunks(pe, n, R, T_LAGS + A_LAGS, step)

            @block.scalar
            def _(act):
                nc.scalar.preload_act_table_set(ACT_SET)
                def step(cs):
                    now = present(cs[4:], B_LAGS)
                    if now is not None:
                        lo, hi, t = now
                        act.wait_ge(shift_done, t - 1)
                        for l in range(lo, hi):
                            c = cs[4 + l]
                            if c.slot_used():
                                act.wait_ge(stored[l][c.slot], c.landed(16, 1))
                            for k in range(TPC):
                                j = 4 * l + k
                                last = nc.scalar.activation(normed[:, l, c.slot, k, :], before_norm(l, c)[:, k, :],
                                                            ACT.Identity, bias=shift[:, j:j + 1], scale=rstd[:, j:j + 1])
                            last.then_inc(applied[l], 1)
                    for l in range(2):
                        c = cs[l]
                        if c is None:
                            continue
                        act.wait_ge(transposed[l], c.count())
                        if c.has(2):
                            act.wait_ge(z_done[l], c.count(2))
                        nc.scalar.activation(xT[:, l, c.slot % 2, :], psT[l][:, :], ACT.Copy).then_inc(xT_copied[l], 1)
                    now = present(cs[2:4], A_LAGS)
                    if now is not None:
                        lo, hi, t = now
                        act.drain()
                        act.wait_ge(stats_done, t)
                        ln_rstd(nc, act, mv[:, lo * 4:hi * 4, 1], rstd[:, lo * 4:hi * 4], w["eps"]).then_inc(rstd_done, 1)
                run_chunks(act, n, R, T_LAGS + A_LAGS + B_LAGS, step)

            @block.vector
            def _(dve):
                def step(cs):
                    a, b = cs[0:2], cs[2:4]
                    now_b = present(b, B_LAGS)
                    if now_b is not None:
                        lo, hi, t = now_b
                        dve.wait_ge(rstd_done, t - 1)
                        for l in range(2):
                            if b[l] is not None and b[l].has(1):
                                dve.wait_ge(applied[l], b[l].count(1))
                        nc.vector.scalar_tensor_tensor(shift[:, lo * 4:hi * 4], mv[:, lo * 4:hi * 4, 0], -1.0,
                                                       rstd[:, lo * 4:hi * 4], ALU.mult, ALU.mult).then_inc(shift_done, 1)
                    now_a = present(a, A_LAGS)
                    if now_a is None:
                        return
                    lo, hi, t = now_a
                    if a[1] is not None:
                        c = a[1]
                        dve.wait_ge(z_done[1], c.count())
                        nc.vector.scalar_tensor_tensor(y[:, c.slot % 2], tiles(psZ[1][c.slot % 2][:, :]), 0.0,
                                                       source(1, c), ALU.max, ALU.add).then_inc(y_done, 1)
                    if a[0] is not None:
                        dve.wait_ge(z_done[0], a[0].count())
                        ln_stats(nc, before_norm(0, a[0]), stats, mv)
                    dve.drain()
                    if a[1] is not None:
                        ln_stats(nc, before_norm(1, a[1]), stats, mv, at=4)
                        dve.drain()
                    for k in range(4 * lo, 4 * hi):
                        last = nc.vector.bn_aggr(mv[:, k, :], stats[:, k, :])
                    last.then_inc(stats_done, 1)
                    dve.drain()
                run_chunks(dve, n, R, A_LAGS + B_LAGS, step)
        end_phase(nc, P)


class Sizes:
    def __init__(self, N, E):
        self.N, self.E = N, E
        self.NQ = -(-N // 128)
        self.LE = 125
        self.GT = 4
        self.TT = E // self.LE
        assert E % self.LE == 0 and self.TT % (2 * self.GT) == 0
        self.ED = -(-E // CH) * CH
        self.EC = -(-2 * E // CH) * CH


class Tables:
    pass


def build_sort(nc, g, w, T, A):
    N, E, NQ, LE, GT, TT = g.N, g.E, g.NQ, g.LE, g.GT, g.TT
    GE = GT * LE
    RING = 2 * GT
    with ExitStack() as ctx:
        P = Phase(nc, ctx, "sort")
        ends = P.sb("ends", [LE, 2, TT], I32)
        kind = P.sb("kind", [LE, TT], I32)
        ew = P.sb("ew", [LE, TT])
        part = P.sb("part", [LE, 2 * TT], I32)
        key = P.sb("key", [LE, 2 * TT])
        lane = P.sb("lane", [LE, 2 * TT])
        quot = P.sb("quot", [LE, 2 * TT])
        iota_q = P.sb("iota_q", [128, NQ], F16)
        iota_l = P.sb("iota_l", [128, 128], F16)
        iota_p = P.sb("iota_p", [128, 1])
        earlier = P.sb("earlier", [LE, LE])
        below = P.sb("below", [128, 128])
        zeros = P.sb("zeros", [128, NQ])
        hist = P.sb("hist", [128, 2, NQ])
        base = P.sb("base", [128, 2, NQ])
        nv_tab = P.sb("nv_tab", [128, NQ])
        row_sum = P.sb("row_sum", [128, 2])
        row_pre = P.sb("row_pre", [128, 2])
        running = P.sb("running", [128, 2, NQ])
        oh_lane = P.sb("oh_lane", [LE, 4, 128], BF16)
        oh_quot = P.sb("oh_quot", [LE, 4, NQ], BF16)
        key_row = P.sb("key_row", [128, 2, GE], I32)
        lane_row = P.sb("lane_row", [128, GE], I32)
        oh_row = P.sb("oh_row", [128, 2, GE])
        junk = P.sb("junk", [LE, 3, NQ])
        junk2 = P.sb("junk2", [LE, LE])
        rank = P.sb("rank", [LE, 2])
        found = P.sb("found", [LE, 3, GT])
        at_c = P.sb("at_c", [LE, 2, GT], I32)
        at_d = P.sb("at_d", [LE, 2, GT], I32)
        out_c = P.sb("out_c", [LE, 2, GT, 2], I32)
        out_d = P.sb("out_d", [LE, 2, GT, REC], I32)
        pad = P.sb("pad", [128, REC], I32)
        ps_look = [[P.ps(f"look{k}{s}") for s in range(2)] for k in range(3)]
        ps_run = P.ps("run")
        loaded, made, cols_ready = P.sem("loaded"), P.sem("made"), P.sem("cols_ready")
        oh1, hist_done = P.sem("oh1"), P.sem("hist_done")
        sums_ready, pre_done, base_ready = P.sem("sums_ready"), P.sem("pre_done"), P.sem("base_ready")
        oh_ready, updated, run_copied, looked, selected = (
            P.sem(s) for s in ("oh_ready", "updated", "run_copied", "looked", "selected"))
        row_ready, row_used, rec_ready = P.sem("row_ready"), P.sem("row_used"), P.sem("rec_ready")
        keys_landed, attrs_landed, scattered = (P.sems(s, 2) for s in ("keys_landed", "attrs_landed", "scattered"))
        padded = P.sem("padded")
        A_keys = [A["dst"], A["src"]]
        full_q = N // 128

        def col(t, c):
            return t[:, c.i:c.i + 1] if isinstance(c.i, int) else t[:, bass.ds(c.i, 1)]

        def group(c):
            s = c.slot // GT
            return Chunk(c.turn * 2 + s, s, c.turn, 2)

        def seg(t, start, size):
            return t[start:start + size] if isinstance(start, int) else t[bass.ds(start, size)]

        with nc.Block() as block:
            @block.sync
            def _(sp):
                with nc.allow_non_contiguous_dma(reason="one word per edge"):
                    for k in range(2):
                        sp.dma_start(ends[:, k, :], A_keys[k].rearrange("(j p) -> p j", p=LE)).then_inc(loaded, 16)
                    sp.dma_start(kind[:, :], A["edge_type_64"].rearrange("(j p) -> p j", p=LE)).then_inc(loaded, 16)
                    sp.dma_start(ew[:, :], A["edge_weight"].rearrange("(j p) -> p j", p=LE)).then_inc(loaded, 16)
                    sp.wait_ge(made, 1)
                    sp.dma_start(nv_tab[:, 0:full_q],
                                 A["node_vec"][0:128 * full_q].rearrange("(q p) -> p q", p=128)).then_inc(loaded, 16)
                    if N % 128:
                        sp.dma_start(nv_tab[0:N % 128, full_q:NQ],
                                     A["node_vec"][128 * full_q:N].rearrange("(p q) -> p q", q=1)).then_inc(loaded, 16)
                n_pads = 0
                for table, width, used, slots in ((T.rec_c, 2, 2 * E, g.EC), (T.rec_d, REC, E, g.ED)):
                    sp.dma_start(table[0:1, :], pad[0:1, 0:width]).then_inc(padded, 16)
                    n_pads += 1
                    at = 1 + used
                    while at < slots + 2:
                        k = min(128, slots + 2 - at)
                        sp.dma_start(table[at:at + k, :], pad[0:k, 0:width]).then_inc(padded, 16)
                        at += k
                        n_pads += 1

                def step(cs):
                    c = cs[0]
                    k = step.k
                    first = c.i - k * (TT // GT)
                    if not isinstance(first, int):
                        first = sp.snap(first)
                    start = first * GE if isinstance(first, int) else sp.snap(first * GE)
                    if c.has(2):
                        sp.wait_ge(row_used, c.count(2))
                    sp.dma_start(key_row[:, c.slot, :], seg(A_keys[k], start, GE).partition_broadcast(128))\
                      .then_inc(keys_landed[c.slot], 16)
                    if k == 0:
                        if c.slot_used():
                            sp.wait_ge(scattered[c.slot], c.landed(16 * 2 * GT, 1))
                        hold(sp, w)
                        for lo, hi, name in ((W_SH, W_SH + N_SH, "edge_attr_4"), (W_LEN, W_LEN + N_LEN, "edge_attr_10")):
                            src = seg(A[name], start, GE)
                            sp.dma_start(out_d[:, c.slot, :, lo:hi], src.rearrange("(j p) c -> p j c", p=LE).bitcast(I32))\
                              .then_inc(attrs_landed[c.slot], 16)
                for step.k in range(2):
                    run_chunks(sp, TT // GT, 2, [0], step, base=step.k * (TT // GT))
                sp.wait_ge(padded, 16 * n_pads)

            @block.gpsimd
            def _(pool):
                nc.gpsimd.memset(nv_tab[:, :], 0.0)
                nc.gpsimd.memset(zeros[:, :], 0.0)
                nc.gpsimd.memset(pad[:, :], 0)
                nc.gpsimd.memset(out_d[:, :, :, :], 0)
                nc.gpsimd.memset(earlier[:, :], 1.0)
                nc.gpsimd.memset(below[:, :], 1.0)
                nc.gpsimd.iota(iota_q[:, :], pattern=[[1, NQ]], base=0, channel_multiplier=0,
                               allow_small_or_imprecise_dtypes=True)
                nc.gpsimd.iota(iota_l[:, :], pattern=[[1, 128]], base=0, channel_multiplier=0,
                               allow_small_or_imprecise_dtypes=True)
                nc.gpsimd.iota(iota_p[:, :], pattern=[[0, 1]], base=0, channel_multiplier=1,
                               allow_small_or_imprecise_dtypes=True)
                pool.drain()
                nc.gpsimd.affine_select(out=earlier[:, :], in_=earlier[:, :], compare_op=ALU.is_gt, fill=0.0, base=0,
                                        pattern=[[-1, LE]], channel_multiplier=1)
                nc.gpsimd.affine_select(out=below[:, :], in_=below[:, :], compare_op=ALU.is_gt, fill=0.0, base=0,
                                        pattern=[[1, 128]], channel_multiplier=-1)
                nc.gpsimd.memset(pad[:, 0:1], N)
                pool.drain()
                nc.gpsimd.memset(zeros[:, 0:1], 0.0).then_inc(made, 1)
                bound_c, bound_d = pool.to_reg(g.EC + 1), pool.to_reg(g.ED + 1)

                def step(cs):
                    c = cs[0]
                    pool.wait_ge(rec_ready, c.count())
                    hold(pool, w)
                    for t in range(GT):
                        pool.indirect_dma_start(T.rec_c, bass.IndirectOffsetOnAxis(ap=at_c[:, c.slot, t:t + 1], axis=0),
                                                out_c[:, c.slot, t, :], None, bounds_check=bound_c, oob_is_err=False)\
                            .then_inc(scattered[c.slot], 16)
                        if step.k == 0:
                            pool.indirect_dma_start(T.rec_d, bass.IndirectOffsetOnAxis(ap=at_d[:, c.slot, t:t + 1], axis=0),
                                                    out_d[:, c.slot, t, :], None, bounds_check=bound_d, oob_is_err=False)\
                                .then_inc(scattered[c.slot], 16)
                for step.k in range(2):
                    run_chunks(pool, TT // GT, 2, [0], step, base=step.k * (TT // GT))
                for s in range(2):
                    pool.wait_ge(scattered[s], 16 * 3 * GT * (TT // GT) // 2)

            @block.tensor
            def _(pe):
                pe.wait_ge(made, 1)
                for k in range(2):
                    def step(cs):
                        c = cs[0]
                        pe.wait_ge(oh1, c.count())
                        nc.tensor.matmul(ps_look[k][0][:, 0:NQ], oh_lane[:, c.slot % 4, :], oh_quot[:, c.slot % 4, :],
                                         start=isinstance(c.i, int) and c.i == k * TT,
                                         stop=isinstance(c.i, int) and c.i == k * TT + TT - 1).then_inc(hist_done, 1)
                    run_chunks(pe, TT, RING, [0], step, base=k * TT)
                pe.wait_ge(sums_ready, 1)
                nc.tensor.matmul(ps_look[2][0][:, 0:2], below[:, :], row_sum[:, :], start=True, stop=True).then_inc(pre_done, 1)
                pe.wait_ge(base_ready, 1)
                pe.wait_ge(loaded, 16 * (6 if N % 128 else 5))
                nc.tensor.matmul(ps_run[:, 0:NQ], w["ident"][:, :], base[:, 0, :], start=True, stop=True).then_inc(updated, 1)
                for k in range(2):
                    def step(cs):
                        c = cs[0]
                        pe.wait_ge(oh_ready, c.count())
                        pe.wait_ge(run_copied, c.count())
                        nc.tensor.matmul(ps_run[:, 0:NQ], oh_lane[:, c.slot % 4, :], oh_quot[:, c.slot % 4, :],
                                         start=False, stop=True, skip_group_check=True).then_inc(updated, 1)
                        gr = group(c)
                        pe.wait_ge(row_ready, gr.count())
                        if c.has(2):
                            pe.wait_ge(selected, c.count(2))
                        t = c.slot % GT
                        oh = oh_row[:, gr.slot, t * LE:(t + 1) * LE]
                        tabs = [running[:, c.slot % 2, :]] + ([base[:, 1, :], nv_tab[:, :]] if k == 0 else [])
                        for i, tab in enumerate(tabs):
                            ins = nc.tensor.matmul(ps_look[i][c.slot % 2][0:LE, 0:NQ], oh, tab, start=True, stop=True)
                        ins.then_inc(looked, 1)
                    run_chunks(pe, TT, RING, [0], step, base=k * TT)

            @block.scalar
            def _(act):
                nc.scalar.preload_act_table_set(ACT_SET)
                act.wait_ge(updated, 1)
                nc.scalar.activation(running[:, 0, :], ps_run[:, 0:NQ], ACT.Copy).then_inc(run_copied, 1)

                def step(cs):
                    c = cs[0]
                    if isinstance(c.i, int) and c.i == 2 * TT - 1:
                        return
                    act.wait_ge(updated, c.i + 2)
                    if c.has(1):
                        act.wait_ge(looked, c.count(1))
                    nc.scalar.activation(running[:, (c.slot + 1) % 2, :], ps_run[:, 0:NQ], ACT.Copy).then_inc(run_copied, 1)
                run_chunks(act, 2 * TT, RING, [0], step)

            @block.vector
            def _(dve):
                v = nc.vector
                dve.wait_ge(made, 1)
                dve.wait_ge(loaded, 16 * (6 if N % 128 else 5))
                both = ends[:, :, :].rearrange("p k j -> p (k j)")
                v.tensor_copy(key[:, :], both)
                v.tensor_scalar(part[:, :], both, 127, None, ALU.bitwise_and)
                dve.drain()
                v.tensor_copy(lane[:, :], part[:, :])
                dve.drain()
                v.tensor_scalar(part[:, :], both, 7, None, ALU.logical_shift_right)
                dve.drain()
                v.tensor_copy(quot[:, :], part[:, :])
                dve.drain()

                def one_hots(c, s, sem):
                    v.tensor_scalar(oh_lane[:, s, :], iota_l[0:LE, :], col(lane, c), None, ALU.is_equal)
                    v.tensor_scalar(oh_quot[:, s, :], iota_q[0:LE, :], col(quot, c), None, ALU.is_equal)\
                     .then_inc(sem, 1)

                def step(cs):
                    if cs[0].has(4):
                        dve.wait_ge(hist_done, cs[0].count(4))
                    one_hots(cs[0], cs[0].slot % 4, oh1)
                run_chunks(dve, 2 * TT, RING, [0], step)
                dve.wait_ge(hist_done, 2 * TT)
                for k in range(2):
                    v.tensor_copy(hist[:, k, :], ps_look[k][0][:, 0:NQ])
                dve.drain()
                v.tensor_reduce(row_sum[:, :], hist[:, :, :], AX_X, ALU.add).then_inc(sums_ready, 1)
                dve.wait_ge(pre_done, 1)
                v.tensor_copy(row_pre[:, :], ps_look[2][0][:, 0:2])
                dve.drain()
                for k in range(2):
                    v.tensor_tensor_scan(base[:, k, :], hist[:, k, :], zeros[:, :], row_pre[:, k:k + 1], ALU.add, ALU.add)
                dve.drain()
                v.tensor_tensor(base[:, :, :], base[:, :, :], hist[:, :, :], ALU.subtract)
                dve.drain()
                v.scalar_tensor_tensor(base[:, 0, :], base[:, 0, :], 1.0, base[:, 1, :], ALU.add, ALU.add).then_inc(base_ready, 1)

                for k in range(2):
                    def step(cs):
                        c = cs[0]
                        dve.drain()
                        if c is not None:
                            gr = group(c)
                            if c.slot % GT == 0:
                                dve.wait_ge(keys_landed[gr.slot], gr.landed(16))
                                if c.has(GT + 1):
                                    dve.wait_ge(looked, c.count(GT + 1))
                                v.tensor_scalar(lane_row[:, :], key_row[:, gr.slot, :], 127, None, ALU.bitwise_and)
                                dve.drain()
                                v.tensor_scalar(oh_row[:, gr.slot, :], lane_row[:, :], iota_p[:, 0:1], None,
                                                ALU.is_equal).then_inc(row_ready, 1)
                            if c.has(4):
                                dve.wait_ge(updated, c.count(3))
                            one_hots(c, c.slot % 4, oh_ready)
                            t = c.slot % GT
                            ins = v.scalar_tensor_tensor(junk2[:, :], key_row[0:LE, gr.slot, t * LE:(t + 1) * LE],
                                                         col(key, c), earlier[:, :], ALU.is_equal, ALU.mult,
                                                         accum_out=rank[:, c.slot % 2:c.slot % 2 + 1])
                            if t == GT - 1:
                                ins.then_inc(row_used, 1)
                        c = cs[1]
                        if c is None:
                            return
                        gr = group(c)
                        t = c.slot % GT
                        dve.wait_ge(looked, c.count())
                        for i in range(3 if k == 0 else 1):
                            first = rank[:, c.slot % 2:c.slot % 2 + 1] if i == 0 else 0.0
                            ins = v.tensor_tensor_reduce(junk[:, i, :], ps_look[i][c.slot % 2][0:LE, 0:NQ],
                                                         oh_quot[:, c.slot % 4, :], 1.0, first, ALU.mult, ALU.add,
                                                         found[:, i, t:t + 1])
                        ins.then_inc(selected, 1)
                        if t != GT - 1:
                            return
                        rel = c.i - (GT - 1 + k * TT)
                        dve.drain()
                        wait_scattered(gr, k)
                        def cols(tab, start):
                            return tab[:, start:start + GT] if isinstance(start, int) else tab[:, bass.ds(start, GT)]
                        v.tensor_copy(at_c[:, gr.slot, :], found[:, 0, :])
                        v.tensor_copy(out_c[:, gr.slot, :, 0], cols(ends[:, k, :], rel))
                        if k == 0:
                            dve.wait_ge(attrs_landed[gr.slot], gr.landed(32))
                            v.tensor_copy(out_c[:, gr.slot, :, 1], cols(ends[:, 1, :], rel))
                            v.tensor_tensor(at_d[:, gr.slot, :], found[:, 0, :], found[:, 1, :], ALU.subtract)
                            v.tensor_copy(out_d[:, gr.slot, :, W_DST], cols(ends[:, 0, :], rel))
                            v.tensor_copy(out_d[:, gr.slot, :, W_SRC], cols(ends[:, 1, :], rel))
                            v.tensor_copy(out_d[:, gr.slot, :, W_TYPE], cols(kind[:, :], rel))
                            v.tensor_copy(out_d[:, gr.slot, :, W_EW], cols(ew[:, :].bitcast(I32), rel))
                            v.tensor_copy(out_d[:, gr.slot, :, W_NV], found[:, 2, :].bitcast(I32))
                        else:
                            v.tensor_copy(out_c[:, gr.slot, :, 1], cols(ends[:, 0, :], rel))
                        dve.drain().then_inc(rec_ready, 1)

                    def wait_scattered(gr, k):
                        half = TT // GT // 2
                        if k == 0:
                            if gr.slot_used():
                                dve.wait_ge(scattered[gr.slot], gr.landed(16 * 2 * GT, 1))
                        else:
                            dve.wait_ge(scattered[gr.slot], (gr.turn - half) * (16 * GT) + 16 * 2 * GT * half)
                    run_chunks(dve, TT, RING, [0, 1], step, base=k * TT)
        end_phase(nc, P)


class Slots:

    RING = 8

    def __init__(self, P, nc, g, w, table, width, n, backwards):
        self.nc, self.g, self.w, self.table, self.width, self.n, self.back = nc, g, w, table, width, n, backwards
        R = self.RING
        self.rec = P.sb("rec", [128, R, TPC, width], I32)
        self.near = P.sb("near", [128, R, 2, TPC], I32)
        self.same = P.sb("same", [128, R, 2, TPC], BF16)
        self.inner = P.sb("inner", [128, R, TPC])
        self.row = P.sb("row", [128, R, TPC])
        self.to = P.sb("to", [128, R, TPC], I32)
        self.of = P.sb("of", [128, R, 2, TPC], I32)
        self.landed = P.sems("rec_landed", R)
        self.ready = P.sem("idx_ready")

    def pos(self, c):
        return self.n - 1 - c.i if self.back else c.i

    def start(self, eng, c):
        p = self.pos(c)
        return p * CH if isinstance(p, int) else eng.snap(p * CH)

    def rows(self, t, start, off=0):
        part = t[start + off:start + off + CH] if isinstance(start, int) else t[bass.ds(start + off, CH)]
        return part

    def load(self, sp, c, start):
        R = self.rows
        with self.nc.allow_non_contiguous_dma(reason="one word per slot"):
            sp.dma_start(self.rec[:, c.slot], R(self.table, start, 1).rearrange("(t p) w -> p t w", p=128))\
              .then_inc(self.landed[c.slot], 16)
            for k in range(2):
                sp.dma_start(self.near[:, c.slot, k, :],
                             R(self.table, start, 2 * k)[:, 0].rearrange("(t p) -> p t", p=128))\
                  .then_inc(self.landed[c.slot], 16)

    def index(self, dve, c, other_scale=1, to_scale=1, to_plus=0, to_later=False):
        v = self.nc.vector
        dve.wait_ge(self.landed[c.slot], c.landed(48))
        s = c.slot
        node = self.rec[:, s, :, 0]
        first, last = (1, 0) if self.back else (0, 1)
        v.tensor_tensor(self.same[:, s, 0, :], node, self.near[:, s, first, :], ALU.is_equal)
        v.tensor_tensor(self.inner[:, s, :], node, self.near[:, s, last, :], ALU.is_equal)
        v.tensor_scalar(self.of[:, s, 1, :], node, self.g.N - 1, other_scale, ALU.min, ALU.mult)
        v.tensor_scalar(self.of[:, s, 0, :], self.rec[:, s, :, 1], other_scale, None, ALU.mult)
        if to_scale != 1:
            v.tensor_scalar(self.row[:, s, :], node, to_scale, to_plus, ALU.mult, ALU.add)
            node = self.row[:, s, :]
        dve.drain()
        v.tensor_scalar(self.same[:, s, 1, :], self.same[:, s, 0, :], -1.0, -NEG, ALU.add, ALU.mult)
        if not to_later:
            v.scalar_tensor_tensor(self.to[:, s, :], self.inner[:, s, :], float(FAR), node, ALU.mult, ALU.add)
        dve.drain().then_inc(self.ready, 1)

    def index_to(self, c):
        self.nc.vector.scalar_tensor_tensor(self.to[:, c.slot, :], self.inner[:, c.slot, :], float(FAR),
                                            self.rec[:, c.slot, :, 0], ALU.mult, ALU.add)

    def gather(self, pool, c, which, out, table, bound, sem):
        for t in range(TPC):
            pool.indirect_dma_start(out[:, c.slot, t, :], None, table,
                                    bass.IndirectOffsetOnAxis(ap=self.of[:, c.slot, which, t:t + 1], axis=0),
                                    bounds_check=bound, oob_is_err=False).then_inc(sem[c.slot], 16)

    def scatter(self, pool, c, rows, table, bound, sem):
        for t in range(TPC):
            pool.indirect_dma_start(table, bass.IndirectOffsetOnAxis(ap=self.to[:, c.slot, t:t + 1], axis=0),
                                    rows[:, c.slot, t, :], None,
                                    bounds_check=bound, oob_is_err=False).then_inc(sem[c.slot], 16)


def scan(nc, S, out, mask, data, carry, op0, op1):
    if S.back:
        out, mask, data = out[:, ::-1], mask[:, ::-1], data[:, ::-1]
    return nc.vector.tensor_tensor_scan(out, mask, data, carry if carry is not None else 0.0, op0, op1)


def edge_col(S, t):
    return t[:, 0:1] if S.back else t[:, CH - 1:CH]


def turns(n, slot, ring):
    return (n - slot + ring - 1) // ring


def build_layer0(nc, g, w, T, A):
    n = g.ED // CH
    IDX, TURN, MIX, WGT, SUM, ROW, FIN, SAVE = 0, 2, 3, 4, 5, 6, 7, 8
    with ExitStack() as ctx:
        P = Phase(nc, ctx, "l0")
        S = Slots(P, nc, g, w, T.rec_d, REC, n, False)
        R = S.RING
        xs = P.sb("xs", [128, R, TPC, D])
        xd = P.sb("xd", [128, R, TPC, D])
        out = P.sb("out", [128, R, TPC, D])
        xsT = P.sb("xsT", [128, CH])
        xdT = P.sb("xdT", [128, R, CH])
        attrT = P.sb("attrT", [N_ATTR, CH])
        hT = P.sb("hT", [100, CH])
        mask = P.sb("mask", [128, CH])
        sh = P.sb("sh", [128, 2, CH])
        part = P.sb("part", [128, 3, CH])
        msg = P.sb("msg", [128, 2, 3, CH])
        agg = P.sb("agg", [128, 2, CH])
        y = P.sb("y", [128, 2, TPC, D])
        stats, mv = P.sb("stats", [128, 4, 6]), P.sb("mv", [128, 4, 2])
        rstd, shift = P.sb("rstd", [128, 4]), P.sb("shift", [128, 4])
        ps_w = [P.ps(f"ps{k}") for k in range(3)]
        ps_g1, ps_g2, ps_m, ps_o, ps_z = (P.ps("ps_" + k) for k in ("g1", "g2", "m", "o", "z"))
        pe_ = {k: P.sem("pe_" + k) for k in ("tr", "h", "m", "s", "g", "w", "o", "z")}
        ac_ = {k: P.sem("ac_" + k) for k in ("tr", "h", "m", "s", "rstd", "out")}
        ve_ = {k: P.sem("ve_" + k) for k in ("part", "msg", "agg", "y", "stats", "shift")}
        gathered, scattered, saved = P.sems("gathered", R), P.sems("scattered", R), P.sems("saved", R)
        with nc.Block() as block:
            @block.sync
            def _(sp):
                def step(cs):
                    c = cs[0]
                    if c is not None:
                        start = S.start(sp, c)
                        if c.slot_used():
                            sp.wait_ge(ve_["y"], c.count(R))
                        hold(sp, w)
                        S.load(sp, c, start)
                    c = cs[1]
                    if c is not None:
                        start = S.start(sp, c)
                        sp.wait_ge(ac_["out"], c.count())
                        hold(sp, w)
                        sp.dma_start(S.rows(T.x1_slot, start).rearrange("(t p) c -> p t c", p=128), out[:, c.slot])\
                          .then_inc(saved[c.slot], 16)
                run_chunks(sp, n, R, [IDX, SAVE], step)
                for s in range(R):
                    sp.wait_ge(saved[s], 16 * turns(n, s, R))

            @block.gpsimd
            def _(pool):
                bound = pool.to_reg(g.N - 1)

                def step(cs):
                    c = cs[0]
                    if c is not None:
                        pool.wait_ge(S.ready, c.count())
                        hold(pool, w)
                        S.gather(pool, c, 0, xs, T.x, bound, gathered)
                        S.gather(pool, c, 1, xd, T.x, bound, gathered)
                    c = cs[1]
                    if c is not None:
                        pool.wait_ge(ac_["out"], c.count())
                        hold(pool, w)
                        S.scatter(pool, c, out, T.x1, bound, scattered)
                run_chunks(pool, n, R, [IDX, FIN], step)
                for s in range(R):
                    pool.wait_ge(scattered[s], 64 * turns(n, s, R))

            @block.tensor
            def _(pe):
                mm = nc.tensor.matmul

                def step(cs):
                    turn, mix, wgt, sum_, row = cs
                    if row is not None:
                        k = row.slot % 2
                        pe.wait_ge(ve_["agg"], row.count())
                        if row.has(1):
                            pe.wait_ge(ve_["y"], row.count(1))
                        for t in range(TPC):
                            ts = slice(t * TILE, (t + 1) * TILE)
                            mm(ps_z[:, ts], agg[:, k, ts], w["ident"][:, :], start=True, stop=False)
                            last = mm(ps_z[:, ts], xdT[:, row.slot, ts], w["Wsi"][:, :], start=False, stop=True)
                        last.then_inc(pe_["z"], 1)
                    if mix is not None:
                        pe.wait_ge(ac_["tr"], mix.count())
                        if mix.has(1):
                            pe.wait_ge(ve_["part"], mix.count(1))
                        mm(ps_g1[:, :], w["g1"][:, :], xsT[:, :], start=True, stop=True)
                        mm(ps_g2[:, :], w["g2"][:, :], xsT[:, :], start=True, stop=True).then_inc(pe_["g"], 1)
                    if wgt is not None:
                        pe.wait_ge(ac_["h"], wgt.count())
                        pe.wait_ge(ac_["s"], wgt.count())
                        for k in range(3):
                            last = mm(ps_w[k][:, :], w[f"h{k + 1}"][:, :], hT[:, :], start=True, stop=True)
                        last.then_inc(pe_["w"], 1)
                    if sum_ is not None:
                        pe.wait_ge(ve_["msg"], sum_.count())
                        if sum_.has(1):
                            pe.wait_ge(ve_["agg"], sum_.count(1))
                            pe.wait_ge(ac_["m"], sum_.count(1))
                        spread(nc, ps_m, S.same[:, sum_.slot, 0, :], w["identb"]).then_inc(pe_["m"], 1)
                        for k in range(3):
                            last = mm(ps_o[:, :], w[f"o{k + 1}"][:, :], msg[:, sum_.slot % 2, k, :],
                                      start=k == 0, stop=k == 2)
                        last.then_inc(pe_["o"], 1)
                    if mix is not None:
                        if mix.has(1):
                            pe.wait_ge(ve_["msg"], mix.count(1))
                        mm(ps_w[0][0:100, :], w["fc1"][:, :], attrT[:, :], start=True, stop=True).then_inc(pe_["h"], 1)
                        mm(ps_w[1][:, :], w["sel_sh"][:, :], attrT[:, :], start=True, stop=True)
                        mm(ps_w[2][:, :], w["sel_sh0"][:, :], attrT[:, :], start=True, stop=True).then_inc(pe_["s"], 1)
                    if turn is not None:
                        pe.wait_ge(gathered[turn.slot], turn.landed(128))
                        if turn.has(1):
                            pe.wait_ge(ac_["tr"], turn.count(1))
                            pe.wait_ge(ac_["h"], turn.count(1))
                        for t in range(TPC):
                            nc.tensor.transpose(ps_w[0][0:N_ATTR, t * TILE:(t + 1) * TILE],
                                                S.rec[:, turn.slot, t, W_SH:W_SH + N_ATTR].bitcast(F32),
                                                w["ident"][:, :])
                        if turn.has(1):
                            pe.wait_ge(ac_["s"], turn.count(1))
                        transpose4(nc, ps_w[1], xs[:, turn.slot], w["ident"])
                        transpose4(nc, ps_w[2], xd[:, turn.slot], w["ident"]).then_inc(pe_["tr"], 1)
                run_chunks(pe, n, R, [TURN, MIX, WGT, SUM, ROW], step)

            @block.scalar
            def _(act):
                nc.scalar.preload_act_table_set(ACT_SET)
                ac = nc.scalar.activation

                def step(cs):
                    turn, mix, sum_, row, fin = cs
                    if fin is not None:
                        act.wait_ge(ve_["shift"], fin.count())
                        if fin.slot_used():
                            act.wait_ge(saved[fin.slot], fin.landed(16, 1))
                            act.wait_ge(scattered[fin.slot], fin.landed(64, 1))
                        apply_rows(nc, out[:, fin.slot], y[:, fin.slot % 2], shift, rstd).then_inc(ac_["out"], 1)
                    if sum_ is not None:
                        act.wait_ge(pe_["m"], sum_.count())
                        if sum_.has(1):
                            act.wait_ge(ve_["agg"], sum_.count(1))
                        ac(mask[:, :], ps_m[:, :], ACT.Copy).then_inc(ac_["m"], 1)
                    if mix is not None:
                        act.wait_ge(pe_["h"], mix.count())
                        if mix.has(1):
                            act.wait_ge(pe_["w"], mix.count(1))
                        ac(hT[:, :], ps_w[0][0:100, :], ACT.Relu).then_inc(ac_["h"], 1)
                        act.wait_ge(pe_["s"], mix.count())
                        if mix.has(1):
                            act.wait_ge(ve_["part"], mix.count(1))
                        ac(sh[:, 0, :], ps_w[1][:, :], ACT.Copy)
                        ac(sh[:, 1, :], ps_w[2][:, :], ACT.Copy).then_inc(ac_["s"], 1)
                    if turn is not None:
                        act.wait_ge(pe_["tr"], turn.count())
                        if turn.slot_used():
                            act.wait_ge(pe_["z"], turn.count(R))
                        ac(xsT[:, :], ps_w[1][:, :], ACT.Copy)
                        ac(attrT[:, :], ps_w[0][0:N_ATTR, :], ACT.Copy)
                        ac(xdT[:, turn.slot, :], ps_w[2][:, :], ACT.Copy).then_inc(ac_["tr"], 1)
                    if row is not None:
                        act.drain()
                        act.wait_ge(ve_["stats"], row.count())
                        ln_rstd(nc, act, mv[:, :, 1], rstd[:, :], w["eps"]).then_inc(ac_["rstd"], 1)
                run_chunks(act, n, R, [TURN, MIX, SUM, ROW, FIN], step)

            @block.vector
            def _(dve):
                v = nc.vector

                def step(cs):
                    m, mix, wgt, sum_, row, fin = cs
                    dve.drain()
                    if fin is not None:
                        dve.wait_ge(ac_["rstd"], fin.count())
                        if fin.has(1):
                            dve.wait_ge(ac_["out"], fin.count(1))
                        make_shift(nc, shift, mv, rstd).then_inc(ve_["shift"], 1)
                    if m is not None:
                        S.index(dve, m, to_later=True)
                    if row is not None:
                        if row.slot_used():
                            dve.wait_ge(scattered[row.slot], row.landed(64, 1))
                        S.index_to(row)
                        dve.wait_ge(pe_["z"], row.count())
                        v.tensor_tensor(y[:, row.slot % 2], tiles(ps_z[:, :]), xd[:, row.slot], ALU.add)\
                         .then_inc(ve_["y"], 1)
                    if wgt is not None:
                        dve.wait_ge(pe_["w"], wgt.count())
                        if wgt.has(2):
                            dve.wait_ge(pe_["o"], wgt.count(2))
                        for k in range(3):
                            last = v.tensor_tensor(msg[:, wgt.slot % 2, k, :], ps_w[k][:, :], part[:, k, :], ALU.mult)
                        last.then_inc(ve_["msg"], 1)
                    if row is not None:
                        dve.drain()
                        ln_stats(nc, y[:, row.slot % 2], stats, mv)
                        dve.drain()
                        ln_aggregate(nc, stats, mv, TPC).then_inc(ve_["stats"], 1)
                    if sum_ is not None:
                        k = sum_.slot % 2
                        dve.wait_ge(pe_["o"], sum_.count())
                        dve.wait_ge(ac_["m"], sum_.count())
                        if sum_.has(2):
                            dve.wait_ge(pe_["z"], sum_.count(2))
                        carry = None if isinstance(sum_.i, int) and sum_.i == 0 else edge_col(S, agg[:, 1 - k, :])
                        scan(nc, S, agg[:, k, :], mask[:, :], ps_o[:, :], carry, ALU.mult, ALU.add)\
                            .then_inc(ve_["agg"], 1)
                    if mix is not None:
                        dve.wait_ge(pe_["g"], mix.count())
                        dve.wait_ge(ac_["s"], mix.count())
                        v.tensor_tensor(part[:, 0, :], ps_g1[:, :], sh[:, 0, :], ALU.mult)
                        v.tensor_tensor(part[:, 1, :], ps_g2[:, :], sh[:, 1, :], ALU.mult)
                        v.tensor_tensor(part[:, 2, :], ps_g2[:, :], sh[:, 0, :], ALU.mult).then_inc(ve_["part"], 1)
                run_chunks(dve, n, R, [IDX, MIX, WGT, SUM, ROW, FIN], step)
        end_phase(nc, P)


def make_shift(nc, shift, mv, rstd):
    return nc.vector.scalar_tensor_tensor(shift[:, :], mv[:, :, 0], -1.0, rstd[:, :], ALU.mult, ALU.mult)


def apply_rows(nc, out, y, shift, rstd):
    last = None
    for t in range(TPC):
        last = nc.scalar.activation(out[:, t, :], y[:, t, :], ACT.Identity, bias=shift[:, t:t + 1],
                                    scale=rstd[:, t:t + 1])
    return last


def finish_rows(nc, dve, b, y, stats, mv, rstd, out, ve_, rstd_done):
    dve.drain()
    ln_stats(nc, y, stats, mv)
    dve.drain()
    ln_aggregate(nc, stats, mv, TPC).then_inc(ve_["stats"], 1)
    dve.drain()
    dve.wait_ge(rstd_done, b.count())
    ln_apply(nc, out[:, b.slot], y, mv, rstd).then_inc(ve_["out"], 1)


def build_layer1(nc, g, w, T, A):
    n = g.ED // CH
    with ExitStack() as ctx:
        P = Phase(nc, ctx, "l1")
        S = Slots(P, nc, g, w, T.rec_d, REC, n, False)
        R = S.RING
        xs = P.sb("xs", [128, R, TPC, D])
        xd = P.sb("xd", [128, R, TPC, D])
        out = P.sb("out", [128, R, TPC, D])
        xsT = P.sb("xsT", [128, CH])
        xdT = P.sb("xdT", [128, 2, CH])
        mask = P.sb("mask", [128, CH])
        ones = P.sb("ones", [128, CH])
        sums, degree = P.sb("sums", [128, 2, CH]), P.sb("degree", [128, 2, CH])
        inv = P.sb("inv", [128, CH])
        mean = P.sb("mean", [128, 2, CH])
        y = P.sb("y", [128, TPC, D])
        stats, mv, rstd = P.sb("stats", [128, 4, 6]), P.sb("mv", [128, 4, 2]), P.sb("rstd", [128, 4])
        ps = [P.ps(f"ps{k}") for k in range(4)]
        pe_ = {k: P.sem("pe_" + k) for k in ("tr", "trd", "m", "z")}
        ac_ = {k: P.sem("ac_" + k) for k in ("tr", "trd", "m", "inv", "rstd")}
        ve_ = {k: P.sem("ve_" + k) for k in ("sum", "mean", "y", "stats", "out", "ones")}
        gathered, scattered, loaded = P.sems("gathered", R), P.sems("scattered", R), P.sems("loaded", R)
        with nc.Block() as block:
            @block.sync
            def _(sp):
                def step(cs):
                    c = cs[0]
                    start = S.start(sp, c)
                    if c.slot_used():
                        sp.wait_ge(scattered[c.slot], c.landed(64, 1))
                    hold(sp, w)
                    S.load(sp, c, start)
                    sp.dma_start(xd[:, c.slot], S.rows(T.x1_slot, start).rearrange("(t p) c -> p t c", p=128))\
                      .then_inc(loaded[c.slot], 16)
                run_chunks(sp, n, R, [0], step)

            @block.gpsimd
            def _(pool):
                bound = pool.to_reg(g.N - 1)

                def step(cs):
                    c = cs[0]
                    if c is not None:
                        pool.wait_ge(S.ready, c.count())
                        hold(pool, w)
                        S.gather(pool, c, 0, xs, T.x1, bound, gathered)
                    c = cs[1]
                    if c is not None:
                        pool.wait_ge(ve_["out"], c.count())
                        hold(pool, w)
                        S.scatter(pool, c, out, T.x2, bound, scattered)
                run_chunks(pool, n, R, [0, 2], step)
                for s in range(R):
                    pool.wait_ge(scattered[s], 64 * turns(n, s, R))

            @block.tensor
            def _(pe):
                mm = nc.tensor.matmul

                def step(cs):
                    a, b = cs
                    if a is not None:
                        pe.wait_ge(gathered[a.slot], a.landed(64))
                        if a.has(1):
                            pe.wait_ge(ac_["tr"], a.count(1))
                        transpose4(nc, ps[0], xs[:, a.slot], w["ident"]).then_inc(pe_["tr"], 1)
                        if a.has(1):
                            pe.wait_ge(ac_["m"], a.count(1))
                        spread(nc, ps[2], S.same[:, a.slot, 0, :], w["identb"]).then_inc(pe_["m"], 1)
                        pe.wait_ge(loaded[a.slot], a.landed(16))
                        if a.has(1):
                            pe.wait_ge(ac_["trd"], a.count(1))
                        transpose4(nc, ps[1], xd[:, a.slot], w["ident"]).then_inc(pe_["trd"], 1)
                    if b is not None:
                        pe.wait_ge(ve_["mean"], b.count())
                        pe.wait_ge(ac_["trd"], b.count())
                        if b.has(1):
                            pe.wait_ge(ve_["y"], b.count(1))
                        add_bias(nc, ps[3], w, "bias1")
                        for t in range(TPC):
                            ts = slice(t * TILE, (t + 1) * TILE)
                            mm(ps[3][:, ts], xdT[:, b.slot % 2, ts], w["W1a"][:, :], start=False, stop=False)
                            last = mm(ps[3][:, ts], mean[:, b.slot % 2, ts], w["W1b"][:, :], start=False,
                                      stop=t == TPC - 1)
                        last.then_inc(pe_["z"], 1)
                run_chunks(pe, n, R, [0, 1], step)

            @block.scalar
            def _(act):
                nc.scalar.preload_act_table_set(ACT_SET)
                ac = nc.scalar.activation

                def step(cs):
                    a, b = cs
                    if a is not None:
                        act.wait_ge(pe_["tr"], a.count())
                        if a.has(1):
                            act.wait_ge(ve_["sum"], a.count(1))
                        ac(xsT[:, :], ps[0][:, :], ACT.Copy).then_inc(ac_["tr"], 1)
                        act.wait_ge(pe_["m"], a.count())
                        ac(mask[:, :], ps[2][:, :], ACT.Copy).then_inc(ac_["m"], 1)
                        act.wait_ge(ve_["sum"], a.count())
                        ac(inv[:, :], degree[:, a.slot % 2, :], ACT.Ln)
                        act.drain()
                        ac(inv[:, :], inv[:, :], ACT.Exp, scale=-1.0).then_inc(ac_["inv"], 1)
                        act.wait_ge(pe_["trd"], a.count())
                        if a.has(2):
                            act.wait_ge(pe_["z"], a.count(2))
                        ac(xdT[:, a.slot % 2, :], ps[1][:, :], ACT.Copy).then_inc(ac_["trd"], 1)
                    if b is not None:
                        act.wait_ge(ve_["stats"], b.count())
                        ln_rstd(nc, act, mv[:, :, 1], rstd[:, :], w["eps"]).then_inc(ac_["rstd"], 1)
                run_chunks(act, n, R, [0, 1], step)

            @block.vector
            def _(dve):
                v = nc.vector
                v.memset(ones[:, :], 1.0)

                def step(cs):
                    m, a, b = cs
                    dve.drain()
                    if m is not None:
                        S.index(dve, m)
                    if a is not None:
                        k = a.slot % 2
                        first = isinstance(a.i, int) and a.i == 0
                        dve.wait_ge(ac_["tr"], a.count())
                        dve.wait_ge(ac_["m"], a.count())
                        scan(nc, S, degree[:, k, :], mask[:, :], ones[:, :],
                             None if first else edge_col(S, degree[:, 1 - k, :]), ALU.mult, ALU.add)
                        scan(nc, S, sums[:, k, :], mask[:, :], xsT[:, :],
                             None if first else edge_col(S, sums[:, 1 - k, :]), ALU.mult, ALU.add)\
                            .then_inc(ve_["sum"], 1)
                        dve.drain()
                        dve.wait_ge(ac_["inv"], a.count())
                        if a.has(2):
                            dve.wait_ge(pe_["z"], a.count(2))
                        v.tensor_tensor(mean[:, k, :], sums[:, k, :], inv[:, :], ALU.mult).then_inc(ve_["mean"], 1)
                    if b is not None:
                        dve.wait_ge(pe_["z"], b.count())
                        v.scalar_tensor_tensor(y[:, :, :], tiles(ps[3][:, :]), 0.0, xd[:, b.slot], ALU.max, ALU.add)\
                            .then_inc(ve_["y"], 1)
                        finish_rows(nc, dve, b, y, stats, mv, rstd, out, ve_, ac_["rstd"])
                run_chunks(dve, n, R, [0, 2, 3], step)
        end_phase(nc, P)


def build_layer2_scores(nc, g, w, T, A):
    n = g.EC // CH
    assert n == -(-g.N // CH)
    with ExitStack() as ctx:
        P = Phase(nc, ctx, "l2a")
        S = Slots(P, nc, g, w, T.rec_c, 2, n, False)
        R = S.RING
        xo = P.sb("xo", [128, R, TPC, D])
        xt = P.sb("xt", [128, R, TPC, D])
        xoT = P.sb("xoT", [128, 2, CH])
        xtT = P.sb("xtT", [128, 2, CH])
        fresh = P.sb("fresh", [128, 2, CH])
        raw = P.sb("raw", [128, 2, 2, CH])
        proj = P.sb("proj", [128, R, CH])
        kept = P.sb("kept", [128, R, 3, CH])
        high = P.sb("high", [128, CH])
        ps = [P.ps(f"ps{k}") for k in range(6)]
        node_x = P.sb("node_x", [128, R, TPC, D])
        node_xT = P.sb("node_xT", [128, 2, CH])
        node_low = P.sb("node_low", [128, TPC, D])
        node_y = P.sb("node_y", [128, 2, TPC, D])
        node_out = P.sb("node_out", [128, R, 2, TPC, D])
        stats, mv = P.sb("stats", [128, 4, 6]), P.sb("mv", [128, 4, 2])
        rstd, shift = P.sb("rstd", [128, 2, TPC]), P.sb("shift", [128, 4])
        ps_xT, ps_z = P.ps("xT"), P.ps("z")
        node_loaded, node_stored = P.sems("node_loaded", R), P.sems("node_stored", R)
        node_ = {k: P.sem("node_" + k) for k in
                 ("turned", "xT", "z", "y", "elu", "stats", "rstd", "shift", "out3", "out4")}
        x34 = [T.x34[:, k, :] for k in range(2)]

        def node_rows(table, c):
            start = g.N - CH if isinstance(c.i, int) and c.i == n - 1 else c.i * CH
            part = table[start:start + CH, :] if isinstance(start, int) else table[bass.ds(start, CH), :]
            return part.rearrange("(p t) c -> p t c", t=TPC)
        pe_ = {k: P.sem("pe_" + k) for k in ("tr", "m", "s", "p")}
        ac_ = {k: P.sem("ac_" + k) for k in ("tr", "m", "s", "p")}
        ve_ = {k: P.sem("ve_" + k) for k in ("s", "max")}
        gathered, saved = P.sems("gathered", R), P.sems("saved", R)
        with nc.Block() as block:
            @block.sync
            def _(sp):
                def step(cs):
                    c = cs[0]
                    if c is not None:
                        start = S.start(sp, c)
                        if c.slot_used():
                            sp.wait_ge(saved[c.slot], c.landed(48, 1))
                        hold(sp, w)
                        S.load(sp, c, start)
                        if c.slot_used():
                            sp.wait_ge(node_["y"], c.count(R))
                        hold(sp, w)
                        sp.dma_start(node_x[:, c.slot], node_rows(T.x2, c)).then_inc(node_loaded[c.slot], 16)
                    c = cs[1]
                    if c is not None:
                        p = S.pos(c)
                        p0 = p * 128 if isinstance(p, int) else sp.snap(p * 128)
                        p1 = p * 4 if isinstance(p, int) else sp.snap(p * 4)
                        sp.wait_ge(ac_["p"], c.count())
                        hold(sp, w)
                        sp.dma_start(at_rows(T.proj2, p0, 128), proj[:, c.slot, :]).then_inc(saved[c.slot], 16)
                        sp.dma_start(at_rows(T.row2, p0, 128), xt[:, c.slot].rearrange("p t c -> p (t c)"))\
                          .then_inc(saved[c.slot], 16)
                        sp.wait_ge(ve_["max"], c.count())
                        hold(sp, w)
                        sp.dma_start(at_rows(T.score2, p1, 4), kept[0:128:32, c.slot].rearrange("p k c -> p (k c)"))\
                          .then_inc(saved[c.slot], 16)
                    c = cs[2]
                    if c is not None:
                        sp.wait_ge(node_["out3"], c.count())
                        hold(sp, w)
                        sp.wait_ge(node_["out4"], c.count())
                        hold(sp, w)
                        if isinstance(c.i, int) and c.i == n - 1:
                            sp.wait_ge(node_stored[(n - 2) % R], 32 * turns(n - 1, (n - 2) % R, R))
                        for k in range(2):
                            sp.dma_start(node_rows(x34[k], c), node_out[:, c.slot, k]).then_inc(node_stored[c.slot], 16)
                run_chunks(sp, n, R, [0, 6, 7], step)
                for s in range(R):
                    sp.wait_ge(node_stored[s], 32 * turns(n, s, R))
                    sp.wait_ge(saved[s], 48 * turns(n, s, R))

            @block.gpsimd
            def _(pool):
                bound = pool.to_reg(g.N - 1)

                def step(cs):
                    c = cs[0]
                    pool.wait_ge(S.ready, c.count())
                    hold(pool, w)
                    S.gather(pool, c, 0, xo, T.x2, bound, gathered)
                    S.gather(pool, c, 1, xt, T.x2, bound, gathered)
                run_chunks(pool, n, R, [0], step)

            @block.tensor
            def _(pe):
                mm = nc.tensor.matmul

                def step(cs):
                    a, b = cs
                    if a is not None:
                        pe.wait_ge(gathered[a.slot], a.landed(128))
                        if a.has(1):
                            pe.wait_ge(ac_["tr"], a.count(1))
                        transpose4(nc, ps[0], xo[:, a.slot], w["ident"])
                        transpose4(nc, ps[1], xt[:, a.slot], w["ident"]).then_inc(pe_["tr"], 1)
                        if a.has(1):
                            pe.wait_ge(ac_["m"], a.count(1))
                        spread(nc, ps[2], S.same[:, a.slot, 1, :], w["identb"]).then_inc(pe_["m"], 1)
                    if b is not None:
                        k = b.slot % 2
                        pe.wait_ge(ac_["tr"], b.count())
                        if b.has(1):
                            pe.wait_ge(ac_["s"], b.count(1))
                        mm(ps[3][:, :], w["Asrc"][:, :], xoT[:, k, :], start=True, stop=False)
                        mm(ps[3][:, :], w["Adst"][:, :], xtT[:, k, :], start=False, stop=True)
                        mm(ps[4][:, :], w["Aself"][:, :], xtT[:, k, :], start=True, stop=True).then_inc(pe_["s"], 1)
                        if b.has(1):
                            pe.wait_ge(ac_["p"], b.count(1))
                        mm(ps[5][:, :], w["W2"][:, :], xoT[:, k, :], start=True, stop=True).then_inc(pe_["p"], 1)
                        pe.wait_ge(node_["xT"], b.count())
                        if b.has(1):
                            pe.wait_ge(node_["elu"], b.count(1))
                        add_bias(nc, ps_z, w, "bias2")
                        for t in range(TPC):
                            ts = slice(t * TILE, (t + 1) * TILE)
                            last = mm(ps_z[:, ts], node_xT[:, k, ts], w["W2"][:, :], start=False, stop=t == TPC - 1)
                        last.then_inc(node_["z"], 1)
                    if a is not None:
                        pe.wait_ge(node_loaded[a.slot], a.landed(16))
                        if a.has(1):
                            pe.wait_ge(node_["xT"], a.count(1))
                        transpose4(nc, ps_xT, node_x[:, a.slot], w["ident"]).then_inc(node_["turned"], 1)
                run_chunks(pe, n, R, [0, 1], step)

            @block.scalar
            def _(act):
                nc.scalar.preload_act_table_set(ACT_SET)
                ac = nc.scalar.activation

                def step(cs):
                    a, b, d = cs
                    if a is not None:
                        k = a.slot % 2
                        act.wait_ge(pe_["tr"], a.count())
                        if a.has(2):
                            act.wait_ge(pe_["p"], a.count(2))
                        ac(xoT[:, k, :], ps[0][:, :], ACT.Copy)
                        ac(xtT[:, k, :], ps[1][:, :], ACT.Copy).then_inc(ac_["tr"], 1)
                        act.wait_ge(pe_["m"], a.count())
                        if a.has(2):
                            act.wait_ge(ve_["max"], a.count(2))
                        ac(fresh[:, k, :], ps[2][:, :], ACT.Copy).then_inc(ac_["m"], 1)
                    if b is not None:
                        k = b.slot % 2
                        act.wait_ge(pe_["s"], b.count())
                        if b.has(2):
                            act.wait_ge(ve_["s"], b.count(2))
                        ac(raw[:, k, 0, :], ps[3][:, :], ACT.Copy)
                        ac(raw[:, k, 1, :], ps[4][:, :], ACT.Copy).then_inc(ac_["s"], 1)
                        act.wait_ge(pe_["p"], b.count())
                        if b.slot_used():
                            act.wait_ge(saved[b.slot], b.landed(48, 1))
                        ac(proj[:, b.slot, :], ps[5][:, :], ACT.Identity, bias=w["bias2c"][:, 0:1]).then_inc(ac_["p"], 1)
                    if d is not None:
                        act.wait_ge(node_["shift"], d.count())
                        if d.slot_used():
                            act.wait_ge(node_stored[d.slot], d.landed(32, 1))
                        apply_rows(nc, node_out[:, d.slot, 1], node_y[:, d.slot % 2], shift, rstd[:, 1, :])\
                            .then_inc(node_["out4"], 1)
                    if a is not None:
                        act.wait_ge(node_["turned"], a.count())
                        if a.has(2):
                            act.wait_ge(node_["z"], a.count(2))
                        ac(node_xT[:, a.slot % 2, :], ps_xT[:, :], ACT.Copy).then_inc(node_["xT"], 1)
                    if b is not None:
                        act.wait_ge(node_["y"], b.count())
                        ac(node_low[:, :, :], tiles(ps_z[:, :]), ACT.Relu, scale=-1.0)
                        act.drain()
                        ac(node_low[:, :, :], node_low[:, :, :], ACT.Exp, scale=-1.0).then_inc(node_["elu"], 1)
                        act.drain()
                        act.wait_ge(node_["stats"], b.count())
                        ln_twice_rstd(nc, act, mv[:, :, 1], rstd, w).then_inc(node_["rstd"], 1)
                run_chunks(act, n, R, [0, 1, 2], step)

            @block.vector
            def _(dve):
                v = nc.vector

                def step(cs):
                    m, b, d = cs
                    dve.drain()
                    if d is not None:
                        dve.wait_ge(node_["rstd"], d.count())
                        if d.has(1):
                            dve.wait_ge(node_["out4"], d.count(1))
                        make_shift(nc, shift, mv, rstd[:, 1, :]).then_inc(node_["shift"], 1)
                        if d.slot_used():
                            dve.wait_ge(node_stored[d.slot], d.landed(32, 1))
                        ln_apply(nc, node_out[:, d.slot, 0], node_y[:, d.slot % 2], mv, rstd[:, 0, :])\
                            .then_inc(node_["out3"], 1)
                    if m is not None:
                        S.index(dve, m)
                    if b is not None:
                        k = b.slot % 2
                        dve.wait_ge(ac_["s"], b.count())
                        dve.wait_ge(ac_["m"], b.count())
                        if b.slot_used():
                            dve.wait_ge(saved[b.slot], b.landed(48, 1))
                        v.scalar_tensor_tensor(kept[:, b.slot, 0:2, :], raw[:, k, :, :], 0.2, raw[:, k, :, :],
                                               ALU.mult, ALU.max).then_inc(ve_["s"], 1)
                        dve.drain()
                        v.tensor_tensor(high[:, :], kept[:, b.slot, 0, :], kept[:, b.slot, 1, :], ALU.max)
                        dve.drain()
                        first = isinstance(b.i, int) and b.i == 0
                        scan(nc, S, kept[:, b.slot, 2, :], fresh[:, k, :], high[:, :],
                             None if first else edge_col(S, kept[:, (b.slot - 1) % R, 2, :]), ALU.add, ALU.max)\
                            .then_inc(ve_["max"], 1)
                        yb = node_y[:, k]
                        dve.wait_ge(node_["z"], b.count())
                        v.scalar_tensor_tensor(yb, tiles(ps_z[:, :]), 0.0, node_x[:, b.slot], ALU.max, ALU.add)\
                         .then_inc(node_["y"], 1)
                        dve.drain()
                        dve.wait_ge(node_["elu"], b.count())
                        v.scalar_tensor_tensor(yb, node_low[:, :, :], -1.0, yb, ALU.add, ALU.add)
                        dve.drain()
                        ln_stats(nc, yb, stats, mv)
                        dve.drain()
                        ln_aggregate(nc, stats, mv, TPC).then_inc(node_["stats"], 1)
                run_chunks(dve, n, R, [0, 5, 6], step)
        end_phase(nc, P)


def at_rows(t, start, size):
    return t[start:start + size, :] if isinstance(start, int) else t[bass.ds(start, size), :]


def build_layer2_sums(nc, g, w, T, A):
    n = g.EC // CH
    x34 = T.x34.rearrange("n k d -> n (k d)")
    with ExitStack() as ctx:
        P = Phase(nc, ctx, "l2b")
        S = Slots(P, nc, g, w, T.rec_c, 2, n, True)
        R = S.RING
        proj = P.sb("proj", [128, R, CH])
        xt = P.sb("xt", [128, R, TPC, D])
        score = P.sb("score", [128, R, 3, CH])
        xtT = P.sb("xtT", [128, 2, CH])
        top = P.sb("top", [128, 2, CH])
        exps = P.sb("exps", [128, CH])
        den, num = P.sb("den", [128, 2, CH]), P.sb("num", [128, 2, CH])
        weighted = P.sb("weighted", [128, CH])
        on = P.sb("on", [128, 2, CH])
        share = P.sb("share", [128, 2, TPC * 4])
        inv = P.sb("inv", [128, TPC * 4])
        z = P.sb("z", [128, TPC, D])
        low = P.sb("low", [128, TPC, D])
        y = P.sb("y", [128, 2, TPC, D])
        out = P.sb("out", [128, R, TPC, 2 * D])
        stats, mv = P.sb("stats", [128, 4, 6]), P.sb("mv", [128, 4, 2])
        rstd, shift = P.sb("rstd", [128, 2, TPC]), P.sb("shift", [128, 2, TPC])
        ps_on, ps_new, ps_xt, ps_num, ps_den, ps_self, ps_score, ps_top = (
            P.ps("ps_" + k) for k in ("on", "new", "xt", "num", "den", "self", "score", "top"))
        pe_ = {k: P.sem("pe_" + k) for k in ("tr", "m", "score", "self", "rows")}
        ac_ = {k: P.sem("ac_" + k) for k in ("tr", "on", "exp", "share", "elu", "rstd", "out")}
        ve_ = {k: P.sem("ve_" + k) for k in ("top", "diff", "less", "num", "z", "stats", "shift")}
        loaded, scattered = P.sems("loaded", R), P.sems("scattered", R)
        with nc.Block() as block:
            @block.sync
            def _(sp):
                def step(cs):
                    c = cs[0]
                    start = S.start(sp, c)
                    p = S.pos(c)
                    p0 = p * 128 if isinstance(p, int) else sp.snap(p * 128)
                    p1 = p * 4 if isinstance(p, int) else sp.snap(p * 4)
                    if c.slot_used():
                        sp.wait_ge(scattered[c.slot], c.landed(64, 1))
                    hold(sp, w)
                    S.load(sp, c, start)
                    sp.dma_start(proj[:, c.slot, :], at_rows(T.proj2, p0, 128)).then_inc(loaded[c.slot], 16)
                    sp.dma_start(xt[:, c.slot].rearrange("p t c -> p (t c)"), at_rows(T.row2, p0, 128))\
                      .then_inc(loaded[c.slot], 16)
                    for h in range(4):
                        src = T.score2[p1 + h] if isinstance(p1, int) else T.score2[bass.ds(p1 + h, 1), :].squeeze(0)
                        sp.dma_start(score[32 * h:32 * h + 32, c.slot].rearrange("p k c -> p (k c)"),
                                     src.partition_broadcast(32)).then_inc(loaded[c.slot], 16)
                run_chunks(sp, n, R, [0], step)

            @block.gpsimd
            def _(pool):
                bound = pool.to_reg(g.N - 1)

                def step(cs):
                    c = cs[0]
                    pool.wait_ge(ac_["out"], c.count())
                    hold(pool, w)
                    S.scatter(pool, c, out, x34, bound, scattered)
                run_chunks(pool, n, R, [0], step)
                for s in range(R):
                    pool.wait_ge(scattered[s], 64 * turns(n, s, R))

            @block.tensor
            def _(pe):
                mm = nc.tensor.matmul

                def step(cs):
                    p, a, b = cs
                    if b is not None:
                        k = b.slot % 2
                        pe.wait_ge(ve_["num"], b.count())
                        if b.has(1):
                            pe.wait_ge(ve_["z"], b.count(1))
                        for t in range(TPC):
                            ts = slice(t * TILE, (t + 1) * TILE)
                            nc.tensor.transpose(ps_num[:, ts], num[:, k, ts], w["ident"][:, :])
                            last = nc.tensor.transpose(ps_den[:, ts], den[:, k, ts], w["ident"][:, :])
                        last.then_inc(pe_["rows"], 1)
                    if p is not None:
                        pe.wait_ge(S.ready, p.count())
                        if p.has(1):
                            pe.wait_ge(ac_["on"], p.count(1))
                            pe.wait_ge(ve_["top"], p.count(1))
                        spread(nc, ps_on, S.same[:, p.slot, 0, :], w["identb"])
                        spread(nc, ps_new, S.same[:, p.slot, 1, :], w["identb"]).then_inc(pe_["m"], 1)
                        pe.wait_ge(loaded[p.slot], p.landed(96))
                        if p.has(1):
                            pe.wait_ge(ac_["tr"], p.count(1))
                        transpose4(nc, ps_xt, xt[:, p.slot], w["ident"]).then_inc(pe_["tr"], 1)
                    if a is not None:
                        k = a.slot % 2
                        pe.wait_ge(ve_["top"], a.count())
                        if a.has(1):
                            pe.wait_ge(ve_["less"], a.count(1))
                        for t in range(TPC):
                            ts = slice(t * TILE, (t + 1) * TILE)
                            nc.tensor.transpose(ps_score[:, ts], score[:, a.slot, 1, ts], w["ident"][:, :])
                            last = nc.tensor.transpose(ps_top[:, ts], top[:, k, ts], w["ident"][:, :])
                        last.then_inc(pe_["score"], 1)
                        pe.wait_ge(ac_["tr"], a.count())
                        if a.has(1):
                            pe.wait_ge(ve_["z"], a.count(1))
                        add_bias(nc, ps_self, w, "bias2")
                        for t in range(TPC):
                            ts = slice(t * TILE, (t + 1) * TILE)
                            last = mm(ps_self[:, ts], xtT[:, k, ts], w["W2"][:, :], start=False, stop=t == TPC - 1)
                        last.then_inc(pe_["self"], 1)
                run_chunks(pe, n, R, [1, 2, 3], step)

            @block.scalar
            def _(act):
                nc.scalar.preload_act_table_set(ACT_SET)
                ac = nc.scalar.activation

                def step(cs):
                    p, a, b, d = cs
                    if a is not None:
                        act.wait_ge(ve_["diff"], a.count())
                        ac(exps[:, :], exps[:, :], ACT.Exp).then_inc(ac_["exp"], 1)
                    if d is not None:
                        act.wait_ge(ve_["shift"], d.count())
                        for i in range(2):
                            for t in range(TPC):
                                last = ac(out[:, d.slot, t, i * D:(i + 1) * D], y[:, d.slot % 2, t, :], ACT.Identity,
                                          bias=shift[:, i, t:t + 1], scale=rstd[:, i, t:t + 1])
                        last.then_inc(ac_["out"], 1)
                    if b is not None:
                        act.wait_ge(ve_["z"], b.count())
                        ac(low[:, :, :], z[:, :, :], ACT.Relu, scale=-1.0)
                        act.drain()
                        ac(low[:, :, :], low[:, :, :], ACT.Exp, scale=-1.0).then_inc(ac_["elu"], 1)
                    if a is not None:
                        act.wait_ge(ve_["less"], a.count())
                        ac(share[:, a.slot % 2, :], share[:, a.slot % 2, :], ACT.Exp).then_inc(ac_["share"], 1)
                    if p is not None:
                        act.wait_ge(pe_["m"], p.count())
                        if p.has(2):
                            act.wait_ge(ve_["num"], p.count(2))
                        ac(on[:, p.slot % 2, :], ps_on[:, :], ACT.Copy).then_inc(ac_["on"], 1)
                        act.wait_ge(pe_["tr"], p.count())
                        if p.has(2):
                            act.wait_ge(pe_["self"], p.count(2))
                        ac(xtT[:, p.slot % 2, :], ps_xt[:, :], ACT.Copy).then_inc(ac_["tr"], 1)
                    if b is not None:
                        act.wait_ge(ve_["stats"], b.count())
                        ln_twice_rstd(nc, act, mv[:, :, 1], rstd, w).then_inc(ac_["rstd"], 1)
                run_chunks(act, n, R, [1, 2, 3, 4], step)

            @block.vector
            def _(dve):
                v = nc.vector

                def by_head(t):
                    return t.rearrange("p t (h d) -> p (t h) d", h=4)

                def widen(cols):
                    return cols.unsqueeze(2).to_broadcast([128, TPC * 4, 32])

                def step(cs):
                    m, a, b, d = cs
                    dve.drain()
                    if a is not None:
                        k = a.slot % 2
                        first = isinstance(a.i, int) and a.i == 0

                        def carry(t):
                            return None if first else edge_col(S, t[:, 1 - k, :])
                        dve.wait_ge(loaded[a.slot], a.landed(96))
                        dve.wait_ge(pe_["m"], a.count())
                        sc = score[:, a.slot]
                        scan(nc, S, top[:, k, :], ps_new[:, :], sc[:, 2, :], carry(top), ALU.add, ALU.max)\
                            .then_inc(ve_["top"], 1)
                    if d is not None:
                        dve.wait_ge(ac_["rstd"], d.count())
                        if d.has(1):
                            dve.wait_ge(ac_["out"], d.count(1))
                        for i in range(2):
                            last = v.scalar_tensor_tensor(shift[:, i, :], mv[:, :, 0], -1.0, rstd[:, i, :],
                                                          ALU.mult, ALU.mult)
                        last.then_inc(ve_["shift"], 1)
                    dve.drain()
                    if a is not None:
                        v.tensor_tensor(exps[:, :], sc[:, 0, :], top[:, k, :], ALU.subtract).then_inc(ve_["diff"], 1)
                    if b is not None:
                        dve.wait_ge(ac_["share"], b.count())
                        dve.wait_ge(pe_["rows"], b.count())
                        mine = share[:, b.slot % 2, :]
                        v.tensor_tensor(inv[:, :], ps_den[:, 0:CH:32], mine, ALU.add)
                        v.tensor_tensor(by_head(z[:, :, :]), by_head(tiles(ps_self[:, :])), widen(mine), ALU.mult)
                        dve.drain()
                        v.tensor_scalar(inv[:, :], inv[:, :], 1e-12, None, ALU.max)
                        v.tensor_tensor(z[:, :, :], z[:, :, :], tiles(ps_num[:, :]), ALU.add)
                        dve.drain()
                        v.reciprocal(inv[:, :], inv[:, :])
                    dve.drain()
                    if a is not None:
                        dve.wait_ge(ac_["exp"], a.count())
                        dve.wait_ge(ac_["on"], a.count())
                        v.tensor_tensor(weighted[:, :], exps[:, :], proj[:, a.slot, :], ALU.mult)
                    if b is not None:
                        v.tensor_tensor(by_head(z[:, :, :]), by_head(z[:, :, :]), widen(inv[:, :]), ALU.mult)\
                         .then_inc(ve_["z"], 1)
                    if a is not None:
                        scan(nc, S, den[:, k, :], on[:, k, :], exps[:, :], carry(den), ALU.mult, ALU.add)
                    dve.drain()
                    if b is not None:
                        v.scalar_tensor_tensor(y[:, b.slot % 2], z[:, :, :], 0.0, xt[:, b.slot], ALU.max, ALU.add)
                    if a is not None:
                        scan(nc, S, num[:, k, :], on[:, k, :], weighted[:, :], carry(num), ALU.mult, ALU.add)\
                            .then_inc(ve_["num"], 1)
                    if m is not None:
                        S.index(dve, m)
                    if a is not None:
                        dve.wait_ge(pe_["score"], a.count())
                        v.tensor_copy(share[:, k, :], ps_top[:, 0:CH:32])
                        dve.drain()
                        v.tensor_tensor(share[:, k, :], ps_score[:, 0:CH:32], share[:, k, :], ALU.subtract)\
                         .then_inc(ve_["less"], 1)
                    if b is not None:
                        dve.drain()
                        dve.wait_ge(ac_["elu"], b.count())
                        yb = y[:, b.slot % 2]
                        v.scalar_tensor_tensor(yb, low[:, :, :], -1.0, yb, ALU.add, ALU.add)
                        dve.drain()
                        ln_stats(nc, yb, stats, mv)
                        dve.drain()
                        ln_aggregate(nc, stats, mv, TPC).then_inc(ve_["stats"], 1)
                run_chunks(dve, n, R, [0, 2, 3, 4], step)
        end_phase(nc, P)


def build_layer3_scores(nc, g, w, T, A):
    n = g.ED // CH
    x_rows = T.x34.rearrange("n k d -> (n k) d")
    IDX, TURN, SEL, REL, HID, WGT, KVQ, MAX, SAVE = 0, 2, 3, 4, 5, 6, 7, 8, 9
    with ExitStack() as ctx:
        P = Phase(nc, ctx, "l3a")
        S = Slots(P, nc, g, w, T.rec_d, REC, n, False)
        R = S.RING
        xs, xd = P.sb("xs", [128, R, TPC, D]), P.sb("xd", [128, R, TPC, D])
        xsT, xdT = P.sb("xsT", [128, R, CH]), P.sb("xdT", [128, R, CH])
        fresh = P.sb("fresh", [128, R, CH])
        attr = P.sb("attr", [128, R, TPC, 3])
        attrT = P.sb("attrT", [3, CH])
        oh_type = P.sb("oh_type", [64, 2, CH])
        tm, rel = P.sb("tm", [128, 4, CH]), P.sb("rel", [128, 4, CH])
        hT, dw = P.sb("hT", [128, CH]), P.sb("dw", [128, CH])
        msg = P.sb("msg", [128, 2, CH])
        qT, qk = P.sb("qT", [128, CH]), P.sb("qk", [128, 2, CH])
        value = P.sb("value", [128, R, CH])
        kept = P.sb("kept", [128, R, 2, CH])
        ps_type, ps_dt, ps_rel_h, ps_wgt_attr, ps_v, ps_s_xs, ps_k_xd, ps_q_mask = (
            P.ps(k) for k in ("type", "dt", "rel_h", "wgt_attr", "v", "s_xs", "k_xd", "q_mask"))
        pe_ = {k: P.sem("pe_" + k) for k in ("tr", "sel", "rel", "h", "dw", "kvq", "s")}
        ac_ = {k: P.sem("ac_" + k) for k in ("tr", "dt", "h", "dw", "q", "s")}
        ve_ = {k: P.sem("ve_" + k) for k in ("attr", "type", "rel", "msg", "qk", "max")}
        gathered, saved, row_saved = P.sems("gathered", R), P.sems("saved", R), P.sems("row_saved", R)
        with nc.Block() as block:
            @block.sync
            def _(sp):
                def step(cs):
                    load, row, done = cs
                    if load is not None:
                        start = S.start(sp, load)
                        if load.slot_used():
                            sp.wait_ge(row_saved[load.slot], load.landed(16, 1))
                            hold(sp, w)
                            sp.wait_ge(pe_["tr"], load.count(R))
                            hold(sp, w)
                        S.load(sp, load, start)
                    if row is not None:
                        p = S.pos(row)
                        p0 = p * 128 if isinstance(p, int) else sp.snap(p * 128)
                        sp.wait_ge(gathered[row.slot], row.landed(128))
                        hold(sp, w)
                        sp.dma_start(at_rows(T.row3, p0, 128), xd[:, row.slot].rearrange("p t c -> p (t c)"))\
                          .then_inc(row_saved[row.slot], 16)
                    if done is not None:
                        p = S.pos(done)
                        p0 = p * 128 if isinstance(p, int) else sp.snap(p * 128)
                        p1 = p * 8 if isinstance(p, int) else sp.snap(p * 8)
                        sp.wait_ge(ve_["max"], done.count())
                        hold(sp, w)
                        sp.dma_start(at_rows(T.value3, p0, 128), value[:, done.slot, :]).then_inc(saved[done.slot], 16)
                        sp.dma_start(at_rows(T.score3, p1, 8), kept[0:128:16, done.slot].rearrange("p k c -> p (k c)"))\
                          .then_inc(saved[done.slot], 16)
                run_chunks(sp, n, R, [IDX, TURN, SAVE], step)
                for s in range(R):
                    sp.wait_ge(saved[s], 32 * turns(n, s, R))
                    sp.wait_ge(row_saved[s], 16 * turns(n, s, R))

            @block.gpsimd
            def _(pool):
                bound = pool.to_reg(2 * g.N - 1)

                def step(cs):
                    c = cs[0]
                    pool.wait_ge(S.ready, c.count())
                    hold(pool, w)
                    S.gather(pool, c, 0, xs, x_rows, bound, gathered)
                    S.gather(pool, c, 1, xd, x_rows, bound, gathered)
                run_chunks(pool, n, R, [0], step)

            @block.tensor
            def _(pe):
                mm = nc.tensor.matmul

                def step(cs):
                    turn, sel, relc, hid, wgt, kvq, mx = cs
                    if hid is not None:
                        pe.wait_ge(ve_["rel"], hid.count())
                        mm(ps_rel_h[:, :], w["R1a"][:, :], xsT[:, hid.slot, :], start=True, stop=False)
                        mm(ps_rel_h[:, :], w["R1b"][:, :], rel[:, hid.slot % 4, :], start=False, stop=False)
                        mm(ps_rel_h[:, :], w["W1c"][:, :], tm[0:1, hid.slot % 4, :], start=False, stop=True)\
                            .then_inc(pe_["h"], 1)
                    if sel is not None:
                        pe.wait_ge(ac_["tr"], sel.count())
                        if sel.has(1):
                            pe.wait_ge(ve_["type"], sel.count(1))
                            pe.wait_ge(ac_["dt"], sel.count(1))
                        mm(ps_type[0:64, :], w["sel_type"][:, :], attrT[:, :], start=True, stop=True)
                        mm(ps_dt[:, :], w["sel_dt"][:, :], attrT[:, :], start=True, stop=True).then_inc(pe_["sel"], 1)
                    if wgt is not None:
                        pe.wait_ge(ac_["h"], wgt.count())
                        if wgt.has(1):
                            pe.wait_ge(ac_["dw"], wgt.count(1))
                        mm(ps_wgt_attr[:, :], w["R2"][:, :], hT[:, :], start=True, stop=True).then_inc(pe_["dw"], 1)
                    if kvq is not None:
                        pe.wait_ge(ve_["msg"], kvq.count())
                        if kvq.has(1):
                            pe.wait_ge(ve_["qk"], kvq.count(1))
                            pe.wait_ge(ac_["q"], kvq.count(1))
                        mm(ps_q_mask[:, :], w["Wq"][:, :], xdT[:, kvq.slot, :], start=True, stop=True)
                        mm(ps_k_xd[:, :], w["Wk"][:, :], msg[:, kvq.slot % 2, :], start=True, stop=True)
                        mm(ps_v[:, :], w["Wv"][:, :], msg[:, kvq.slot % 2, :], start=True, stop=True)\
                            .then_inc(pe_["kvq"], 1)
                    if relc is not None:
                        pe.wait_ge(ve_["type"], relc.count())
                        if relc.has(1):
                            pe.wait_ge(ac_["h"], relc.count(1))
                        mm(ps_rel_h[:, :], w["rel"][:, :], oh_type[:, relc.slot % 2, :], start=True, stop=True)\
                            .then_inc(pe_["rel"], 1)
                    if mx is not None:
                        pe.wait_ge(ve_["qk"], mx.count())
                        if mx.has(1):
                            pe.wait_ge(ac_["s"], mx.count(1))
                        mm(ps_s_xs[:, :], w["heads16"][:, :], qk[:, mx.slot % 2, :], start=True, stop=True)\
                            .then_inc(pe_["s"], 1)
                    if turn is not None:
                        pe.wait_ge(gathered[turn.slot], turn.landed(128))
                        if turn.has(1):
                            pe.wait_ge(ac_["tr"], turn.count(1))
                        if turn.has(KVQ - TURN):
                            pe.wait_ge(ve_["qk"], turn.count(KVQ - TURN))
                            pe.wait_ge(ac_["q"], turn.count(KVQ - TURN))
                        if turn.has(WGT - TURN):
                            pe.wait_ge(ac_["dw"], turn.count(WGT - TURN))
                        pe.wait_ge(ve_["attr"], turn.count())
                        transpose4(nc, ps_k_xd, xd[:, turn.slot], w["ident"])
                        for t in range(TPC):
                            nc.tensor.transpose(ps_wgt_attr[0:3, t * TILE:(t + 1) * TILE], attr[:, turn.slot, t, :],
                                                w["ident"][:, :])
                        spread(nc, ps_q_mask, S.same[:, turn.slot, 1, :], w["identb"])
                        if turn.has(MAX - TURN):
                            pe.wait_ge(ac_["s"], turn.count(MAX - TURN))
                        transpose4(nc, ps_s_xs, xs[:, turn.slot], w["ident"]).then_inc(pe_["tr"], 1)
                run_chunks(pe, n, R, [TURN, SEL, REL, HID, WGT, KVQ, MAX], step)

            @block.scalar
            def _(act):
                nc.scalar.preload_act_table(ACT.Sigmoid)
                ac = nc.scalar.activation

                def step(cs):
                    turn, sel, hid, wgt, kvq, mx = cs
                    if hid is not None:
                        act.wait_ge(pe_["h"], hid.count())
                        if hid.has(1):
                            act.wait_ge(pe_["dw"], hid.count(1))
                        ac(hT[:, :], ps_rel_h[:, :], ACT.Relu, bias=w["b1"][:, 0:1]).then_inc(ac_["h"], 1)
                    if sel is not None:
                        act.wait_ge(pe_["sel"], sel.count())
                        if sel.has(4):
                            act.wait_ge(pe_["h"], sel.count(4))
                        ac(tm[:, sel.slot % 4, :], ps_dt[:, :], ACT.Sigmoid, scale=w["inv_tc"][:, 0:1])\
                            .then_inc(ac_["dt"], 1)
                    if wgt is not None:
                        act.wait_ge(pe_["dw"], wgt.count())
                        if wgt.has(1):
                            act.wait_ge(ve_["msg"], wgt.count(1))
                        ac(dw[:, :], ps_wgt_attr[:, :], ACT.Sigmoid, bias=w["b2"][:, 0:1]).then_inc(ac_["dw"], 1)
                    if kvq is not None:
                        act.wait_ge(pe_["kvq"], kvq.count())
                        if kvq.has(1):
                            act.wait_ge(ve_["qk"], kvq.count(1))
                        if kvq.slot_used():
                            act.wait_ge(saved[kvq.slot], kvq.landed(32, 1))
                        ac(qT[:, :], ps_q_mask[:, :], ACT.Identity, bias=w["bq"][:, 0:1])
                        ac(value[:, kvq.slot, :], ps_v[:, :], ACT.Identity, bias=w["bias3v"][:, 0:1])\
                            .then_inc(ac_["q"], 1)
                    if mx is not None:
                        act.wait_ge(pe_["s"], mx.count())
                        ac(kept[:, mx.slot, 0, :], ps_s_xs[:, :], ACT.Copy, scale=0.25).then_inc(ac_["s"], 1)
                    if turn is not None:
                        act.wait_ge(pe_["tr"], turn.count())
                        if turn.slot_used():
                            act.wait_ge(ve_["max"], turn.count(R))
                        ac(xdT[:, turn.slot, :], ps_k_xd[:, :], ACT.Copy)
                        ac(attrT[:, :], ps_wgt_attr[0:3, :], ACT.Copy)
                        ac(fresh[:, turn.slot, :], ps_q_mask[:, :], ACT.Copy)
                        ac(xsT[:, turn.slot, :], ps_s_xs[:, :], ACT.Copy).then_inc(ac_["tr"], 1)
                run_chunks(act, n, R, [TURN, SEL, HID, WGT, KVQ, MAX], step)

            @block.vector
            def _(dve):
                v = nc.vector

                def step(cs):
                    m, sel, relc, wgt, kvq, mx = cs
                    dve.drain()
                    if sel is not None:
                        dve.wait_ge(pe_["sel"], sel.count())
                        if sel.has(2):
                            dve.wait_ge(pe_["rel"], sel.count(2))
                        v.tensor_scalar(oh_type[:, sel.slot % 2, :], ps_type[0:64, :], w["iota64"][:, 0:1], None,
                                        ALU.is_equal).then_inc(ve_["type"], 1)
                    if wgt is not None:
                        if wgt.has(2):
                            dve.wait_ge(pe_["kvq"], wgt.count(2))
                        mine = msg[:, wgt.slot % 2, :]
                        v.tensor_tensor(mine, xsT[:, wgt.slot, :], rel[:, wgt.slot % 4, :], ALU.mult)
                        dve.drain()
                        dve.wait_ge(ac_["dw"], wgt.count())
                        v.tensor_tensor(mine, mine, dw[:, :], ALU.mult).then_inc(ve_["msg"], 1)
                    if kvq is not None:
                        dve.wait_ge(ac_["q"], kvq.count())
                        if kvq.has(2):
                            dve.wait_ge(pe_["s"], kvq.count(2))
                        v.scalar_tensor_tensor(qk[:, kvq.slot % 2, :], ps_k_xd[:, :], w["bk"][:, 0:1], qT[:, :],
                                               ALU.add, ALU.mult).then_inc(ve_["qk"], 1)
                    if relc is not None:
                        dve.wait_ge(pe_["rel"], relc.count())
                        dve.wait_ge(ac_["dt"], relc.count())
                        v.tensor_tensor(rel[:, relc.slot % 4, :], ps_rel_h[:, :], tm[:, relc.slot % 4, :], ALU.mult)\
                         .then_inc(ve_["rel"], 1)
                    if mx is not None:
                        dve.wait_ge(ac_["s"], mx.count())
                        first = isinstance(mx.i, int) and mx.i == 0
                        scan(nc, S, kept[:, mx.slot, 1, :], fresh[:, mx.slot, :], kept[:, mx.slot, 0, :],
                             None if first else edge_col(S, kept[:, (mx.slot - 1) % R, 1, :]), ALU.add, ALU.max)\
                            .then_inc(ve_["max"], 1)
                    if m is not None:
                        S.index(dve, m, other_scale=2)
                        v.tensor_copy(attr[:, m.slot, :, 0], S.rec[:, m.slot, :, W_TYPE])
                        v.tensor_copy(attr[:, m.slot, :, 1:3], S.rec[:, m.slot, :, W_NV:W_NV + 2].bitcast(F32))\
                         .then_inc(ve_["attr"], 1)
                run_chunks(dve, n, R, [IDX, SEL, REL, WGT, KVQ, MAX], step)
        end_phase(nc, P)


def build_layer3_sums(nc, g, w, T, A):
    n = g.ED // CH
    x_rows = T.x34.rearrange("n k d -> (n k) d")
    with ExitStack() as ctx:
        P = Phase(nc, ctx, "l3b")
        S = Slots(P, nc, g, w, T.rec_d, REC, n, True)
        R = S.RING
        value = P.sb("value", [128, R, CH])
        xd = P.sb("xd", [128, R, TPC, D])
        score = P.sb("score", [128, R, 2, CH])
        goes_on = P.sb("goes_on", [128, 2, CH])
        fresh = P.sb("fresh", [128, 2, CH])
        top = P.sb("top", [128, 2, CH])
        exps = P.sb("exps", [128, 2, CH])
        den, num = P.sb("den", [128, 2, CH]), P.sb("num", [128, 2, CH])
        weighted, inv = P.sb("weighted", [128, CH]), P.sb("inv", [128, TPC * 8])
        z = P.sb("z", [128, TPC, D])
        y = P.sb("y", [128, TPC, D])
        out = P.sb("out", [128, R, TPC, D])
        stats, mv, rstd = P.sb("stats", [128, 4, 6]), P.sb("mv", [128, 4, 2]), P.sb("rstd", [128, 4])
        ps = [P.ps(f"ps{k}") for k in range(4)]
        pe_ = {k: P.sem("pe_" + k) for k in ("m", "z")}
        ac_ = {k: P.sem("ac_" + k) for k in ("m", "exp", "rstd")}
        ve_ = {k: P.sem("ve_" + k) for k in ("diff", "num", "z", "stats", "out")}
        loaded, scattered = P.sems("loaded", R), P.sems("scattered", R)
        with nc.Block() as block:
            @block.sync
            def _(sp):
                def step(cs):
                    c = cs[0]
                    start = S.start(sp, c)
                    p = S.pos(c)
                    p0 = p * 128 if isinstance(p, int) else sp.snap(p * 128)
                    p1 = p * 8 if isinstance(p, int) else sp.snap(p * 8)
                    if c.slot_used():
                        sp.wait_ge(scattered[c.slot], c.landed(64, 1))
                    hold(sp, w)
                    S.load(sp, c, start)
                    sp.dma_start(value[:, c.slot, :], at_rows(T.value3, p0, 128)).then_inc(loaded[c.slot], 16)
                    sp.dma_start(xd[:, c.slot].rearrange("p t c -> p (t c)"), at_rows(T.row3, p0, 128))\
                      .then_inc(loaded[c.slot], 16)
                    for h in range(8):
                        src = T.score3[p1 + h] if isinstance(p1, int) else T.score3[bass.ds(p1 + h, 1), :].squeeze(0)
                        sp.dma_start(score[16 * h:16 * h + 16, c.slot].rearrange("p k c -> p (k c)"),
                                     src.partition_broadcast(16)).then_inc(loaded[c.slot], 16)
                run_chunks(sp, n, R, [0], step)

            @block.gpsimd
            def _(pool):
                bound = pool.to_reg(2 * g.N - 1)

                def step(cs):
                    c = cs[0]
                    pool.wait_ge(ve_["out"], c.count())
                    hold(pool, w)
                    S.scatter(pool, c, out, x_rows, bound, scattered)
                run_chunks(pool, n, R, [0], step)
                for s in range(R):
                    pool.wait_ge(scattered[s], 64 * turns(n, s, R))

            @block.tensor
            def _(pe):
                def step(cs):
                    a, b = cs
                    if a is not None:
                        pe.wait_ge(S.ready, a.count())
                        if a.has(1):
                            pe.wait_ge(ac_["m"], a.count(1))
                        spread(nc, ps[0], S.same[:, a.slot, 0, :], w["identb"])
                        spread(nc, ps[1], S.same[:, a.slot, 1, :], w["identb"]).then_inc(pe_["m"], 1)
                    if b is not None:
                        pe.wait_ge(ve_["num"], b.count())
                        if b.has(1):
                            pe.wait_ge(ve_["z"], b.count(1))
                        for t in range(TPC):
                            ts = slice(t * TILE, (t + 1) * TILE)
                            nc.tensor.transpose(ps[2][:, ts], num[:, b.slot % 2, ts], w["ident"][:, :])
                            last = nc.tensor.matmul(ps[3][:, 8 * t:8 * t + 8], den[:, b.slot % 2, ts],
                                                    w["pick16"][:, :], start=True, stop=True)
                        last.then_inc(pe_["z"], 1)
                run_chunks(pe, n, R, [0, 1], step)

            @block.scalar
            def _(act):
                nc.scalar.preload_act_table_set(ACT_SET)
                ac = nc.scalar.activation

                def step(cs):
                    a, b = cs
                    if a is not None:
                        k = a.slot % 2
                        act.wait_ge(pe_["m"], a.count())
                        if a.has(2):
                            act.wait_ge(ve_["num"], a.count(2))
                        ac(goes_on[:, k, :], ps[0][:, :], ACT.Copy)
                        ac(fresh[:, k, :], ps[1][:, :], ACT.Copy).then_inc(ac_["m"], 1)
                        act.wait_ge(ve_["diff"], a.count())
                        ac(exps[:, k, :], exps[:, k, :], ACT.Exp).then_inc(ac_["exp"], 1)
                    if b is not None:
                        act.wait_ge(ve_["stats"], b.count())
                        ln_rstd(nc, act, mv[:, :, 1], rstd[:, :], w["eps"]).then_inc(ac_["rstd"], 1)
                run_chunks(act, n, R, [0, 1], step)

            @block.vector
            def _(dve):
                v = nc.vector

                def by_head(t):
                    return t.rearrange("p t (h d) -> p (t h) d", h=8)

                def step(cs):
                    m, a, b = cs
                    dve.drain()
                    if a is not None:
                        k = a.slot % 2
                        first = isinstance(a.i, int) and a.i == 0
                        dve.wait_ge(loaded[a.slot], a.landed(160))
                        dve.wait_ge(ac_["m"], a.count())
                        scan(nc, S, top[:, k, :], fresh[:, k, :], score[:, a.slot, 1, :],
                             None if first else edge_col(S, top[:, 1 - k, :]), ALU.add, ALU.max)
                        dve.drain()
                        v.tensor_tensor(exps[:, k, :], score[:, a.slot, 0, :], top[:, k, :], ALU.subtract)\
                         .then_inc(ve_["diff"], 1)
                    if b is not None:
                        dve.wait_ge(pe_["z"], b.count())
                        v.reciprocal(inv[:, :], ps[3][:, 0:TPC * 8])
                        dve.drain()
                        v.tensor_tensor(by_head(z[:, :, :]), by_head(tiles(ps[2][:, :])),
                                        inv[:, :].unsqueeze(2).to_broadcast([128, TPC * 8, 16]), ALU.mult)\
                         .then_inc(ve_["z"], 1)
                        dve.drain()
                        v.tensor_tensor(y[:, :, :], z[:, :, :], xd[:, b.slot], ALU.add)
                    if a is not None:
                        dve.wait_ge(ac_["exp"], a.count())
                        if a.has(2):
                            dve.wait_ge(pe_["z"], a.count(2))
                        scan(nc, S, den[:, k, :], goes_on[:, k, :], exps[:, k, :],
                             None if first else edge_col(S, den[:, 1 - k, :]), ALU.mult, ALU.add)
                        v.tensor_tensor(weighted[:, :], exps[:, k, :], value[:, a.slot, :], ALU.mult)
                    if b is not None:
                        dve.drain()
                        ln_stats(nc, y, stats, mv)
                        dve.drain()
                        ln_aggregate(nc, stats, mv, TPC).then_inc(ve_["stats"], 1)
                    dve.drain()
                    if a is not None:
                        scan(nc, S, num[:, k, :], goes_on[:, k, :], weighted[:, :],
                             None if first else edge_col(S, num[:, 1 - k, :]), ALU.mult, ALU.add)\
                            .then_inc(ve_["num"], 1)
                    if m is not None:
                        S.index(dve, m, to_scale=2, to_plus=1)
                    if b is not None:
                        dve.wait_ge(ac_["rstd"], b.count())
                        ln_apply(nc, out[:, b.slot], y, mv, rstd).then_inc(ve_["out"], 1)
                run_chunks(dve, n, R, [0, 2, 3], step)
        end_phase(nc, P)


def build_program(nc, A, stage="all"):
    g = Sizes(A["x"].shape[0], A["src"].shape[0])
    T = Tables()
    T.x = A["x"]

    def table(name, shape, dt=F32):
        return A[name] if name in A else nc.dram_tensor(name, shape, dt).ap()
    T.x1, T.x2, T.x1_slot = table("x1", [g.N, D]), table("x2", [g.N, D]), table("x1_slot", [g.ED, D])
    T.x34 = A["x34"]
    T.rec_c = table("rec_c", [g.EC + 2, 2], I32)
    T.rec_d = table("rec_d", [g.ED + 2, REC], I32)
    nd, nC = g.ED // CH, g.EC // CH
    T.proj2, T.row2 = table("proj2", [nC * 128, CH]), table("row2", [nC * 128, TPC * D])
    T.score2 = table("score2", [nC * 4, 3 * CH])
    T.value3, T.row3 = table("value3", [nd * 128, CH]), table("row3", [nd * 128, TPC * D])
    T.score3 = table("score3", [nd * 8, 2 * CH])
    with ExitStack() as ctx:
        P = Phase(nc, ctx, "w")
        w = build_constants(nc, P, g, A)
        order = ["iso", "sort", "l0", "l1", "l2a", "l2b", "l3a", "l3b"]
        last = len(order) if stage == "all" else order.index(stage) + 1
        for s in order[:last]:
            {"iso": lambda: build_isolated(nc, g, w, T), "sort": lambda: build_sort(nc, g, w, T, A),
             "l0": lambda: build_layer0(nc, g, w, T, A), "l1": lambda: build_layer1(nc, g, w, T, A),
             "l2a": lambda: build_layer2_scores(nc, g, w, T, A), "l2b": lambda: build_layer2_sums(nc, g, w, T, A),
             "l3a": lambda: build_layer3_scores(nc, g, w, T, A), "l3b": lambda: build_layer3_sums(nc, g, w, T, A)}[s]()


_INS = ["x", "src", "dst", "edge_attr_10", "edge_attr_4", "edge_type_64", "edge_weight", "node_vec",
        "L0_gnn_W_si_0e", "L0_gnn_W_si_1o", "L0_gnn_W_l1_0e", "L0_gnn_W_l1_1o", "L0_gnn_W_fc1", "L0_gnn_W_fc2",
        "L0_gnn_W_l2_0e", "L0_gnn_W_l2_1o", "L1_gnn_W", "L1_gnn_b", "L2_gnn_W", "L2_gnn_attn_src",
        "L2_gnn_attn_dst", "L2_gnn_bias", "L3_gnn_rel_table", "L3_gnn_Wq", "L3_gnn_bq", "L3_gnn_Wk", "L3_gnn_bk",
        "L3_gnn_Wv", "L3_gnn_bv", "L3_gnn_W1", "L3_gnn_b1", "L3_gnn_W2", "L3_gnn_b2", "L3_gnn_time_coeff"]


def kernel(**inputs):
    import numpy as np
    import concourse.bacc as bacc
    from concourse import mybir as _mybir
    from concourse.bass_utils import run_bass_kernel_spmd

    nc = bacc.Bacc("TRN2", target_bir_lowering=False, num_devices=1)
    arrays, A = {}, {}
    for name in _INS:
        a = np.atleast_1d(np.ascontiguousarray(inputs[name]))
        arrays[name] = a
        A[name] = nc.dram_tensor(name, a.shape, _mybir.dt.from_np(a.dtype), kind="ExternalInput").ap()
    n, d = inputs["x"].shape
    A["x34"] = nc.dram_tensor("x34", [n, 2, d], _mybir.dt.float32, kind="ExternalOutput").ap()
    build_program(nc, A)
    result = run_bass_kernel_spmd(nc, [arrays], core_ids=[0])
    return result.results[0]["x34"].reshape(n, 2, d)[:, 1, :]
```
